# Optimizing a Trainium2 kernel written in Bass

```python
import numpy as np
import jax
import jax.numpy as jnp

def _softmax(x, axis=-1):
    return jax.nn.softmax(x, axis=axis)

def _gelu(x):
    return jax.nn.gelu(x, approximate=True)

def _silu(x):
    return jax.nn.silu(x)

def _sigmoid(x):
    return jax.nn.sigmoid(x)

def _layernorm(x, axis=-1, eps=1e-05):
    m = jnp.mean(x, axis=axis, keepdims=True)
    v = jnp.var(x, axis=axis, keepdims=True)
    return (x - m) / jnp.sqrt(v + eps)

def _scatter_add(tgt, idx, src, axis=0):
    return tgt.at[idx].add(src)

def _segment_sum(src, seg, n):
    return jax.ops.segment_sum(src, seg, n)
kernel_name = 'mk_vit_tower_cls_d1_tok_img1024_r4_5435bf'

def setup_inputs(seed: int=0):
    np.random.seed(seed)
    _w = jnp.asarray

    def _rec_inputs():
        import jax
        import jax.numpy as jnp
        _rk = jax.random.key(seed)
        x = -0.00150118 + 0.499729 * jax.random.normal(jax.random.fold_in(_rk, 1), (8, 256, 64, 2), jnp.float32)
        cls_tok = 0.02 * jax.random.normal(jax.random.fold_in(_rk, 5), (1, 1, 256), jnp.float32)
        return (x, cls_tok)
    x, cls_tok = _rec_inputs()

    def _L0_tok_setup():
        import jax, jax.numpy as jnp
        import numpy as np
        import math
        H = 256
        N = 64
        CH = 1
        SEQ_L = 256
        key = jax.random.key(seed)
        k1, k2, k3, k4 = jax.random.split(key, 4)
        log_dt = jax.random.uniform(k1, (H,), dtype=jnp.float32, minval=math.log(0.001), maxval=math.log(0.1))
        inv_A_real = jnp.log(0.5 * jnp.ones((H, N), jnp.float32)) + 0.1 * jax.random.normal(k2, (H, N), dtype=jnp.float32)
        A_imag = jnp.broadcast_to(math.pi * jnp.arange(N, dtype=jnp.float32), (H, N)).copy()
        B_ri = jax.random.normal(k3, (H, N, 2), dtype=jnp.float32) * 0.5
        C_ri = jax.random.normal(k4, (CH, H, N, 2), dtype=jnp.float32) * 0.5
        return {'log_dt': log_dt, 'inv_A_real': inv_A_real, 'A_imag': A_imag, 'B_ri': B_ri, 'C_ri': C_ri, 'L': SEQ_L}
    _L0_tok_all = _L0_tok_setup()
    _L0_tok_in = {k: v for k, v in _L0_tok_all.items() if k in ('log_dt', 'inv_A_real', 'A_imag', 'B_ri')}
    del _L0_tok_all

    def _L0_attn_setup():
        import jax, jax.numpy as jnp
        import numpy as np
        D_MODEL = 256
        N_HEADS = 4
        KEY_DIM = 256
        VALUE_DIM = 512
        DK = KEY_DIM // N_HEADS
        DV = VALUE_DIM // N_HEADS
        LOW_RANK = 16
        GATE_NORM = 16.0
        EPS = 1e-05

        def _gla_scan(q, k, v, gk):
            B, H, L, dk = q.shape
            dv = v.shape[-1]
            qs = jnp.moveaxis(q, 2, 0)
            ks_ = jnp.moveaxis(k, 2, 0)
            vs = jnp.moveaxis(v, 2, 0)
            gs = jnp.moveaxis(gk, 2, 0)

            def step(S, inp):
                q_t, k_t, v_t, g_t = inp
                S = S * jnp.exp(g_t)[..., None] + k_t[..., None] * v_t[..., None, :]
                o_t = jnp.einsum('bhk,bhkv->bhv', q_t, S)
                return (S, o_t)
            S0 = jnp.zeros((B, H, dk, dv), q.dtype)
            _, os = jax.lax.scan(step, S0, (qs, ks_, vs, gs))
            return jnp.moveaxis(os, 0, 2)
        key = jax.random.key(seed)
        ks = jax.random.split(key, 10)
        B, L = (2, 512)
        gain = 2.0 ** (-2.5)

        def xavier(k, shape, g=gain):
            fan_in, fan_out = (shape[0], shape[1])
            a = g * np.sqrt(6.0 / (fan_in + fan_out))
            return jax.random.uniform(k, shape, jnp.float32, -a, a)
        return {'x': jax.random.normal(ks[0], (B, L, D_MODEL), jnp.float32), 'Wq': xavier(ks[1], (D_MODEL, KEY_DIM)), 'Wk': xavier(ks[2], (D_MODEL, KEY_DIM)), 'Wv': xavier(ks[3], (D_MODEL, VALUE_DIM)), 'Wg': xavier(ks[4], (D_MODEL, VALUE_DIM)), 'gk_w1': xavier(ks[5], (D_MODEL, LOW_RANK)), 'gk_w2': xavier(ks[6], (LOW_RANK, KEY_DIM)), 'gk_b2': jnp.zeros((KEY_DIM,), jnp.float32), 'g_norm_w': jnp.ones((DV,), jnp.float32), 'Wo': xavier(ks[7], (VALUE_DIM, D_MODEL))}
    _L0_attn_all = _L0_attn_setup()
    _L0_attn_in = {k: v for k, v in _L0_attn_all.items() if k in ('Wq', 'Wk', 'Wv', 'Wg', 'gk_w1', 'gk_w2', 'gk_b2', 'g_norm_w', 'Wo')}
    del _L0_attn_all

    def _L0_ffn_setup():
        import jax, jax.numpy as jnp
        import numpy as np
        DIM = 256
        N_EXPERTS = 8
        D_FF = 512
        TOP_K = 2
        key = jax.random.key(seed)
        ks = jax.random.split(key, 5)
        s = 0.02
        return {'x': jax.random.normal(ks[0], (2, 512, DIM), dtype=jnp.float32), 'gate_w': jax.random.normal(ks[1], (N_EXPERTS, DIM), dtype=jnp.float32) * s, 'w1': jax.random.normal(ks[2], (N_EXPERTS, D_FF, DIM), dtype=jnp.float32) * s, 'w2': jax.random.normal(ks[3], (N_EXPERTS, DIM, D_FF), dtype=jnp.float32) * s, 'w3': jax.random.normal(ks[4], (N_EXPERTS, D_FF, DIM), dtype=jnp.float32) * s}
    _L0_ffn_all = _L0_ffn_setup()
    _L0_ffn_in = {k: v for k, v in _L0_ffn_all.items() if k in ('gate_w', 'w1', 'w2', 'w3')}
    del _L0_ffn_all
    return {'x': x, 'cls_tok': cls_tok, 'L0_tok_log_dt': _L0_tok_in['log_dt'], 'L0_tok_inv_A_real': _L0_tok_in['inv_A_real'], 'L0_tok_A_imag': _L0_tok_in['A_imag'], 'L0_tok_B_ri': _L0_tok_in['B_ri'], 'L0_attn_Wq': _L0_attn_in['Wq'], 'L0_attn_Wk': _L0_attn_in['Wk'], 'L0_attn_Wv': _L0_attn_in['Wv'], 'L0_attn_Wg': _L0_attn_in['Wg'], 'L0_attn_gk_w1': _L0_attn_in['gk_w1'], 'L0_attn_gk_w2': _L0_attn_in['gk_w2'], 'L0_attn_gk_b2': _L0_attn_in['gk_b2'], 'L0_attn_g_norm_w': _L0_attn_in['g_norm_w'], 'L0_attn_Wo': _L0_attn_in['Wo'], 'L0_ffn_gate_w': _L0_ffn_in['gate_w'], 'L0_ffn_w1': _L0_ffn_in['w1'], 'L0_ffn_w2': _L0_ffn_in['w2'], 'L0_ffn_w3': _L0_ffn_in['w3']}

def reference(x, cls_tok, L0_tok_log_dt, L0_tok_inv_A_real, L0_tok_A_imag, L0_tok_B_ri, L0_attn_Wq, L0_attn_Wk, L0_attn_Wv, L0_attn_Wg, L0_attn_gk_w1, L0_attn_gk_w2, L0_attn_gk_b2, L0_attn_g_norm_w, L0_attn_Wo, L0_ffn_gate_w, L0_ffn_w1, L0_ffn_w2, L0_ffn_w3):
    import jax
    import jax.numpy as jnp

    def _L0_tok_ref(log_dt, inv_A_real, A_imag, B_ri, C_ri, L):
        import jax, jax.numpy as jnp
        import numpy as np
        import math
        H = 256
        N = 64
        CH = 1
        SEQ_L = 256
        dt = jnp.exp(log_dt)
        A = -jnp.exp(inv_A_real) + 1j * A_imag
        B = B_ri[..., 0] + 1j * B_ri[..., 1]
        C = C_ri[..., 0] + 1j * C_ri[..., 1]
        dtA = A * dt[:, None]
        dA = (1.0 + dtA / 2) / (1.0 - dtA / 2)
        C_term = C * B[None]
        log_dA = jnp.log(dA)
        V = jnp.exp(log_dA[:, :, None] * jnp.arange(L))
        K = 2.0 * jnp.einsum('chn,hnl->chl', C_term, V).real
        return K.astype(jnp.float32)

    def _L0_attn_ref(x, Wq, Wk, Wv, Wg, gk_w1, gk_w2, gk_b2, g_norm_w, Wo):
        import jax, jax.numpy as jnp
        import numpy as np
        D_MODEL = 256
        N_HEADS = 4
        KEY_DIM = 256
        VALUE_DIM = 512
        DK = KEY_DIM // N_HEADS
        DV = VALUE_DIM // N_HEADS
        LOW_RANK = 16
        GATE_NORM = 16.0
        EPS = 1e-05

        def _gla_scan(q, k, v, gk):
            B, H, L, dk = q.shape
            dv = v.shape[-1]
            qs = jnp.moveaxis(q, 2, 0)
            ks_ = jnp.moveaxis(k, 2, 0)
            vs = jnp.moveaxis(v, 2, 0)
            gs = jnp.moveaxis(gk, 2, 0)

            def step(S, inp):
                q_t, k_t, v_t, g_t = inp
                S = S * jnp.exp(g_t)[..., None] + k_t[..., None] * v_t[..., None, :]
                o_t = jnp.einsum('bhk,bhkv->bhv', q_t, S)
                return (S, o_t)
            S0 = jnp.zeros((B, H, dk, dv), q.dtype)
            _, os = jax.lax.scan(step, S0, (qs, ks_, vs, gs))
            return jnp.moveaxis(os, 0, 2)
        B, L, _ = x.shape
        scale = DK ** (-0.5)

        def heads(t, d):
            return t.reshape(B, L, N_HEADS, d).transpose(0, 2, 1, 3)
        q = heads(x @ Wq, DK) * scale
        k = heads(x @ Wk, DK)
        v = heads(x @ Wv, DV)
        gk = heads(jax.nn.log_sigmoid(x @ gk_w1 @ gk_w2 + gk_b2) / GATE_NORM, DK)
        o = _gla_scan(q, k, v, gk)
        o = o.transpose(0, 2, 1, 3)
        g = (x @ Wg).reshape(B, L, N_HEADS, DV)
        rms = o * jax.lax.rsqrt(jnp.mean(o * o, axis=-1, keepdims=True) + EPS)
        o = rms * g_norm_w * (g * jax.nn.sigmoid(g))
        o = o.reshape(B, L, VALUE_DIM)
        return o @ Wo

    def _L0_ffn_ref(x, gate_w, w1, w2, w3):
        import jax, jax.numpy as jnp
        import numpy as np
        DIM = 256
        N_EXPERTS = 8
        D_FF = 512
        TOP_K = 2
        orig_shape = x.shape
        xf = x.reshape(-1, orig_shape[-1])
        scores = jnp.einsum('td,ed->te', xf, gate_w)
        probs = jax.nn.softmax(scores.astype(jnp.float32), axis=-1)
        weights, idx = jax.lax.top_k(probs, TOP_K)
        weights = weights / jnp.sum(weights, axis=-1, keepdims=True)
        weights = weights.astype(x.dtype)
        x1 = jax.nn.silu(jnp.einsum('td,efd->tef', xf, w1))
        x3 = jnp.einsum('td,efd->tef', xf, w3)
        out_all = jnp.einsum('tef,edf->ted', x1 * x3, w2)
        expert_outs = jnp.take_along_axis(out_all, idx[:, :, None], axis=1)
        result = jnp.einsum('tkd,tk->td', expert_outs, weights)
        return result.reshape(orig_shape)
    h = _L0_tok_ref(L0_tok_log_dt, L0_tok_inv_A_real, L0_tok_A_imag, L0_tok_B_ri, x, 256)
    h = jnp.concatenate([jnp.broadcast_to(cls_tok, (h.shape[0], 1, h.shape[2])), h], axis=1)
    h = h + _L0_attn_ref(_layernorm(h, axis=-1), L0_attn_Wq, L0_attn_Wk, L0_attn_Wv, L0_attn_Wg, L0_attn_gk_w1, L0_attn_gk_w2, L0_attn_gk_b2, L0_attn_g_norm_w, L0_attn_Wo)
    h = h + _L0_ffn_ref(_layernorm(h, axis=-1), L0_ffn_gate_w, L0_ffn_w1, L0_ffn_w2, L0_ffn_w3)
    return h

_drawn_inputs = setup_inputs


def setup_inputs(seed=0):
    import zlib

    import numpy as np

    out = dict(_drawn_inputs(seed))
    spreads = {'L0_attn_gk_b2': (0.0, 0.8), 'L0_attn_g_norm_w': (1.0, 0.6)}
    factors = {'cls_tok': 8.0,
     'L0_attn_Wq': 8.0,
     'L0_attn_Wk': 8.0,
     'L0_attn_Wv': 8.0,
     'L0_attn_Wg': 8.0,
     'L0_attn_gk_w1': 8.0,
     'L0_attn_gk_w2': 8.0,
     'L0_attn_Wo': 8.0,
     'L0_ffn_gate_w': 8.0,
     'L0_ffn_w1': 8.0,
     'L0_ffn_w2': 8.0,
     'L0_ffn_w3': 8.0}
    for name, (base, spread) in spreads.items():
        noise = np.random.default_rng([zlib.crc32(name.encode()), seed]).standard_normal(out[name].shape)
        drawn = base * np.exp(spread * noise) if base else spread * noise
        out[name] = jnp.asarray(drawn.astype(out[name].dtype))
    for name, factor in factors.items():
        out[name] = (out[name] * factor).astype(out[name].dtype)
    return out
```

```python
from contextlib import ExitStack
import math

import numpy as np
import concourse.bass as bass
from concourse import mybir

F32 = mybir.dt.float32
I32 = mybir.dt.int32
U32 = mybir.dt.uint32
ALU = mybir.AluOpType
ACT = mybir.ActivationFunctionType

P = 128
BATCH = 8
TOK = 256
D = 256
N_STATE = 64

HEADS = 4
DK = 64
DV = 128
VD = HEADS * DV
RANK = 16
CH = 2
SUB = 32
NSUB = P // SUB
GATE_NORM = 16.0
EPS = 1e-5
E = 8
FF = 512
EW = 2 * 2 * FF + FF // P * D
TILES = BATCH * CH
REGION = BATCH * TOK + P + 8
SPARE = E * REGION
PAIRED = 2 * (BATCH * TOK + 1)
SLOTS = -(-((PAIRED + E * (P - 1)) // P) // 2) * 2

PAIRS = TOK // 2
LOW = 8
POW = 64
SHIFTS = D // POW
GROUP = 16
TURNS = PAIRS // GROUP
ROWS = 2 * BATCH * SHIFTS


def stage_kernel(nc, ctx, params, bri, crv, h_rows, loads):
    def sb(name, shape, dt=F32):
        return ctx.enter_context(nc.sbuf_tensor(name, shape, dt))

    def sem(name):
        return ctx.enter_context(nc.semaphore(name))

    logs = sb("logs", [P, 3, PAIRS])
    b_in = sb("b_in", [P, 2, PAIRS])
    c_in = sb("c_in", [P, 2, PAIRS, BATCH])
    et = sb("et", [P, 2, PAIRS])
    ek = sb("ek", [P, 2, PAIRS])
    er = sb("er", [P, 2, PAIRS])
    ep = sb("ep", [P, 2, PAIRS])
    ei = sb("ei", [P, 2, PAIRS], I32)
    ab = sb("ab", [P, 2, PAIRS])
    tmp = sb("tmp", [P, 4, PAIRS])
    zp = sb("zp", [P, 8, 2, PAIRS])
    low = sb("low", [P, 2, PAIRS, LOW])
    lt = sb("lt", [P, 2, 2, PAIRS, 4])
    w = sb("w", [P, 3, PAIRS, SHIFTS])
    v = [sb(f"v{u}", [P, 2, GROUP, POW]) for u in range(2)]
    vt = sb("vt", [P, 2, 2, GROUP, POW // 2])
    x = [sb(f"x{u}", [P, 2, GROUP, ROWS]) for u in range(2)]
    xt = sb("xt", [P, 2, 2, GROUP, BATCH, SHIFTS])
    k_sb = [sb(f"k_sb{u}", [ROWS, GROUP, POW]) for u in range(2)]
    k_ps = [ctx.enter_context(nc.psum_tensor(f"k_ps{u}", [ROWS, GROUP, POW], F32)) for u in range(2)]

    params_in = sem("params_in")
    chain = sem("a_chain")
    powers_ready = sem("powers_ready")
    xzero = sem("xzero")
    v_step = sem("v_step")
    v_ready = sem("v_ready")
    x_step = sem("x_step")
    x_ready = sem("x_ready")
    products_done = sem("products_done")
    k_copied = sem("k_copied")
    k_stored = [sem(f"k_stored{u}") for u in range(2)]

    with nc.Block() as block:
        @block.sync
        def _(sp):
            sp.dma_start(logs[:], params).then_inc(params_in, 16)
            sp.dma_start(b_in[:], bri).then_inc(params_in, 16)
            sp.dma_start(c_in[:], crv).then_inc(params_in, 16)
            loads(sp)

            def turn(t, u):
                sp.wait_ge(k_copied, t + 1)
                for par in range(2):
                    half = ROWS // 2
                    src = k_sb[u][par * half:(par + 1) * half]
                    dst = h_rows[bass.ds(t * 2 * GROUP + par, GROUP, step=2)] \
                        .rearrange("j c (a b) -> (c a) j b", b=POW)
                    sp.dma_start(dst, src).then_inc(k_stored[u], 16)

            with sp.Fori(0, TURNS // 2) as i:
                for u in range(2):
                    turn(2 * i + u, u)
            for u in range(2):
                sp.wait_ge(k_stored[u], 16 * TURNS)

        @block.vector
        def _(dve):
            count = [0]

            def link(ins):
                count[0] += 1
                ins.then_inc(chain, 1)
                dve.wait_ge(chain, count[0])

            dve.wait_ge(params_in, 48)
            big = 1.5 * 2.0 ** 23
            lg = logs[:, 0:2]
            link(nc.vector.tensor_scalar(et[:], lg, 1.0 / math.log(2.0), big, ALU.mult, ALU.add))
            link(nc.vector.tensor_scalar(ek[:], et[:], -big, -126.0, ALU.add, ALU.max))
            hi = 0.693359375
            link(nc.vector.scalar_tensor_tensor(er[:], ek[:], -hi, lg, ALU.mult, ALU.add))
            link(nc.vector.scalar_tensor_tensor(er[:], ek[:], hi - math.log(2.0), er[:], ALU.mult, ALU.add))
            link(nc.vector.tensor_scalar(et[:], ek[:], 127.0, 2.0 ** 23, ALU.add, ALU.mult))
            link(nc.vector.tensor_copy(ei[:], et[:]))
            link(nc.vector.tensor_scalar(ep[:], er[:], 1.0 / math.factorial(7), None, ALU.mult))
            for k in range(6, 0, -1):
                link(nc.vector.scalar_tensor_tensor(ep[:], ep[:], 1.0 / math.factorial(k), er[:], ALU.add, ALU.mult))
            link(nc.vector.scalar_tensor_tensor(ek[:], ep[:], 1.0, ei[:].bitcast(F32), ALU.add, ALU.mult))
            link(nc.vector.scalar_tensor_tensor(ab[:, 0], ek[:, 1], 0.5, ek[:, 0], ALU.mult, ALU.mult))
            link(nc.vector.scalar_tensor_tensor(ab[:, 1], logs[:, 2], 0.5, ek[:, 0], ALU.mult, ALU.mult))
            a, b = ab[:, 0], ab[:, 1]
            link(nc.vector.tensor_scalar(tmp[:, 0], a, 1.0, None, ALU.add))
            link(nc.vector.tensor_tensor(tmp[:, 0], tmp[:, 0], tmp[:, 0], ALU.mult))
            link(nc.vector.tensor_tensor(tmp[:, 1], b, b, ALU.mult))
            link(nc.vector.tensor_tensor(tmp[:, 0], tmp[:, 0], tmp[:, 1], ALU.add))
            link(nc.vector.reciprocal(tmp[:, 0], tmp[:, 0]))
            link(nc.vector.tensor_tensor(tmp[:, 2], a, a, ALU.mult))
            link(nc.vector.tensor_tensor(tmp[:, 2], tmp[:, 2], tmp[:, 1], ALU.add))
            link(nc.vector.tensor_scalar(tmp[:, 2], tmp[:, 2], -1.0, 1.0, ALU.mult, ALU.add))
            link(nc.vector.tensor_tensor(zp[:, 0, 0], tmp[:, 2], tmp[:, 0], ALU.mult))
            link(nc.vector.scalar_tensor_tensor(zp[:, 0, 1], b, 2.0, tmp[:, 0], ALU.mult, ALU.mult))
            for k in range(1, 8):
                zr, zi = zp[:, k - 1, 0], zp[:, k - 1, 1]
                nc.vector.tensor_tensor(tmp[:, 0:2], zp[:, k - 1], zp[:, k - 1], ALU.mult).then_inc(chain, 1)
                count[0] += 1
                link(nc.vector.scalar_tensor_tensor(zp[:, k, 1], zr, 2.0, zi, ALU.mult, ALU.mult))
                link(nc.vector.tensor_tensor(zp[:, k, 0], tmp[:, 0], tmp[:, 1], ALU.subtract))

            def times(out_re, out_im, p, q, zr, zi, src, op_im=ALU.add, neg=False):
                nc.vector.tensor_tensor(p, src, zr, ALU.mult).then_inc(chain, 1)
                count[0] += 1
                link(nc.vector.tensor_tensor(q, src, zi, ALU.mult))
                nc.vector.tensor_tensor(out_re, p[:, 0], q[:, 1], ALU.subtract).then_inc(chain, 1)
                count[0] += 1
                link(nc.vector.tensor_tensor(out_im, p[:, 1], q[:, 0], ALU.add))

            link(nc.vector.memset(low[:, 0, :, 0:1], 1.0))
            link(nc.vector.memset(low[:, 1, :, 0:1], 0.0))
            link(nc.vector.tensor_copy(low[:, :, :, 1], zp[:, 0]))
            for k in (1, 2):
                n = 2 ** k
                zr = zp[:, k, 0].unsqueeze(1).unsqueeze(3).to_broadcast([P, 2, PAIRS, n])
                zi = zp[:, k, 1].unsqueeze(1).unsqueeze(3).to_broadcast([P, 2, PAIRS, n])
                times(low[:, 0, :, n:2 * n], low[:, 1, :, n:2 * n], lt[:, 0, :, :, 0:n], lt[:, 1, :, :, 0:n],
                      zr, zi, low[:, :, :, 0:n])
            link(nc.vector.tensor_scalar(tmp[:, 0:2], b_in[:], 2.0, None, ALU.mult))
            cur = tmp[:, 0:2]
            wsrc = sb("wsrc", [P, SHIFTS, 2, PAIRS])
            link(nc.vector.tensor_copy(wsrc[:, 0], cur))
            for dst, src, k in ((1, 0, 6), (2, 0, 7), (3, 1, 7)):
                zr = zp[:, k, 0].unsqueeze(1).to_broadcast([P, 2, PAIRS])
                zi = zp[:, k, 1].unsqueeze(1).to_broadcast([P, 2, PAIRS])
                times(wsrc[:, dst, 0], wsrc[:, dst, 1], tmp[:, 0:2], tmp[:, 2:4], zr, zi, wsrc[:, src])
            link(nc.vector.tensor_copy(w[:, 0], wsrc[:, :, 0].rearrange("p a j -> p j a")))
            link(nc.vector.tensor_scalar(w[:, 1], wsrc[:, :, 1].rearrange("p a j -> p j a"), -1.0, None, ALU.mult))
            nc.vector.tensor_scalar(w[:, 2], wsrc[:, :, 0].rearrange("p a j -> p j a"), -1.0, None, ALU.mult) \
                .then_inc(powers_ready, 1)

            per_turn = 13

            def turn(t, u, first):
                base = t * per_turn
                js = bass.ds(t * GROUP, GROUP)
                if not first:
                    dve.wait_ge(products_done, t - 1)
                nc.vector.tensor_copy(v[u][:, :, :, 0:LOW], low[:, :, js, :]).then_inc(v_step, 1)
                dve.wait_ge(v_step, base + 1)
                done = 1
                for k in (3, 4, 5):
                    n = 2 ** k
                    zr = zp[:, k, 0, js].unsqueeze(1).unsqueeze(3).to_broadcast([P, 2, GROUP, n])
                    zi = zp[:, k, 1, js].unsqueeze(1).unsqueeze(3).to_broadcast([P, 2, GROUP, n])
                    p, q = vt[:, 0, :, :, 0:n], vt[:, 1, :, :, 0:n]
                    nc.vector.tensor_tensor(p, v[u][:, :, :, 0:n], zr, ALU.mult).then_inc(v_step, 1)
                    nc.vector.tensor_tensor(q, v[u][:, :, :, 0:n], zi, ALU.mult).then_inc(v_step, 1)
                    done += 2
                    dve.wait_ge(v_step, base + done)
                    nc.vector.tensor_tensor(v[u][:, 0, :, n:2 * n], p[:, 0], q[:, 1], ALU.subtract).then_inc(v_step, 1)
                    last = nc.vector.tensor_tensor(v[u][:, 1, :, n:2 * n], p[:, 1], q[:, 0], ALU.add)
                    last.then_inc(v_step, 1)
                    done += 2
                    dve.wait_ge(v_step, base + done)
                nc.vector.sem_inc(v_ready, 1)

            for u in range(2):
                turn(u, u, True)
            with dve.Fori(1, TURNS // 2) as i:
                for u in range(2):
                    turn(2 * i + u, u, False)

        @block.gpsimd
        def _(pool):
            for u in range(2):
                nc.gpsimd.memset(x[u][:], 0.0).then_inc(xzero, 1)
            pool.wait_ge(xzero, 2)
            pool.wait_ge(powers_ready, 1)

            def turn(t, u, first):
                js = bass.ds(t * GROUP, GROUP)
                shape = [P, GROUP, BATCH, SHIFTS]
                for half in range(2):
                    for r in range(2):
                        cc = c_in[:, half, js].unsqueeze(3).to_broadcast(shape)
                        ww = w[:, half + r, js].unsqueeze(2).to_broadcast(shape)
                        nc.gpsimd.tensor_tensor(xt[:, half, r], cc, ww, ALU.mult).then_inc(x_step, 1)
                pool.wait_ge(x_step, 6 * t + 4)
                if not first:
                    pool.wait_ge(products_done, t - 1)
                for par in range(2):
                    ps = slice(par * N_STATE, (par + 1) * N_STATE)
                    cols = slice(par * ROWS // 2, (par + 1) * ROWS // 2)
                    nc.gpsimd.tensor_tensor(x[u][ps, :, :, cols], xt[ps, 0].rearrange("p r j c a -> p r j (c a)"),
                                            xt[ps, 1].rearrange("p r j c a -> p r j (c a)"), ALU.add) \
                        .then_inc(x_step, 1)
                pool.wait_ge(x_step, 6 * t + 6)
                nc.gpsimd.sem_inc(x_ready, 1)

            for u in range(2):
                turn(u, u, True)
            with pool.Fori(1, TURNS // 2) as i:
                for u in range(2):
                    turn(2 * i + u, u, False)

        @block.tensor
        def _(pe):
            def turn(t, u, first):
                pe.wait_ge(x_ready, t + 1)
                pe.wait_ge(v_ready, t + 1)
                if not first:
                    pe.wait_ge(k_copied, t - 1)
                for j in range(GROUP):
                    for r in range(2):
                        last = nc.tensor.matmul(k_ps[u][:, j], x[u][:, r, j], v[u][:, r, j],
                                                start=(r == 0), stop=(r == 1))
                last.then_inc(products_done, 1)

            for u in range(2):
                turn(u, u, True)
            with pe.Fori(1, TURNS // 2) as i:
                for u in range(2):
                    turn(2 * i + u, u, False)

        @block.scalar
        def _(act):
            def turn(t, u, first):
                act.wait_ge(products_done, t + 1)
                if not first:
                    act.wait_ge(k_stored[u], 16 * (t - u))
                nc.scalar.copy(k_sb[u][:], k_ps[u][:]).then_inc(k_copied, 1)

            for u in range(2):
                turn(u, u, True)
            with act.Fori(1, TURNS // 2) as i:
                for u in range(2):
                    turn(2 * i + u, u, False)



class Steps:

    def __init__(self, eng, sem, base=0, apart=None):
        self.eng, self.sem, self.base, self.n, self.apart = eng, sem, base, 0, apart

    def mark(self, ins):
        ins.then_inc(self.sem, 1)
        self.n += 1

    def wait(self):
        self.eng.wait_ge(self.sem, self.base + self.n)

    def wait_apart(self):
        self.wait()
        self.eng.sem_inc(self.apart, 1)

    def link(self, ins):
        self.mark(ins)
        self.wait()


def moments(nc, st, src, stats, mom):
    st.mark(nc.vector.bn_stats(stats, src))
    if st.apart is None:
        st.wait()
    else:
        st.wait_apart()
    st.link(nc.vector.bn_aggr(mom, stats))


def rsqrt(nc, st, out, src, scale, eps):
    st.link(nc.scalar.activation(out, src, ACT.Ln, scale=scale, bias=eps))
    return nc.scalar.activation(out, out, ACT.Exp, scale=-0.5)


class Shared:

    def __init__(self, nc, ctx):
        def sb(name, shape, dt=F32):
            return ctx.enter_context(nc.sbuf_tensor(name, shape, dt))

        self.wq = sb("wq", [P, 2, D])
        self.wk = sb("wk", [P, 2, D])
        self.wv = sb("wv", [P, 2, VD])
        self.wg = sb("wg", [P, 2, VD])
        self.wo = sb("wo", [P, HEADS, D])
        self.gw1 = sb("gw1", [P, 2, RANK])
        self.gw2 = sb("gw2", [RANK, D])
        self.gb2 = sb("gb2", [P, 2])
        self.gnorm = sb("gnorm", [P, 1])
        self.gate = sb("gate", [P, 2, E])
        self.cls = sb("cls", [1, D])
        self.one = sb("one", [1, 1])
        self.eps = sb("eps", [P, 1])
        self.ident = sb("ident", [P, P])
        self.causal = sb("causal", [P, P])
        self.before = sb("before", [P, P])
        self.ones = sb("ones", [P, P])
        self.iota8 = sb("iota8", [P, E])
        self.region = sb("region", [P, E])
        self.spare = sb("spare", [P, 1])
        self.row0 = sb("row0", [P, 1])
        self.keep = sb("keep", [P, CH * 2 * P])
        self.s_cls = sb("s_cls", [P, 2, 2 * DV])
        self.h2 = sb("h2", [P, TILES + 1, D])
        self.x2c = sb("x2c", [P, D])
        self.sc_cls = sb("sc_cls", [P, E])
        self.top = sb("top", [P, TILES + 1, 8])
        self.pos = sb("pos", [P, TILES + 1, 2])
        self.carry = sb("carry", [P, E])
        self.experts_in = [ctx.enter_context(nc.semaphore(f"experts_in{e}")) for e in range(E)]
        self.weights_in = ctx.enter_context(nc.semaphore("weights_in"))


def load_weights(sp, sh, ins):
    pairs = [(sh.wq, ins["Wq"].rearrange("(k p) n -> p k n", p=P)), (sh.wk, ins["Wk"].rearrange("(k p) n -> p k n", p=P)),
             (sh.wv, ins["Wv"].rearrange("(k p) n -> p k n", p=P)), (sh.wg, ins["Wg"].rearrange("(k p) n -> p k n", p=P)),
             (sh.wo, ins["Wo"].rearrange("(k p) n -> p k n", p=P)), (sh.gw1, ins["gk_w1"].rearrange("(k p) n -> p k n", p=P)),
             (sh.gw2, ins["gk_w2"]), (sh.gb2, ins["gk_b2"]), (sh.gnorm, ins["gnorm"]), (sh.gate, ins["gate"]), (sh.cls, ins["cls"])]
    for dst, src in pairs:
        sp.dma_start(dst[:], src).then_inc(sh.weights_in, 16)
    return 16 * len(pairs)


def stage_class_token(nc, ctx, sh, bk, weights_count):
    def sb(name, shape, dt=F32):
        return ctx.enter_context(nc.sbuf_tensor(name, shape, dt))

    xn = sb("c_xn", [1, D])
    stats = sb("c_stats", [1, 6])
    mom = sb("c_mom", [1, 2])
    xc = sb("c_xc", [P, 2])
    qk = sb("c_qk", [1, 2, D])
    vg = sb("c_vg", [1, 2, VD])
    og = sb("c_og", [1, VD])
    sq = sb("c_sq", [1, VD])
    dot = sb("c_dot", [1, 2, HEADS])
    oc = sb("c_oc", [P, HEADS])
    x2t = sb("c_x2t", [P, 2])
    self_chain = ctx.enter_context(nc.semaphore("c_chain"))
    pool_made = ctx.enter_context(nc.semaphore("c_pool_made"))
    eps_made = ctx.enter_context(nc.semaphore("c_eps_made"))
    a_chain = ctx.enter_context(nc.semaphore("c_act_chain"))
    rstd = sb("c_rstd", [1, 2])
    dve_did = ctx.enter_context(nc.semaphore("c_dve_did"))
    act_did = ctx.enter_context(nc.semaphore("c_act_did"))
    pe_did = ctx.enter_context(nc.semaphore("c_pe_did"))

    with nc.Block() as block:
        @block.gpsimd
        def _(pool):
            nc.gpsimd.memset(sh.ident[:], 0.0).then_inc(pool_made, 1)
            nc.gpsimd.memset(sh.causal[:], 1.0).then_inc(pool_made, 1)
            nc.gpsimd.memset(sh.before[:], 1.0).then_inc(pool_made, 1)
            nc.gpsimd.memset(sh.ones[:], 1.0).then_inc(pool_made, 1)
            nc.gpsimd.memset(sh.keep[:], 1.0).then_inc(pool_made, 1)
            nc.gpsimd.memset(sh.row0[:], 0.0).then_inc(pool_made, 1)
            pool.wait_ge(pool_made, 6)
            nc.gpsimd.affine_select(out=sh.ident[:], in_=sh.ident[:], compare_op=ALU.not_equal, fill=1.0, base=0,
                                    pattern=[[-1, P]], channel_multiplier=1).then_inc(pool_made, 1)
            nc.gpsimd.affine_select(out=sh.causal[:], in_=sh.causal[:], compare_op=ALU.is_ge, fill=0.0, base=0,
                                    pattern=[[1, P]], channel_multiplier=-1).then_inc(pool_made, 1)
            nc.gpsimd.affine_select(out=sh.before[:], in_=sh.before[:], compare_op=ALU.is_ge, fill=0.0, base=-1,
                                    pattern=[[1, P]], channel_multiplier=-1).then_inc(pool_made, 1)
            nc.gpsimd.affine_select(out=sh.row0[:], in_=sh.row0[:], compare_op=ALU.not_equal, fill=1.0, base=0,
                                    pattern=[[0, 1]], channel_multiplier=1).then_inc(pool_made, 1)
            nc.gpsimd.memset(sh.keep[:].rearrange("p (b s) -> p b s", s=SUB)[:, :, 0:1], 0.0).then_inc(pool_made, 1)
            nc.gpsimd.iota(sh.iota8[:], [[1, E]], base=0, channel_multiplier=0,
                           allow_small_or_imprecise_dtypes=True).then_inc(pool_made, 1)
            nc.gpsimd.iota(sh.region[:], [[REGION, E]], base=0, channel_multiplier=0,
                           allow_small_or_imprecise_dtypes=True).then_inc(pool_made, 1)
            nc.gpsimd.iota(sh.spare[:], [[0, 1]], base=SPARE, channel_multiplier=1,
                           allow_small_or_imprecise_dtypes=True).then_inc(pool_made, 1)
            nc.gpsimd.memset(sh.x2c[:], 0.0).then_inc(pool_made, 1)
            nc.gpsimd.memset(sh.s_cls[:], 0.0).then_inc(pool_made, 1)
            nc.gpsimd.memset(sh.h2[:, TILES], 0.0).then_inc(pool_made, 1)
            nc.gpsimd.memset(sh.eps[:], EPS).then_inc(eps_made, 1)
            nc.gpsimd.memset(sh.sc_cls[:], 0.0).then_inc(pool_made, 1)

        @block.vector
        def _(dve):
            st = Steps(dve, self_chain)
            dve.wait_ge(sh.weights_in, weights_count)
            st.link(nc.vector.memset(sh.one[:], 1.0))
            moments(nc, st, sh.cls[:], stats[:], mom[:])
            nc.vector.sem_inc(dve_did, 1)
            st.link(nc.vector.tensor_scalar(sh.wo[:], sh.wo[:], sh.gnorm[:], None, ALU.mult))
            dve.wait_ge(act_did, 1)
            st.link(nc.vector.tensor_scalar(xn[:], sh.cls[:], mom[:, 0:1], rstd[:, 0:1], ALU.subtract, ALU.mult))
            nc.vector.sem_inc(dve_did, 1)
            dve.wait_ge(pe_did, 2)
            st.mark(nc.vector.tensor_copy(qk[:], bk[1][0:1].rearrange("p (r n) -> p r n", r=2)))
            st.link(nc.vector.tensor_copy(vg[:, 0], bk[2][0:1]))
            nc.vector.sem_inc(dve_did, 1)
            st.link(nc.vector.scalar_tensor_tensor(sq[:, 0:D], qk[:, 0], DK ** -0.5, qk[:, 1], ALU.mult, ALU.mult))
            st.link(nc.vector.reduce_sum(dot[:, 0], sq[:, 0:D].rearrange("p (h c) -> p h c", c=DK), axis=mybir.AxisListType.X))
            bh = dot[:, 0].unsqueeze(2).to_broadcast([1, HEADS, DV])
            hv = lambda t: t.rearrange("p (h c) -> p h c", c=DV)
            st.link(nc.vector.tensor_tensor(hv(og[:]), hv(vg[:, 0]), bh, ALU.mult))
            st.link(nc.vector.tensor_tensor(sq[:], og[:], og[:], ALU.mult))
            st.link(nc.vector.reduce_sum(dot[:, 1], hv(sq[:]), axis=mybir.AxisListType.X))
            nc.vector.sem_inc(dve_did, 1)
            dve.wait_ge(act_did, 4)
            br = dot[:, 1].unsqueeze(2).to_broadcast([1, HEADS, DV])
            st.link(nc.vector.tensor_tensor(hv(og[:]), hv(og[:]), br, ALU.mult))
            st.link(nc.vector.tensor_tensor(og[:], og[:], vg[:, 1], ALU.mult))
            nc.vector.sem_inc(dve_did, 1)
            dve.wait_ge(pe_did, 3)
            dve.wait_ge(pool_made, 18)
            for par in range(2):
                rows, cols = slice(par * DK, (par + 1) * DK), slice(par * DV, (par + 1) * DV)
                st.link(nc.vector.tensor_copy(sh.s_cls[rows, :, cols], bk[4][rows].rearrange("p (t n) -> p t n", t=2)[:, :, cols]))
            dve.wait_ge(pe_did, 5)
            dve.wait_ge(pool_made, 18)
            st.link(nc.vector.tensor_tensor(sh.h2[0:1, TILES], bk[6][0:1, 0:D], sh.cls[:], ALU.add))
            moments(nc, st, sh.h2[0:1, TILES], stats[:], mom[:])
            nc.vector.sem_inc(dve_did, 1)
            dve.wait_ge(act_did, 6)
            st.link(nc.vector.tensor_scalar(sh.x2c[0:1], sh.h2[0:1, TILES], mom[:, 0:1], rstd[:, 1:2], ALU.subtract, ALU.mult))
            nc.vector.sem_inc(dve_did, 1)
            dve.wait_ge(pe_did, 7)
            st.link(nc.vector.tensor_copy(sh.sc_cls[0:1], bk[0][0:1, 16:16 + E]))

        @block.tensor
        def _(pe):
            def column(out, row, n):
                for k in range(n):
                    last = nc.tensor.matmul(out[:, k:k + 1], row[:, k * P:(k + 1) * P], sh.one[:], start=True, stop=True)
                return last

            def rows(out, lhs, w):
                for k in range(2):
                    last = nc.tensor.matmul(out, lhs[:, k:k + 1], w[:, k], start=(k == 0), stop=(k == 1))
                return last

            pe.wait_ge(dve_did, 2)
            column(bk[0], xn, 2).then_inc(pe_did, 1)
            pe.wait_ge(act_did, 2)
            rows(bk[1][0:1, 0:D], xc, sh.wq)
            rows(bk[1][0:1, D:2 * D], xc, sh.wk)
            rows(bk[2][0:1, :], xc, sh.wv)
            rows(bk[3][0:1, :], xc, sh.wg).then_inc(pe_did, 1)
            pe.wait_ge(dve_did, 3)
            for t in range(2):
                last = nc.tensor.matmul(bk[4][:, t * D:(t + 1) * D], qk[:, 1, t * P:(t + 1) * P],
                                        vg[:, 0, t * D:(t + 1) * D], start=True, stop=True)
            last.then_inc(pe_did, 1)
            pe.wait_ge(dve_did, 5)
            column(bk[5], og, HEADS).then_inc(pe_did, 1)
            pe.wait_ge(act_did, 5)
            for h in range(HEADS):
                last = nc.tensor.matmul(bk[6][0:1, 0:D], oc[:, h:h + 1], sh.wo[:, h], start=(h == 0), stop=(h == HEADS - 1))
            last.then_inc(pe_did, 1)
            pe.wait_ge(dve_did, 7)
            column(bk[7], sh.x2c[0:1], 2).then_inc(pe_did, 1)
            pe.wait_ge(act_did, 7)
            rows(bk[0][0:1, 16:16 + E], x2t, sh.gate).then_inc(pe_did, 1)

        @block.scalar
        def _(act):
            st = Steps(act, a_chain)
            act.wait_ge(eps_made, 1)
            act.wait_ge(dve_did, 1)
            rsqrt(nc, st, rstd[:, 0:1], mom[:, 1:2], 1.0, sh.eps[0:1]).then_inc(act_did, 1)
            act.wait_ge(pe_did, 1)
            nc.scalar.copy(xc[:], bk[0][:, 0:2]).then_inc(act_did, 1)
            act.wait_ge(pe_did, 2)
            nc.scalar.activation(vg[:, 1], bk[3][0:1, :], ACT.Silu).then_inc(act_did, 1)
            act.wait_ge(dve_did, 4)
            rsqrt(nc, st, dot[:, 1], dot[:, 1], 1.0 / DV, sh.eps[0:1]).then_inc(act_did, 1)
            act.wait_ge(pe_did, 4)
            nc.scalar.copy(oc[:], bk[5][:, 0:HEADS]).then_inc(act_did, 1)
            act.wait_ge(dve_did, 6)
            rsqrt(nc, st, rstd[:, 1:2], mom[:, 1:2], 1.0, sh.eps[0:1]).then_inc(act_did, 1)
            act.wait_ge(pe_did, 6)
            nc.scalar.copy(x2t[:], bk[7][:, 0:2]).then_inc(act_did, 1)


def stage_attention(nc, ctx, sh, bk, h_rows, x_slots, experts, w_dram):
    def sb(name, shape, dt=F32):
        return ctx.enter_context(nc.sbuf_tensor(name, shape, dt))

    def sem(name):
        return ctx.enter_context(nc.semaphore(name))

    spare = experts[:].rearrange("p e n -> p (e n)")[:, E // 2 * EW:]
    taken = [0]

    def carve(*shape):
        n = math.prod(shape)
        at = spare[:, taken[0]:taken[0] + n]
        taken[0] += n
        names = "abcd"[:len(shape)]
        return at.rearrange(f"p ({' '.join(names)}) -> p {' '.join(names)}", **dict(zip(names, shape)))

    hx = [sb(f"hx{u}", [P, CH, D]) for u in range(2)]
    xn = sb("xn", [P, CH, D])
    xt = [sb(f"xt{u}", [P, 2, CH * P]) for u in range(2)]
    t16 = sb("t16", [RANK, CH * P])
    ay = sb("ay", [P, 2, CH * P])
    mn = sb("mn", [P, 2, CH * P])
    ln = sb("ln", [P, 2, CH * P])
    cs = sb("cs", [P, 2 * CH * P])
    ce = sb("ce", [P, 2 * CH * P])
    cm = sb("cm", [P, 2 * CH * P])
    e1 = [sb(f"e1{u}", [P, 2 * CH * P]) for u in range(2)]
    e2 = sb("e2", [P, 2 * CH * P])
    e3 = sb("e3", [P, 2 * CH * P])
    q1 = [carve(2, 2 * CH, P) for u in range(2)]
    qp = sb("qp", [P, 2 * CH * P])
    qs = [carve(2 * CH, P) for u in range(2)]
    WIDE = 2 * CH * P + SUB
    kv = [carve(NSUB * WIDE) for u in range(2)]
    kst = sb("kst", [P, 2, P])
    pb = [sb(f"pb{u}", [P, 2 * CH, NSUB + 1]) for u in range(2)]
    v = [carve(CH, VD) for u in range(2)]
    sg = [carve(CH, VD) for u in range(2)]
    am = sb("am", [P, CH, HEADS, P])
    krow = sb("krow", [P, 2 * P])
    s1 = sb("s1", [P, 2, 2 * DV])
    sq = sb("sq", [P, VD])
    ss = sb("ss", [P, CH, HEADS])
    rs = sb("rs", [P, CH, HEADS])
    og = sb("og", [P, CH, VD])
    ot = sb("ot", [P, CH, HEADS, P])
    x2 = [sb(f"x2{u}", [P, CH, D]) for u in range(2)]
    x2t = sb("x2t", [P, 2, CH * P])
    stats = sb("stats", [P, CH, 6])
    mom = sb("mom", [P, CH, 2])
    rstd = sb("rstd", [P, CH, 1])
    stats2 = sb("stats2", [P, CH, 6])
    mom2 = sb("mom2", [P, CH, 2])
    rstd2 = sb("rstd2", [P, CH, 1])
    ix = sb("ix", [P, CH, 8], U32)
    ixf = sb("ixf", [P, CH, 8])
    oh = sb("oh", [P, 2, CH, E])
    hit = sb("hit", [P, CH, E])
    rank = sb("rank", [P, CH, E])
    pick = sb("pick", [P, 2, CH, E])
    posf = sb("posf", [P, 2, CH])

    h_in = [sem(f"h_in{u}") for u in range(2)]
    dve_step, act_step, pool_step = sem("dve_step"), sem("act_step"), sem("pool_step")
    xn_ready, xt_ps, xt_sb = sem("xn_ready"), sem("xt_ps"), sem("xt_sb")
    t16_ps, t16_sb, y_ps, mn_ready, ln_ready = sem("t16_ps"), sem("t16_sb"), sem("y_ps"), sem("mn_ready"), sem("ln_ready")
    cums_ready, exps_ready = sem("cums_ready"), sem("exps_ready")
    q_ps, k_ps, qk_used, kv_ready = sem("q_ps"), sem("k_pst"), sem("qk_used"), sem("kv_ready")
    v_ps, v_sb, g_ps, sg_sb = sem("v_ps"), sem("v_sb"), sem("g_ps"), sem("sg_sb")
    a_ps, masked, krow_ps, krow_sb = sem("a_ps"), sem("masked"), sem("krow_ps"), sem("krow_sb")
    s_ps, s1_ready, o_ps, squared, gated = sem("s_ps"), sem("s1_ready"), sem("o_ps"), sem("squared"), sem("gated")
    ot_ps, ot_sb, wo_ps, x2_ready = sem("ot_ps"), sem("ot_sb"), sem("wo_ps"), sem("x2_ready")
    x2t_ps, x2t_sb, score_ps, hit_ready = sem("x2t_ps"), sem("x2t_sb"), sem("score_ps"), sem("hit_ready")
    rank_ps, routed = sem("rank_ps"), sem("routed")
    kv_zero = sem("kv_zero")
    q1_ready, idx_ready = sem("q1_ready"), sem("idx_ready")
    apart, pool_apart = sem("apart"), sem("pool_apart")
    sc = sb("sc_now", [P, CH, E])
    hs = sb("hs", [P, CH, D])
    var_ready, rstd_ready, var2_ready, rstd2_ready = sem("var_ready"), sem("rstd_ready"), sem("var2_ready"), sem("rstd2_ready")
    scattered = [sem(f"scattered{u}") for u in range(2)]

    def kv_all(u):
        return kv[u][:, 0:NSUB * 2 * CH * P].rearrange("p (i c j) -> p i c j", i=NSUB, j=P)

    def kv_diag(u):
        return kv[u][:, :].rearrange("p (i w) -> p i w", w=WIDE)[:, :, 0:2 * CH * P] \
            .rearrange("p i (c j) -> p i c j", j=P)[:, :, :, 0:SUB]

    def kv_next(u):
        off = 2 * CH * P
        n = (NSUB - 1) * WIDE
        return kv[u][:, off:off + n].rearrange("p (i w) -> p i w", w=WIDE)[:, :, 0:2 * CH * P] \
            .rearrange("p i (c j) -> p i c j", j=P)[:, :, :, 0:SUB]

    def sub(t):
        return t.rearrange("p (c i s) -> p i c s", i=NSUB, s=SUB)

    def schedule(eng, turn):
        turn(-1, 1, True, False, False)
        turn(0, 0, True, True, False)
        with eng.Fori(0, (BATCH - 2) // 2) as i:
            turn(2 * i + 1, 1, True, True, True)
            turn(2 * i + 2, 0, True, True, True)
        turn(BATCH - 1, 1, False, True, True)
        turn(BATCH, 0, False, False, True)

    with nc.Block() as block:
        @block.sync
        def _(sp):
            def load(b, u):
                src = h_rows[:, bass.ds(b, 1), :].rearrange("(c p) o d -> p (c o) d", p=P)
                sp.dma_start(hx[u][:], src).then_inc(h_in[u], 16)

            for u in range(2):
                load(u, u)
            for e in range(E // 2):
                sp.dma_start(experts[:, e], w_dram[:, e]).then_inc(sh.experts_in[e], 16)
            with sp.Fori(1, BATCH // 2) as i:
                for u in range(2):
                    sp.wait_ge(x2_ready, 2 * i + u - 1)
                    load(2 * i + u, u)

        @block.vector
        def _(dve):
            def route(st, n, scores):
                for c in range(n):
                    st.mark(nc.vector.max(topc[:, c], scores[:, c]))
                st.wait_apart()
                for c in range(n):
                    st.mark(nc.vector.max_index(ix[:, c], topc[:, c], scores[:, c]))
                st.wait()
                st.link(nc.vector.tensor_copy(ixf[:, 0:n], ix[:, 0:n]))
                for k in range(2):
                    st.mark(nc.vector.tensor_tensor(oh[:, k, 0:n], ixf[:, 0:n, k:k + 1].to_broadcast([P, n, E]),
                                                    sh.iota8[:].unsqueeze(1).to_broadcast([P, n, E]), ALU.is_equal))
                st.wait()
                st.mark(nc.vector.tensor_tensor(hit[:, 0:n], oh[:, 0, 0:n], oh[:, 1, 0:n], ALU.add))

            topc = sb("topc", [P, CH, 8])

            def turn(b, u, pre, post, tail):
                first = isinstance(b, int) and b <= 0
                w = 1 - u
                total = 55
                st = Steps(dve, dve_step, (b + 1) * total + PRO, apart)
                if pre:
                    dve.wait_ge(h_in[w], (b + 1 - w) * 8 + 16)
                    for c in range(CH):
                        moments(nc, st, hx[w][:, c], stats[:, c], mom[:, c])
                    nc.vector.sem_inc(var_ready, 1)
                    if not (isinstance(b, int) and b < 0):
                        dve.wait_ge(xt_ps, b + 1)
                    dve.wait_ge(rstd_ready, b + 2)
                    for c in range(CH):
                        st.mark(nc.vector.tensor_scalar(xn[:, c], hx[w][:, c], mom[:, c, 0:1], rstd[:, c], ALU.subtract, ALU.mult))
                    st.wait()
                    nc.vector.sem_inc(xn_ready, 1)
                if post:
                    for c in range(CH):
                        dve.wait_ge(a_ps, CH * b + c + 1)
                        nc.vector.tensor_tensor(am[:, c], bk[6 + c][:].rearrange("p (h i) -> p h i", i=P),
                                                sh.causal[:].unsqueeze(1).to_broadcast([P, HEADS, P]), ALU.mult) \
                            .then_inc(masked, 1)
                if tail:
                    dve.wait_ge(score_ps, b)
                    st.mark(nc.vector.tensor_copy(sc[:], bk[0][:, 0:CH * E].rearrange("p (c e) -> p c e", e=E)))
                    st.wait_apart()
                    route(st, CH, sc)
                    st.mark(nc.vector.tensor_copy(sh.top[:, bass.ds(CH * (b - 1), CH)], topc[:]))
                    st.wait()
                    nc.vector.sem_inc(hit_ready, 1)
                if post:
                    dve.wait_ge(s_ps, b + 1)
                    for t in range(2):
                        for par in range(2):
                            rows, cols = slice(par * DK, (par + 1) * DK), slice(par * DV, (par + 1) * DV)
                            st.mark(nc.vector.scalar_tensor_tensor(
                                s1[rows, t, cols], sh.s_cls[rows, t, cols], pb[u][rows, CH * t, NSUB:NSUB + 1],
                                bk[2][rows, t * 2 * DV + cols.start:t * 2 * DV + cols.stop], ALU.mult, ALU.add))
                    st.wait()
                    nc.vector.sem_inc(s1_ready, 1)
                if pre:
                    dve.wait_ge(y_ps, b + 2)
                    for t in range(2):
                        st.mark(nc.vector.tensor_scalar(mn[:, t], bk[3][:, t * CH * P:(t + 1) * CH * P], sh.gb2[:, t:t + 1], None,
                                                        ALU.add))
                    st.wait()
                    nc.vector.sem_inc(mn_ready, 1)

                def gate_out(c):
                    dve.wait_ge(squared, CH * b + c + 1)
                    for h in range(HEADS):
                        cols = slice(h * DV, (h + 1) * DV)
                        st.mark(nc.vector.scalar_tensor_tensor(og[:, c, cols], bk[6 + c][:, cols], rs[:, c, h:h + 1],
                                                               sg[u][:, c, cols], ALU.mult, ALU.mult))
                    st.wait()
                    nc.vector.sem_inc(gated, 1)

                if post:
                    dve.wait_ge(sg_sb, CH * (b + 1))
                    gate_out(0)
                if pre:
                    dve.wait_ge(ln_ready, b + 2)
                    st.link(nc.vector.scalar_tensor_tensor(mn[:], mn[:], 0.0, ln[:], ALU.min, ALU.subtract))
                    st.link(nc.vector.tensor_tensor_scan(cs[:], sh.keep[:], mn[:].rearrange("p t n -> p (t n)"), 0.0,
                                                         ALU.mult, ALU.add))
                    blk = cs[:].rearrange("p (b s) -> p b s", s=SUB)
                    st.mark(nc.vector.tensor_tensor(ce[:].rearrange("p (b s) -> p b s", s=SUB),
                                                    blk[:, :, SUB - 1:SUB].to_broadcast([P, 2 * CH * NSUB, SUB]), blk, ALU.subtract))
                    st.mark(nc.vector.tensor_scalar(cm[:], cs[:], -80.0 * GATE_NORM, None, ALU.max))
                    st.wait()
                    nc.vector.sem_inc(cums_ready, 1)
                if post:
                    gate_out(1)
                if pre:
                    dve.wait_ge(exps_ready, b + 2)
                    if not (isinstance(b, int) and b <= 0):
                        dve.wait_ge(o_ps, CH * b)
                    dve.wait_ge(kv_zero, 7)
                    dve.wait_ge(k_ps, b + 2)
                    st.mark(nc.vector.tensor_tensor(kv_diag(w), sub(bk[2][:]), sub(e2[:]), ALU.mult))
                    kn, en = sub(bk[2][:])[:, 0:NSUB - 1], sub(e3[:])[:, 0:NSUB - 1]
                    st.mark(nc.vector.tensor_tensor(kv_next(w), kn, en, ALU.mult))
                    if not (isinstance(b, int) and b < 0):
                        dve.wait_ge(krow_ps, b + 1)
                    last = lambda t: t.rearrange("p (t c j) -> p t c j", t=2, c=CH)[:, :, 0, P - SUB:P]
                    st.mark(nc.vector.tensor_tensor(kst[:, :, P - SUB:P], last(bk[2][:]), last(e3[:]), ALU.mult))
                    dve.wait_ge(q_ps, b + 2)
                    if not (isinstance(b, int) and b < 0):
                        dve.wait_ge(kv_ready, b + 1)
                        dve.wait_ge(q1_ready, 2 * (b + 1))
                    st.mark(nc.vector.scalar_tensor_tensor(qp[:], bk[1][:], DK ** -0.5, e1[w][:], ALU.mult, ALU.mult))
                    st.wait()
                    nc.vector.sem_inc(qk_used, 1)
                if tail:
                    dve.wait_ge(rank_ps, b + 1)
                    ranks = bk[0][:, 16:16 + CH * E].rearrange("p (c e) -> p c e", e=E)
                    counts = bk[0][:, 32:32 + CH * E].rearrange("p (c e) -> p c e", e=E)
                    st.link(nc.vector.tensor_tensor(rank[:], ranks, sh.carry[:].unsqueeze(1).to_broadcast([P, CH, E]), ALU.add))
                    st.mark(nc.vector.tensor_tensor(rank[:, 1], rank[:, 1], counts[:, 0], ALU.add))
                    st.link(nc.vector.tensor_tensor(sh.carry[:], sh.carry[:], counts[:, 0], ALU.add))
                    st.link(nc.vector.tensor_tensor(sh.carry[:], sh.carry[:], counts[:, 1], ALU.add))
                    for k in range(2):
                        st.mark(nc.vector.tensor_tensor(pick[:, k], oh[:, k], rank[:], ALU.mult))
                    st.wait()
                    st.link(nc.vector.reduce_sum(posf[:], pick[:], axis=mybir.AxisListType.X))
                    st.link(nc.vector.tensor_copy(sh.pos[:, bass.ds(CH * (b - 1), CH)], posf[:].rearrange("p k c -> p c k")))
                    nc.vector.sem_inc(routed, 1)
                if post:
                    if not first:
                        dve.wait_ge(scattered[u], 32 * (b - u) + 16)
                    dve.wait_ge(wo_ps, CH * (b + 1))
                    for c in range(CH):
                        st.link(nc.vector.tensor_tensor(hs[:, c], bk[6][:, c * D:(c + 1) * D], hx[u][:, c], ALU.add))
                        moments(nc, st, hs[:, c], stats2[:, c], mom2[:, c])
                    nc.vector.sem_inc(var2_ready, 1)
                    st.mark(nc.vector.tensor_copy(sh.h2[:, bass.ds(CH * b, CH)], hs[:]))
                    dve.wait_ge(rstd2_ready, b + 1)
                    for c in range(CH):
                        st.mark(nc.vector.tensor_scalar(x2[u][:, c], hs[:, c], mom2[:, c, 0:1], rstd2[:, c], ALU.subtract, ALU.mult))
                    st.wait()
                    nc.vector.sem_inc(x2_ready, 1)
                if st.n < total:
                    nc.vector.sem_inc(dve_step, total - st.n)
                assert st.n <= total, st.n

            st = Steps(dve, dve_step, 0, apart)
            route(st, 1, sh.sc_cls[:].unsqueeze(1))
            st.wait()
            st.mark(nc.vector.tensor_copy(sh.top[:, TILES:TILES + 1], topc[:, 0:1]))
            st.link(nc.vector.tensor_scalar(hit[:, 0], hit[:, 0], sh.row0[:], None, ALU.mult))
            nc.vector.sem_inc(hit_ready, 1)
            for k in range(2):
                st.mark(nc.vector.tensor_tensor(pick[:, k, 0], oh[:, k, 0], sh.region[:], ALU.mult))
            st.wait()
            st.link(nc.vector.reduce_sum(posf[:, :, 0:1], pick[:, :, 0:1], axis=mybir.AxisListType.X))
            for k in range(2):
                st.link(nc.vector.tensor_tensor(posf[:, k, 0:1], posf[:, k, 0:1], sh.spare[:], ALU.subtract))
                st.link(nc.vector.scalar_tensor_tensor(posf[:, k, 0:1], posf[:, k, 0:1], sh.row0[:], sh.spare[:], ALU.mult, ALU.add))
            st.link(nc.vector.tensor_copy(sh.pos[:, TILES], posf[:, :, 0]))
            nc.vector.sem_inc(routed, 1)
            dve.wait_ge(rank_ps, 1)
            st.link(nc.vector.tensor_tensor(sh.carry[:], bk[0][:, 32:32 + E], sh.region[:], ALU.add))
            PRO = st.n
            schedule(dve, turn)

        @block.gpsimd
        def _(pool):
            for u in range(2):
                nc.gpsimd.memset(kv[u][:], 0.0).then_inc(kv_zero, 1)
                nc.gpsimd.memset(q1[u][:], 0.0).then_inc(kv_zero, 1)
                nc.gpsimd.memset(pb[u][:, :, 0:1], 1.0).then_inc(kv_zero, 1)
            nc.gpsimd.memset(s1[:], 0.0).then_inc(kv_zero, 1)

            idx = [sb(f"idx{c}{k}", [P, 1], U32) for c in range(CH) for k in range(2)]
            pool.wait_ge(routed, 1)
            for k in range(2):
                nc.gpsimd.tensor_copy(idx[k][:], sh.pos[:, TILES, k:k + 1]).then_inc(idx_ready, 1)
            pool.wait_ge(idx_ready, 2)
            for k in range(2):
                nc.gpsimd.indirect_dma_start(x_slots, bass.IndirectOffsetOnAxis(ap=idx[k][:], axis=0), sh.x2c[:], None) \
                    .then_inc(scattered[k], 16)
                pool.wait_ge(scattered[k], 16)

            def turn(b, u, pre, post, tail):
                w = 1 - u
                total = 13
                st = Steps(pool, pool_step, (b + 1) * total, pool_apart)
                if tail:
                    pool.wait_ge(routed, b + 1)
                    pool.wait_ge(scattered[u], 32 * (b - u) + 16)
                    pool.sem_inc(pool_apart, 1)
                    for c in range(CH):
                        for k in range(2):
                            st.mark(nc.gpsimd.tensor_copy(idx[2 * c + k][:], sh.pos[:, bass.ds(CH * (b - 1) + c, 1), k:k + 1]
                                                          .rearrange("p o k -> p (o k)")))
                    st.wait_apart()
                    for c in range(CH):
                        for k in range(2):
                            nc.gpsimd.indirect_dma_start(
                                x_slots, bass.IndirectOffsetOnAxis(ap=idx[2 * c + k][:], axis=0), x2[w][:, c], None) \
                                .then_inc(scattered[w], 16)
                if pre:
                    pool.wait_ge(qk_used, b + 2)
                    if not (isinstance(b, int) and b < 1):
                        pool.wait_ge(s1_ready, b)
                        pool.wait_ge(o_ps, CH * b)
                    blk = e1[w][:].rearrange("p (c i s) -> p c i s", i=NSUB, s=SUB)[:, :, :, SUB - 1]
                    pool.sem_inc(pool_apart, 1)
                    st.link(nc.gpsimd.tensor_copy(pb[w][:, :, 1:2], blk[:, :, 0:1]))
                    for i in range(1, NSUB):
                        st.link(nc.gpsimd.tensor_tensor(pb[w][:, :, i + 1:i + 2], pb[w][:, :, i:i + 1], blk[:, :, i:i + 1], ALU.mult))
                    st.mark(nc.gpsimd.tensor_tensor(
                        qs[w].rearrange("p c (i s) -> p c i s", s=SUB), qp[:].rearrange("p (c i s) -> p c i s", i=NSUB, s=SUB),
                        pb[w][:, :, 0:NSUB].unsqueeze(3).to_broadcast([P, 2 * CH, NSUB, SUB]), ALU.mult))
                    full = kv_all(w)
                    for i in range(2, NSUB + 1):
                        n = (i - 1) * SUB
                        if i < NSUB:
                            dec = blk[:, :, i - 1:i].to_broadcast([P, 2 * CH, n])
                            st.link(nc.gpsimd.tensor_tensor(full[:, i, :, 0:n], full[:, i - 1, :, 0:n], dec, ALU.mult))
                        else:
                            src = full[:, i - 1].rearrange("p (t c) j -> p t c j", c=CH)[:, :, 0, 0:n]
                            dec = blk.rearrange("p (t c) i -> p t c i", c=CH)[:, :, 0, i - 1:i].to_broadcast([P, 2, n])
                            st.link(nc.gpsimd.tensor_tensor(kst[:, :, 0:n], src, dec, ALU.mult))
                    nc.gpsimd.sem_inc(kv_ready, 1)
                if st.n < total:
                    pass
                if total - st.n:
                    nc.gpsimd.sem_inc(pool_step, total - st.n)

            schedule(pool, turn)
            pool.wait_ge(scattered[0], 16 * 4 * (BATCH // 2) + 16)
            pool.wait_ge(scattered[1], 16 * 4 * (BATCH // 2) + 16)

        @block.scalar
        def _(act):
            def turn(b, u, pre, post, tail):
                w = 1 - u
                total = 15
                st = Steps(act, act_step, (b + 1) * total)
                if pre:
                    act.wait_ge(var_ready, b + 2)
                    rsqrt(nc, st, rstd[:], mom[:, :, 1:2], 1.0, sh.eps[:]).then_inc(rstd_ready, 1)
                if tail:
                    act.wait_ge(x2t_ps, b)
                    nc.scalar.copy(x2t[:], bk[3][:].rearrange("p (k n) -> p k n", k=2)).then_inc(x2t_sb, 1)
                if post:
                    act.wait_ge(krow_ps, b + 1)
                    nc.scalar.copy(krow[:], bk[1][:, 0:2 * P]).then_inc(krow_sb, 1)
                if pre:
                    act.wait_ge(xt_ps, b + 2)
                    nc.scalar.copy(xt[w][:], bk[0][:].rearrange("p (k n) -> p k n", k=2)).then_inc(xt_sb, 1)
                    act.wait_ge(t16_ps, b + 2)
                    nc.scalar.copy(t16[:], bk[0][0:RANK, 0:CH * P]).then_inc(t16_sb, 1)
                    act.wait_ge(mn_ready, b + 2)
                    st.link(nc.scalar.activation(ay[:], mn[:], ACT.Abs))
                    st.link(nc.scalar.activation(ay[:], ay[:], ACT.Exp, scale=-1.0))
                    st.link(nc.scalar.activation(ln[:], ay[:], ACT.Ln, bias=1.0))
                    nc.scalar.sem_inc(ln_ready, 1)

                def squares(c):
                    act.wait_ge(o_ps, CH * b + c + 1)
                    for h in range(HEADS):
                        last = nc.scalar.activation(sq[:, h * DV:(h + 1) * DV], bk[6 + c][:, h * DV:(h + 1) * DV], ACT.Square, accum_out=ss[:, c, h:h + 1])
                        st.mark(last)
                    st.wait()
                    rsqrt(nc, st, rs[:, c], ss[:, c], 1.0 / DV, sh.eps[:]).then_inc(squared, 1)

                if post:
                    squares(0)
                if pre:
                    act.wait_ge(cums_ready, b + 2)
                    nc.scalar.activation(e1[w][:], cs[:], ACT.Exp, scale=1.0 / GATE_NORM)
                    nc.scalar.activation(e2[:], cm[:], ACT.Exp, scale=-1.0 / GATE_NORM)
                    nc.scalar.activation(e3[:], ce[:], ACT.Exp, scale=1.0 / GATE_NORM).then_inc(exps_ready, 1)
                if post:
                    squares(1)
                if pre:
                    for c in range(CH):
                        act.wait_ge(v_ps, CH * (b + 1) + c + 1)
                        nc.scalar.copy(v[w][:, c], bk[4 + c][:]).then_inc(v_sb, 1)
                if pre:
                    act.wait_ge(qk_used, b + 2)
                    for par in range(2):
                        rows = slice(par * DK, (par + 1) * DK)
                        last = nc.scalar.copy(q1[w][rows, par].rearrange("p c j -> p (c j)"), qp[rows])
                        last.then_inc(q1_ready, 1)
                if post:
                    act.wait_ge(ot_ps, CH * b + 1)
                    nc.scalar.copy(ot[:, 0], bk[3][:].rearrange("p (h n) -> p h n", h=HEADS)).then_inc(ot_sb, 1)
                    act.wait_ge(ot_ps, CH * b + 2)
                    nc.scalar.copy(ot[:, 1], bk[3][:].rearrange("p (h n) -> p h n", h=HEADS)).then_inc(ot_sb, 1)
                if pre:
                    for c in range(CH):
                        act.wait_ge(g_ps, CH * (b + 1) + c + 1)
                        nc.scalar.activation(sg[w][:, c], bk[4 + c][:], ACT.Silu).then_inc(sg_sb, 1)
                if post:
                    act.wait_ge(var2_ready, b + 1)
                    rsqrt(nc, st, rstd2[:], mom2[:, :, 1:2], 1.0, sh.eps[:]).then_inc(rstd2_ready, 1)
                if total - st.n:
                    nc.scalar.sem_inc(act_step, total - st.n)

            def wrap(b, u, pre, post, tail):
                turn(b, u, pre, post, tail)

            schedule(act, wrap)

        @block.tensor
        def _(pe):
            def project(out, lhs, rhs):
                for k in range(2):
                    last = nc.tensor.matmul(out, lhs(k), rhs(k), start=(k == 0), stop=(k == 1))
                return last

            pe.wait_ge(hit_ready, 1)
            nc.tensor.matmul(bk[0][:, 32:32 + E], sh.ones[:], hit[:, 0], start=True, stop=True).then_inc(rank_ps, 1)

            def turn(b, u, pre, post, tail):
                w = 1 - u
                if post:
                    pe.wait_ge(kv_ready, b + 1)
                    pe.wait_ge(q1_ready, 2 * (b + 1))
                    if not (isinstance(b, int) and b == 0):
                        pe.wait_ge(x2_ready, b)
                    for c in range(CH):
                        heads = bk[6 + c][:].rearrange("p (h i) -> p h i", i=P)
                        for t in range(2):
                            for i in range(NSUB):
                                cols = slice(i * SUB, (i + 1) * SUB)
                                last = nc.tensor.matmul(heads[:, 2 * t:2 * t + 2, cols], kv_all(u)[:, i, CH * t + c],
                                                        q1[u][:, :, CH * t + c, cols], start=True, stop=True)
                        last.then_inc(a_ps, 1)
                if tail:
                    if not post:
                        pe.wait_ge(x2_ready, b)
                    pe.wait_ge(ot_sb, CH * b)
                    for c in range(CH):
                        for k in range(2):
                            last = nc.tensor.transpose(bk[3][:, k * CH * P + c * P:k * CH * P + (c + 1) * P],
                                                       x2[w][:, c, k * P:(k + 1) * P], sh.ident[:])
                    last.then_inc(x2t_ps, 1)
                if post:
                    for t in range(2):
                        last = nc.tensor.transpose(bk[1][:, t * P:(t + 1) * P], kst[:, t], sh.ident[:])
                    last.then_inc(krow_ps, 1)
                if pre:
                    pe.wait_ge(xn_ready, b + 2)
                    pe.wait_ge(routed, (b if tail else 1))
                    for c in range(CH):
                        for k in range(2):
                            last = nc.tensor.transpose(bk[0][:, k * CH * P + c * P:k * CH * P + (c + 1) * P],
                                                       xn[:, c, k * P:(k + 1) * P], sh.ident[:])
                    last.then_inc(xt_ps, 1)
                    pe.wait_ge(xt_sb, b + 2)
                    project(bk[0][0:RANK, 0:CH * P], lambda k: sh.gw1[:, k], lambda k: xt[w][:, k]).then_inc(t16_ps, 1)
                if post:
                    pe.wait_ge(krow_sb, b + 1)
                    for t in range(2):
                        last = nc.tensor.matmul(bk[2][:, t * 2 * DV:(t + 1) * 2 * DV], krow[:, t * P:(t + 1) * P],
                                                v[u][:, 0, t * 2 * DV:(t + 1) * 2 * DV], start=True, stop=True)
                    last.then_inc(s_ps, 1)

                def outputs(c):
                    pe.wait_ge(masked, CH * b + c + 1)
                    for t in range(2):
                        nc.tensor.matmul(bk[6 + c][:, t * 2 * DV:(t + 1) * 2 * DV], qs[u][:, CH * t + c],
                                         (sh.s_cls if c == 0 else s1)[:, t], start=True, stop=False)
                        for h in (2 * t, 2 * t + 1):
                            cols = slice(h * DV, (h + 1) * DV)
                            last = nc.tensor.matmul(bk[6 + c][:, cols], am[:, c, h], v[u][:, c, cols], start=False, stop=(h % 2 == 1))
                    last.then_inc(o_ps, 1)

                if tail:
                    pe.wait_ge(x2t_sb, b)
                    if pre:
                        pe.wait_ge(t16_sb, b + 2)
                    for c in range(CH):
                        last = project(bk[0][:, c * E:(c + 1) * E], lambda k: x2t[:, k, c * P:(c + 1) * P], lambda k: sh.gate[:, k])
                    last.then_inc(score_ps, 1)
                if post:
                    outputs(0)
                if pre:
                    pe.wait_ge(t16_sb, b + 2)
                    for t in range(2):
                        last = nc.tensor.matmul(bk[3][:, t * CH * P:(t + 1) * CH * P], sh.gw2[:, t * P:(t + 1) * P], t16[:],
                                                start=True, stop=True)
                    last.then_inc(y_ps, 1)
                if post:
                    pe.wait_ge(s1_ready, b + 1)
                    outputs(1)
                if pre:
                    for out, wt, done in ((bk[2], sh.wk, k_ps), (bk[1], sh.wq, q_ps)):
                        for t in range(2):
                            last = project(out[:, t * CH * P:(t + 1) * CH * P], lambda k: wt[:, k, t * P:(t + 1) * P],
                                           lambda k: xt[w][:, k])
                        last.then_inc(done, 1)
                    if not (isinstance(b, int) and b < 0):
                        pe.wait_ge(sg_sb, CH * (b + 1))
                    for c in range(CH):
                        project(bk[4 + c][:], lambda k: xt[w][:, k, c * P:(c + 1) * P], lambda k: sh.wv[:, k]).then_inc(v_ps, 1)
                if tail:
                    pe.wait_ge(hit_ready, b + 1)
                    flat = hit[:].rearrange("p c e -> p (c e)")
                    nc.tensor.matmul(bk[0][:, 16:16 + CH * E], sh.before[:], flat, start=True, stop=True)
                    nc.tensor.matmul(bk[0][:, 32:32 + CH * E], sh.ones[:], flat, start=True, stop=True).then_inc(rank_ps, 1)

                def o_transpose(c):
                    pe.wait_ge(gated, CH * b + c + 1)
                    if c == 0:
                        if pre:
                            pe.wait_ge(mn_ready, b + 2)
                    else:
                        pe.wait_ge(ot_sb, CH * b + 1)
                    for h in range(HEADS):
                        last = nc.tensor.transpose(bk[3][:, h * P:(h + 1) * P], og[:, c, h * DV:(h + 1) * DV], sh.ident[:])
                    last.then_inc(ot_ps, 1)

                def g_rows(c):
                    pe.wait_ge(v_sb, CH * (b + 1) + c + 1)
                    project(bk[4 + c][:], lambda k: xt[w][:, k, c * P:(c + 1) * P], lambda k: sh.wg[:, k]).then_inc(g_ps, 1)

                def out_rows(c):
                    pe.wait_ge(ot_sb, CH * b + c + 1)
                    for h in range(HEADS):
                        last = nc.tensor.matmul(bk[6][:, c * D:(c + 1) * D], ot[:, c, h], sh.wo[:, h],
                                                start=(h == 0), stop=(h == HEADS - 1))
                    last.then_inc(wo_ps, 1)

                if post:
                    o_transpose(0)
                if pre:
                    g_rows(0)
                if post:
                    o_transpose(1)
                    out_rows(0)
                if pre:
                    g_rows(1)
                if post:
                    out_rows(1)

            schedule(pe, turn)


def stage_experts(nc, ctx, sh, bk, experts, w_dram, x_slots, y_slots, out):
    def sb(name, shape, dt=F32):
        return ctx.enter_context(nc.sbuf_tensor(name, shape, dt))

    def sem(name):
        return ctx.enter_context(nc.semaphore(name))

    n_tiles = sb("n_tiles", [P, E])
    ends = sb("ends", [P, E])
    one8 = sb("one8", [P, E])
    pad_f = sb("pad_f", [P, E + 1])
    pad = sb("pad", [P, E + 1], U32)
    zeros = sb("zeros", [P, D])
    lane = sb("lane", [P, 1])
    slot = sb("slot", [1, SLOTS])
    past = sb("past", [1, SLOTS, E])
    tab = sb("tab", [1, 4, SLOTS])
    tabi = sb("tabi", [1, 2, SLOTS], I32)
    shift = sb("shift", [P, E])
    rise = sb("rise", [P, E])
    N = TILES + 1
    above = sb("above", [P, N * 2, E])
    moved = sb("moved", [P, N * 2])
    ypos = sb("ypos", [P, N * 2], U32)
    tw = sb("tw", [P, TILES + 1, 2])
    tz = sb("tz", [P, TILES + 1, 1])
    xs = [sb(f"xs{u}", [P, D]) for u in range(2)]
    xt = [sb(f"ext{u}", [P, 2, P]) for u in range(2)]
    sl = [sb(f"sl{u}", [P, FF]) for u in range(2)]
    hh = [sb(f"hh{u}", [P, FF]) for u in range(2)]
    ht = [sb(f"ht{u}", [P, FF // P, P]) for u in range(2)]
    ys = [sb(f"ys{u}", [P, D]) for u in range(2)]
    RING = 3
    yg = [sb(f"yg{u}", [P, 2, D]) for u in range(2 * RING)]

    step = sem("e_step")
    made = sem("e_made")
    pads_ready, pads_done, table_ready, weights_ready, exp_ready = sem("pads_ready"), sem("pads_done"), sem("table_ready"), sem("tw_ready"), sem("e_exp")
    x_in = [sem(f"x_in{u}") for u in range(2)]
    xt_ps, xt_sb, up_ps, silu_ready, h_ready = sem("ext_ps"), sem("ext_sb"), sem("up_ps"), sem("silu_ready"), sem("h_ready")
    ht_ps, ht_sb, y_ps, y_sb = sem("ht_ps"), sem("ht_sb"), sem("ey_ps"), sem("ey_sb")
    y_stored = [sem(f"y_stored{u}") for u in range(2)]
    tiles_ready = sem("tiles_ready")
    all_stored, ypos_ready = sem("all_stored"), sem("ypos_ready")
    gathered = [sem(f"gathered{u}") for u in range(2 * RING)]
    summed = sem("summed")
    out_stored = sem("out_stored")
    bt, ba, bb, bh, by = bk[0], bk[1:3], bk[3:5], bk[5], bk[6:8]

    def schedule(eng, turn):
        for u in range(2):
            turn(u, u, 4)
        with eng.Fori(1, SLOTS // 2 - 2) as i:
            for u in range(2):
                turn(2 * i + u, u, 4)
        for n in range(4):
            turn(SLOTS - 4 + n, n % 2, 3 - n)

    with nc.Block() as block:
        @block.sync
        def _(sp):
            for e in range(E // 2, E):
                sp.dma_start(experts[:, e], w_dram[:, e]).then_inc(sh.experts_in[e], 16)
            sp.wait_ge(table_ready, 1)
            sp.wait_ge(pads_done, 16 * (E + 1))

            sp.sem_inc(tiles_ready, 1)

            def turn(s, u, left):
                sp.wait_ge(y_sb, s + 1)
                sp.dma_start(y_slots[bass.ds(s * P, P), :], ys[u][:]).then_inc(y_stored[u], 16)

            schedule(sp, turn)
            for u in range(2):
                sp.wait_ge(y_stored[u], 8 * SLOTS)
            nc.sync.sem_inc(all_stored, 1)
            with sp.Fori(0, BATCH) as b:
                for c in range(CH):
                    sp.wait_ge(summed, CH * b + c + 1)
                    sp.dma_start(out[bass.ds(b, 1), 1 + c * P:1 + (c + 1) * P, :].rearrange("o p d -> p (o d)"),
                                 sh.h2[:, bass.ds(CH * b + c, 1)].rearrange("p o d -> p (o d)")).then_inc(out_stored, 16)
            sp.wait_ge(summed, TILES + 1)
            sp.dma_start(out[:, 0:1, :].rearrange("b o d -> o b d"),
                         sh.h2[0:1, TILES].unsqueeze(1).to_broadcast([1, BATCH, D])).then_inc(out_stored, 16)
            sp.wait_ge(out_stored, 16 * (TILES + 1))

        @block.gpsimd
        def _(pool):
            nc.gpsimd.memset(zeros[:], 0.0).then_inc(made, 1)
            nc.gpsimd.iota(lane[:], [[0, 1]], base=0, channel_multiplier=1, allow_small_or_imprecise_dtypes=True).then_inc(made, 1)
            nc.gpsimd.iota(slot[:], [[1, SLOTS]], base=0, channel_multiplier=0, allow_small_or_imprecise_dtypes=True).then_inc(made, 1)
            nc.gpsimd.memset(one8[:], 1.0).then_inc(made, 1)
            pool.wait_ge(pads_ready, 1)
            pool.wait_ge(made, 4)
            for e in range(E + 1):
                nc.gpsimd.indirect_dma_start(x_slots, bass.IndirectOffsetOnAxis(ap=pad[:, e:e + 1], axis=0), zeros[:], None) \
                    .then_inc(pads_done, 16)
            pool.wait_ge(pads_done, 16 * (E + 1))
            pool.wait_ge(all_stored, 1)
            pool.wait_ge(ypos_ready, 1)
            for t in range(N):
                r = t % (2 * RING)
                if t >= 2 * RING:
                    pool.wait_ge(summed, t - 2 * RING + 1)
                for k in range(2):
                    nc.gpsimd.indirect_dma_start(yg[r][:, k], None, y_slots, bass.IndirectOffsetOnAxis(ap=ypos[:, 2 * t + k:2 * t + k + 1], axis=0)) \
                        .then_inc(gathered[r], 16)

        @block.vector
        def _(dve):
            st = Steps(dve, step)
            dve.wait_ge(made, 4)
            big = 1.5 * 2.0 ** 23
            st.link(nc.vector.tensor_tensor(n_tiles[:], sh.carry[:], sh.region[:], ALU.subtract))
            st.mark(nc.vector.tensor_scalar(pad_f[:, 0:E], sh.carry[:], lane[:], None, ALU.add))
            st.link(nc.vector.tensor_copy(pad_f[:, E:E + 1], sh.spare[:]))
            st.link(nc.vector.tensor_copy(pad[:], pad_f[:]))
            nc.vector.sem_inc(pads_ready, 1)
            st.link(nc.vector.tensor_scalar(n_tiles[:], n_tiles[:], 1.0 / P, (P - 1) / (2.0 * P), ALU.mult, ALU.add))
            st.link(nc.vector.tensor_scalar(n_tiles[:], n_tiles[:], big, -big, ALU.add, ALU.add))
            st.link(nc.vector.tensor_tensor_scan(ends[:], one8[:], n_tiles[:], 0.0, ALU.mult, ALU.add))
            shape = [1, SLOTS, E]
            st.link(nc.vector.tensor_tensor(past[:], slot[:].unsqueeze(2).to_broadcast(shape),
                                            ends[0:1].unsqueeze(1).to_broadcast(shape), ALU.is_ge))
            st.link(nc.vector.reduce_sum(tab[:, 0], past[:], axis=mybir.AxisListType.X))
            st.link(nc.vector.tensor_tensor(past[:], past[:], n_tiles[0:1].unsqueeze(1).to_broadcast(shape), ALU.mult))
            st.link(nc.vector.reduce_sum(tab[:, 1], past[:], axis=mybir.AxisListType.X))
            st.link(nc.vector.tensor_tensor(tab[:, 1], slot[:], tab[:, 1], ALU.subtract))
            st.link(nc.vector.tensor_scalar(tab[:, 2], tab[:, 0], float(E), float(P), ALU.is_lt, ALU.mult))
            st.link(nc.vector.tensor_tensor(tab[:, 2], tab[:, 2], tab[:, 1], ALU.mult))
            st.link(nc.vector.scalar_tensor_tensor(tab[:, 3], tab[:, 0], float(REGION), tab[:, 2], ALU.mult, ALU.add))
            st.link(nc.vector.tensor_copy(tabi[:, 0], tab[:, 3]))
            st.link(nc.vector.tensor_scalar(tab[:, 3], tab[:, 0], float(E - 1), None, ALU.min))
            st.link(nc.vector.tensor_copy(tabi[:, 1], tab[:, 3]))
            nc.vector.sem_inc(table_ready, 1)
            st.link(nc.vector.tensor_tensor(shift[:], ends[:], n_tiles[:], ALU.subtract))
            st.link(nc.vector.scalar_tensor_tensor(shift[:], shift[:], float(P), sh.region[:], ALU.mult, ALU.subtract))
            st.mark(nc.vector.tensor_copy(rise[:, 0:1], shift[:, 0:1]))
            st.mark(nc.vector.tensor_tensor(rise[:, 1:E], shift[:, 1:E], shift[:, 0:E - 1], ALU.subtract))
            shape = [P, N * 2, E]
            flat = sh.pos[:].rearrange("p t k -> p (t k)")
            st.link(nc.vector.tensor_tensor(above[:], flat.unsqueeze(2).to_broadcast(shape),
                                            sh.region[:].unsqueeze(1).to_broadcast(shape), ALU.is_ge))
            st.link(nc.vector.tensor_tensor(above[:], above[:], rise[:].unsqueeze(1).to_broadcast(shape), ALU.mult))
            st.link(nc.vector.reduce_sum(moved[:], above[:], axis=mybir.AxisListType.X))
            st.link(nc.vector.tensor_tensor(moved[:], moved[:], flat, ALU.add))
            st.link(nc.vector.tensor_scalar(moved[:], moved[:], float(SLOTS * P - 1), None, ALU.min))
            st.link(nc.vector.tensor_copy(ypos[:], moved[:]))
            nc.vector.sem_inc(ypos_ready, 1)
            st.link(nc.vector.tensor_tensor(tw[:], sh.top[:, :, 0:2], sh.top[:, :, 0:1].to_broadcast([P, TILES + 1, 2]), ALU.subtract))
            nc.vector.sem_inc(weights_ready, 1)
            dve.wait_ge(exp_ready, 1)
            st.link(nc.vector.tensor_tensor(tz[:], tw[:, :, 0:1], tw[:, :, 1:2], ALU.add))
            st.link(nc.vector.reciprocal(tz[:], tz[:]))
            st.link(nc.vector.tensor_tensor(tw[:], tw[:], tz[:].to_broadcast([P, TILES + 1, 2]), ALU.mult))

            def gate(s, u):
                dve.wait_ge(silu_ready, s + 1)
                nc.vector.tensor_tensor(hh[u][:], sl[u][:], bb[u][:], ALU.mult).then_inc(h_ready, 1)

            gate(0, 0)

            def turn(s, u, left):
                dve.wait_ge(ht_ps, s + 1)
                nc.vector.tensor_copy(ht[u][:], bh[:].rearrange("p (j n) -> p j n", n=P)).then_inc(ht_sb, 1)
                if left >= 1:
                    gate(s + 1, 1 - u)

            schedule(dve, turn)
            for t in range(TILES + 1):
                r = t % (2 * RING)
                dve.wait_ge(gathered[r], 32 * (t // (2 * RING) + 1))
                for k in range(2):
                    nc.vector.scalar_tensor_tensor(sh.h2[:, t], yg[r][:, k], tw[:, t, k:k + 1], sh.h2[:, t], ALU.mult, ALU.add) \
                        .then_inc(summed if k else step, 1)
                    if not k:
                        st.n += 1
                        st.wait()

        @block.scalar
        def _(act):
            act.wait_ge(weights_ready, 1)
            nc.scalar.activation(tw[:], tw[:], ACT.Exp).then_inc(exp_ready, 1)

            def load(s, u):
                row = act.value_load(tabi[0:1, 0, bass.ds(s, 1)], min_val=0, max_val=SPARE)
                act.dma_start(xs[u][:], x_slots[bass.ds(row, P), :]).then_inc(x_in[u], 16)

            def x_copy(s, u, more):
                act.wait_ge(xt_ps, s + 1)
                nc.scalar.copy(xt[u][:], bt[:, 0:2 * P].rearrange("p (k n) -> p k n", k=2)).then_inc(xt_sb, 1)
                if more:
                    load(s + 2, u)

            def silu(s, u):
                act.wait_ge(up_ps, s + 1)
                nc.scalar.activation(sl[u][:], ba[u][:], ACT.Silu).then_inc(silu_ready, 1)

            act.wait_ge(table_ready, 1)
            act.wait_ge(tiles_ready, 1)
            for u in range(2):
                load(u, u)
            for u in range(2):
                x_copy(u, u, True)
            silu(0, 0)

            def turn(s, u, left):
                if left >= 2:
                    x_copy(s + 2, u, left >= 4)
                if left >= 1:
                    silu(s + 1, 1 - u)
                act.wait_ge(y_ps, s + 1)
                if not (isinstance(s, int) and s < 2):
                    act.wait_ge(y_stored[u], 8 * (s - u))
                nc.scalar.copy(ys[u][:], by[u][:, 0:D]).then_inc(y_sb, 1)

            schedule(act, turn)

        @block.tensor
        def _(pe):
            pe.wait_ge(table_ready, 1)
            for e in range(E):
                if e < E // 2:
                    pe.wait_ge(sh.experts_in[e], 16)

            def x_transpose(s, u):
                pe.wait_ge(x_in[u], 8 * (s - u) + 16)
                if not (isinstance(s, int) and s == 0):
                    pe.wait_ge(xt_sb, s)
                for k in range(2):
                    last = nc.tensor.transpose(bt[:, k * P:(k + 1) * P], xs[u][:, k * P:(k + 1) * P], sh.ident[:])
                last.then_inc(xt_ps, 1)

            def expert_of(s):
                return pe.value_load(tabi[0:1, 1, bass.ds(s, 1)], min_val=0, max_val=E - 1)

            def up(s, u):
                e = expert_of(s)
                pe.wait_ge(xt_sb, s + 1)
                for m, bank in enumerate((ba[u], bb[u])):
                    for k in range(2):
                        col = (2 * m + k) * FF
                        last = nc.tensor.matmul(bank[:], xt[u][:, k], experts[:, bass.ds(e, 1), col:col + FF]
                                                .rearrange("p o n -> p (o n)"), start=(k == 0), stop=(k == 1))
                last.then_inc(up_ps, 1)

            x_transpose(0, 0)
            x_transpose(1, 1)
            for e in range(E // 2, E):
                pe.wait_ge(sh.experts_in[e], 16)
            up(0, 0)

            def turn(s, u, left):
                if left >= 2:
                    x_transpose(s + 2, u)
                pe.wait_ge(h_ready, s + 1)
                for j in range(FF // P):
                    last = nc.tensor.transpose(bh[:, j * P:(j + 1) * P], hh[u][:, j * P:(j + 1) * P], sh.ident[:])
                last.then_inc(ht_ps, 1)
                if left >= 1:
                    up(s + 1, 1 - u)
                e = expert_of(s)
                pe.wait_ge(ht_sb, s + 1)
                if not (isinstance(s, int) and s < 2):
                    pe.wait_ge(y_sb, s - 1)
                for j in range(FF // P):
                    col = 4 * FF + j * D
                    last = nc.tensor.matmul(by[u][:, 0:D], ht[u][:, j], experts[:, bass.ds(e, 1), col:col + D]
                                            .rearrange("p o n -> p (o n)"), start=(j == 0), stop=(j == FF // P - 1))
                last.then_inc(y_ps, 1)

            schedule(pe, turn)


def build(nc, ins, out):
    h_rows = nc.dram_tensor("h_rows", (TOK, BATCH, D), F32, kind="Internal").ap()
    x_slots = nc.dram_tensor("x_slots", (SPARE + P, D), F32, kind="Internal").ap()
    y_slots = nc.dram_tensor("y_slots", (SLOTS * P, D), F32, kind="Internal").ap()
    with ExitStack() as ctx:
        sh = Shared(nc, ctx)
        count = []
        with ExitStack() as stage:
            stage_kernel(nc, stage, ins["params"], ins["b"], ins["c"], h_rows, lambda sp: count.append(load_weights(sp, sh, ins)))
        experts = ctx.enter_context(nc.sbuf_tensor("experts", [P, E, EW], F32))
        bk = [ctx.enter_context(nc.psum_tensor(f"bank{n}", [P, 512], F32)) for n in range(8)]
        with ExitStack() as stage:
            stage_class_token(nc, stage, sh, bk, count[0])
        with ExitStack() as stage:
            stage_attention(nc, stage, sh, bk, h_rows, x_slots, experts, ins["experts"])
        with ExitStack() as stage:
            stage_experts(nc, stage, sh, bk, experts, ins["experts"], x_slots, y_slots, out)


def kernel(**inputs):
    import numpy as _np
    import concourse.bacc as _bacc
    from concourse import mybir as _mybir
    from concourse.bass_utils import run_bass_kernel_spmd as _run

    g = {k: _np.asarray(a) for k, a in inputs.items()}
    par = lambda a: a.reshape(PAIRS, 2, N_STATE).transpose(1, 2, 0).reshape(P, PAIRS)
    log_dt = _np.repeat(g["L0_tok_log_dt"][:, None], N_STATE, axis=1)
    split = lambda w: w.transpose(2, 0, 1).reshape(w.shape[2] // P, P, E, w.shape[1]).transpose(1, 2, 0, 3).reshape(P, E, -1)
    a = {
        "params": _np.stack([par(log_dt), par(g["L0_tok_inv_A_real"]), par(g["L0_tok_A_imag"])], axis=1),
        "b": _np.stack([par(g["L0_tok_B_ri"][..., r]) for r in range(2)], axis=1),
        "c": g["x"].reshape(BATCH, PAIRS, 2, N_STATE, 2).transpose(2, 3, 4, 1, 0).reshape(P, 2, PAIRS, BATCH),
        "cls": g["cls_tok"].reshape(1, D),
        "Wq": g["L0_attn_Wq"], "Wk": g["L0_attn_Wk"], "Wv": g["L0_attn_Wv"], "Wg": g["L0_attn_Wg"], "Wo": g["L0_attn_Wo"],
        "gk_w1": g["L0_attn_gk_w1"], "gk_w2": g["L0_attn_gk_w2"],
        "gk_b2": g["L0_attn_gk_b2"].reshape(2, P).T,
        "gnorm": g["L0_attn_g_norm_w"].reshape(P, 1),
        "gate": g["L0_ffn_gate_w"].T.reshape(2, P, E).transpose(1, 0, 2),
        "experts": _np.concatenate([split(g["L0_ffn_w1"]), split(g["L0_ffn_w3"]), split(g["L0_ffn_w2"])], axis=2),
    }
    nc = _bacc.Bacc("TRN2", target_bir_lowering=False, num_devices=1)
    arrays, ins = {}, {}
    for name, v in a.items():
        v = _np.ascontiguousarray(v)
        arrays[f"in_{name}"] = v
        ins[name] = nc.dram_tensor(f"in_{name}", v.shape, _mybir.dt.from_np(v.dtype), kind="ExternalInput").ap()
    out = nc.dram_tensor("out", (BATCH, TOK + 1, D), F32, kind="ExternalOutput").ap()
    build(nc, ins, out)
    r = _run(nc, [arrays], core_ids=[0])
    return r.results[0]["out"]
```

```python
from contextlib import ExitStack
import math

import numpy as np
import concourse.bass as bass
from concourse import mybir

F32 = mybir.dt.float32
I32 = mybir.dt.int32
U32 = mybir.dt.uint32
ALU = mybir.AluOpType
ACT = mybir.ActivationFunctionType

P = 128
BATCH = 8
TOK = 256
D = 256
N_STATE = 64

HEADS = 4
DK = 64
DV = 128
VD = HEADS * DV
RANK = 16
CH = 2
SUB = 32
NSUB = P // SUB
GATE_NORM = 16.0
EPS = 1e-5
E = 8
FF = 512
EW = 2 * 2 * FF + FF // P * D
TILES = BATCH * CH
REGION = BATCH * TOK + P + 8
SPARE = E * REGION
PAIRED = 2 * (BATCH * TOK + 1)
SLOTS = -(-((PAIRED + E * (P - 1)) // P) // 2) * 2

PAIRS = TOK // 2
LOW = 8
POW = 64
SHIFTS = D // POW
GROUP = 16
TURNS = PAIRS // GROUP
ROWS = 2 * BATCH * SHIFTS


def stage_kernel(nc, ctx, params, bri, crv, h_rows, loads):
    def sb(name, shape, dt=F32):
        return ctx.enter_context(nc.sbuf_tensor(name, shape, dt))

    def sem(name):
        return ctx.enter_context(nc.semaphore(name))

    logs = sb("logs", [P, 3, PAIRS])
    b_in = sb("b_in", [P, 2, PAIRS])
    c_in = sb("c_in", [P, 2, PAIRS, BATCH])
    et = sb("et", [P, 2, PAIRS])
    ek = sb("ek", [P, 2, PAIRS])
    er = sb("er", [P, 2, PAIRS])
    ep = sb("ep", [P, 2, PAIRS])
    ei = sb("ei", [P, 2, PAIRS], I32)
    ab = sb("ab", [P, 2, PAIRS])
    tmp = sb("tmp", [P, 4, PAIRS])
    zp = sb("zp", [P, 8, 2, PAIRS])
    low = sb("low", [P, 2, PAIRS, LOW])
    lt = sb("lt", [P, 2, 2, PAIRS, 4])
    w = sb("w", [P, 3, PAIRS, SHIFTS])
    v = [sb(f"v{u}", [P, 2, GROUP, POW]) for u in range(2)]
    vt = sb("vt", [P, 2, 2, GROUP, POW // 2])
    x = [sb(f"x{u}", [P, 2, GROUP, ROWS]) for u in range(2)]
    xt = sb("xt", [P, 2, 2, GROUP, BATCH, SHIFTS])
    k_sb = [sb(f"k_sb{u}", [ROWS, GROUP, POW]) for u in range(2)]
    k_ps = [ctx.enter_context(nc.psum_tensor(f"k_ps{u}", [ROWS, GROUP, POW], F32)) for u in range(2)]

    params_in = sem("params_in")
    chain = sem("a_chain")
    powers_ready = sem("powers_ready")
    xzero = sem("xzero")
    v_step = sem("v_step")
    v_ready = sem("v_ready")
    x_step = sem("x_step")
    x_ready = sem("x_ready")
    products_done = sem("products_done")
    k_copied = sem("k_copied")
    k_stored = [sem(f"k_stored{u}") for u in range(2)]

    with nc.Block() as block:
        @block.sync
        def _(sp):
            sp.dma_start(logs[:], params).then_inc(params_in, 16)
            sp.dma_start(b_in[:], bri).then_inc(params_in, 16)
            sp.dma_start(c_in[:], crv).then_inc(params_in, 16)
            loads(sp)

            def turn(t, u):
                sp.wait_ge(k_copied, t + 1)
                for par in range(2):
                    half = ROWS // 2
                    src = k_sb[u][par * half:(par + 1) * half]
                    dst = h_rows[bass.ds(t * 2 * GROUP + par, GROUP, step=2)] \
                        .rearrange("j c (a b) -> (c a) j b", b=POW)
                    sp.dma_start(dst, src).then_inc(k_stored[u], 16)

            with sp.Fori(0, TURNS // 2) as i:
                for u in range(2):
                    turn(2 * i + u, u)
            for u in range(2):
                sp.wait_ge(k_stored[u], 16 * TURNS)

        @block.vector
        def _(dve):
            count = [0]

            def link(ins):
                count[0] += 1
                ins.then_inc(chain, 1)
                dve.wait_ge(chain, count[0])

            dve.wait_ge(params_in, 48)
            big = 1.5 * 2.0 ** 23
            lg = logs[:, 0:2]
            link(nc.vector.tensor_scalar(et[:], lg, 1.0 / math.log(2.0), big, ALU.mult, ALU.add))
            link(nc.vector.tensor_scalar(ek[:], et[:], -big, -126.0, ALU.add, ALU.max))
            hi = 0.693359375
            link(nc.vector.scalar_tensor_tensor(er[:], ek[:], -hi, lg, ALU.mult, ALU.add))
            link(nc.vector.scalar_tensor_tensor(er[:], ek[:], hi - math.log(2.0), er[:], ALU.mult, ALU.add))
            link(nc.vector.tensor_scalar(et[:], ek[:], 127.0, 2.0 ** 23, ALU.add, ALU.mult))
            link(nc.vector.tensor_copy(ei[:], et[:]))
            link(nc.vector.tensor_scalar(ep[:], er[:], 1.0 / math.factorial(7), None, ALU.mult))
            for k in range(6, 0, -1):
                link(nc.vector.scalar_tensor_tensor(ep[:], ep[:], 1.0 / math.factorial(k), er[:], ALU.add, ALU.mult))
            link(nc.vector.scalar_tensor_tensor(ek[:], ep[:], 1.0, ei[:].bitcast(F32), ALU.add, ALU.mult))
            link(nc.vector.scalar_tensor_tensor(ab[:, 0], ek[:, 1], 0.5, ek[:, 0], ALU.mult, ALU.mult))
            link(nc.vector.scalar_tensor_tensor(ab[:, 1], logs[:, 2], 0.5, ek[:, 0], ALU.mult, ALU.mult))
            a, b = ab[:, 0], ab[:, 1]
            link(nc.vector.tensor_scalar(tmp[:, 0], a, 1.0, None, ALU.add))
            link(nc.vector.tensor_tensor(tmp[:, 0], tmp[:, 0], tmp[:, 0], ALU.mult))
            link(nc.vector.tensor_tensor(tmp[:, 1], b, b, ALU.mult))
            link(nc.vector.tensor_tensor(tmp[:, 0], tmp[:, 0], tmp[:, 1], ALU.add))
            link(nc.vector.reciprocal(tmp[:, 0], tmp[:, 0]))
            link(nc.vector.tensor_tensor(tmp[:, 2], a, a, ALU.mult))
            link(nc.vector.tensor_tensor(tmp[:, 2], tmp[:, 2], tmp[:, 1], ALU.add))
            link(nc.vector.tensor_scalar(tmp[:, 2], tmp[:, 2], -1.0, 1.0, ALU.mult, ALU.add))
            link(nc.vector.tensor_tensor(zp[:, 0, 0], tmp[:, 2], tmp[:, 0], ALU.mult))
            link(nc.vector.scalar_tensor_tensor(zp[:, 0, 1], b, 2.0, tmp[:, 0], ALU.mult, ALU.mult))
            for k in range(1, 8):
                zr, zi = zp[:, k - 1, 0], zp[:, k - 1, 1]
                nc.vector.tensor_tensor(tmp[:, 0:2], zp[:, k - 1], zp[:, k - 1], ALU.mult).then_inc(chain, 1)
                count[0] += 1
                link(nc.vector.scalar_tensor_tensor(zp[:, k, 1], zr, 2.0, zi, ALU.mult, ALU.mult))
                link(nc.vector.tensor_tensor(zp[:, k, 0], tmp[:, 0], tmp[:, 1], ALU.subtract))

            def times(out_re, out_im, p, q, zr, zi, src, op_im=ALU.add, neg=False):
                nc.vector.tensor_tensor(p, src, zr, ALU.mult).then_inc(chain, 1)
                count[0] += 1
                link(nc.vector.tensor_tensor(q, src, zi, ALU.mult))
                nc.vector.tensor_tensor(out_re, p[:, 0], q[:, 1], ALU.subtract).then_inc(chain, 1)
                count[0] += 1
                link(nc.vector.tensor_tensor(out_im, p[:, 1], q[:, 0], ALU.add))

            link(nc.vector.memset(low[:, 0, :, 0:1], 1.0))
            link(nc.vector.memset(low[:, 1, :, 0:1], 0.0))
            link(nc.vector.tensor_copy(low[:, :, :, 1], zp[:, 0]))
            for k in (1, 2):
                n = 2 ** k
                zr = zp[:, k, 0].unsqueeze(1).unsqueeze(3).to_broadcast([P, 2, PAIRS, n])
                zi = zp[:, k, 1].unsqueeze(1).unsqueeze(3).to_broadcast([P, 2, PAIRS, n])
                times(low[:, 0, :, n:2 * n], low[:, 1, :, n:2 * n], lt[:, 0, :, :, 0:n], lt[:, 1, :, :, 0:n],
                      zr, zi, low[:, :, :, 0:n])
            link(nc.vector.tensor_scalar(tmp[:, 0:2], b_in[:], 2.0, None, ALU.mult))
            cur = tmp[:, 0:2]
            wsrc = sb("wsrc", [P, SHIFTS, 2, PAIRS])
            link(nc.vector.tensor_copy(wsrc[:, 0], cur))
            for dst, src, k in ((1, 0, 6), (2, 0, 7), (3, 1, 7)):
                zr = zp[:, k, 0].unsqueeze(1).to_broadcast([P, 2, PAIRS])
                zi = zp[:, k, 1].unsqueeze(1).to_broadcast([P, 2, PAIRS])
                times(wsrc[:, dst, 0], wsrc[:, dst, 1], tmp[:, 0:2], tmp[:, 2:4], zr, zi, wsrc[:, src])
            link(nc.vector.tensor_copy(w[:, 0], wsrc[:, :, 0].rearrange("p a j -> p j a")))
            link(nc.vector.tensor_scalar(w[:, 1], wsrc[:, :, 1].rearrange("p a j -> p j a"), -1.0, None, ALU.mult))
            nc.vector.tensor_scalar(w[:, 2], wsrc[:, :, 0].rearrange("p a j -> p j a"), -1.0, None, ALU.mult) \
                .then_inc(powers_ready, 1)

            per_turn = 13

            def turn(t, u, first):
                base = t * per_turn
                js = bass.ds(t * GROUP, GROUP)
                if not first:
                    dve.wait_ge(products_done, t - 1)
                nc.vector.tensor_copy(v[u][:, :, :, 0:LOW], low[:, :, js, :]).then_inc(v_step, 1)
                dve.wait_ge(v_step, base + 1)
                done = 1
                for k in (3, 4, 5):
                    n = 2 ** k
                    zr = zp[:, k, 0, js].unsqueeze(1).unsqueeze(3).to_broadcast([P, 2, GROUP, n])
                    zi = zp[:, k, 1, js].unsqueeze(1).unsqueeze(3).to_broadcast([P, 2, GROUP, n])
                    p, q = vt[:, 0, :, :, 0:n], vt[:, 1, :, :, 0:n]
                    nc.vector.tensor_tensor(p, v[u][:, :, :, 0:n], zr, ALU.mult).then_inc(v_step, 1)
                    nc.vector.tensor_tensor(q, v[u][:, :, :, 0:n], zi, ALU.mult).then_inc(v_step, 1)
                    done += 2
                    dve.wait_ge(v_step, base + done)
                    nc.vector.tensor_tensor(v[u][:, 0, :, n:2 * n], p[:, 0], q[:, 1], ALU.subtract).then_inc(v_step, 1)
                    last = nc.vector.tensor_tensor(v[u][:, 1, :, n:2 * n], p[:, 1], q[:, 0], ALU.add)
                    last.then_inc(v_step, 1)
                    done += 2
                    dve.wait_ge(v_step, base + done)
                nc.vector.sem_inc(v_ready, 1)

            for u in range(2):
                turn(u, u, True)
            with dve.Fori(1, TURNS // 2) as i:
                for u in range(2):
                    turn(2 * i + u, u, False)

        @block.gpsimd
        def _(pool):
            for u in range(2):
                nc.gpsimd.memset(x[u][:], 0.0).then_inc(xzero, 1)
            pool.wait_ge(xzero, 2)
            pool.wait_ge(powers_ready, 1)

            def turn(t, u, first):
                js = bass.ds(t * GROUP, GROUP)
                shape = [P, GROUP, BATCH, SHIFTS]
                for half in range(2):
                    for r in range(2):
                        cc = c_in[:, half, js].unsqueeze(3).to_broadcast(shape)
                        ww = w[:, half + r, js].unsqueeze(2).to_broadcast(shape)
                        nc.gpsimd.tensor_tensor(xt[:, half, r], cc, ww, ALU.mult).then_inc(x_step, 1)
                pool.wait_ge(x_step, 6 * t + 4)
                if not first:
                    pool.wait_ge(products_done, t - 1)
                for par in range(2):
                    ps = slice(par * N_STATE, (par + 1) * N_STATE)
                    cols = slice(par * ROWS // 2, (par + 1) * ROWS // 2)
                    nc.gpsimd.tensor_tensor(x[u][ps, :, :, cols], xt[ps, 0].rearrange("p r j c a -> p r j (c a)"),
                                            xt[ps, 1].rearrange("p r j c a -> p r j (c a)"), ALU.add) \
                        .then_inc(x_step, 1)
                pool.wait_ge(x_step, 6 * t + 6)
                nc.gpsimd.sem_inc(x_ready, 1)

            for u in range(2):
                turn(u, u, True)
            with pool.Fori(1, TURNS // 2) as i:
                for u in range(2):
                    turn(2 * i + u, u, False)

        @block.tensor
        def _(pe):
            def turn(t, u, first):
                pe.wait_ge(x_ready, t + 1)
                pe.wait_ge(v_ready, t + 1)
                if not first:
                    pe.wait_ge(k_copied, t - 1)
                for j in range(GROUP):
                    for r in range(2):
                        last = nc.tensor.matmul(k_ps[u][:, j], x[u][:, r, j], v[u][:, r, j],
                                                start=(r == 0), stop=(r == 1))
                last.then_inc(products_done, 1)

            for u in range(2):
                turn(u, u, True)
            with pe.Fori(1, TURNS // 2) as i:
                for u in range(2):
                    turn(2 * i + u, u, False)

        @block.scalar
        def _(act):
            def turn(t, u, first):
                act.wait_ge(products_done, t + 1)
                if not first:
                    act.wait_ge(k_stored[u], 16 * (t - u))
                nc.scalar.copy(k_sb[u][:], k_ps[u][:]).then_inc(k_copied, 1)

            for u in range(2):
                turn(u, u, True)
            with act.Fori(1, TURNS // 2) as i:
                for u in range(2):
                    turn(2 * i + u, u, False)



class Steps:

    def __init__(self, eng, sem, base=0, apart=None):
        self.eng, self.sem, self.base, self.n, self.apart = eng, sem, base, 0, apart

    def mark(self, ins):
        ins.then_inc(self.sem, 1)
        self.n += 1

    def wait(self):
        self.eng.wait_ge(self.sem, self.base + self.n)

    def wait_apart(self):
        self.wait()
        self.eng.sem_inc(self.apart, 1)

    def link(self, ins):
        self.mark(ins)
        self.wait()


def moments(nc, st, src, stats, mom):
    st.mark(nc.vector.bn_stats(stats, src))
    if st.apart is None:
        st.wait()
    else:
        st.wait_apart()
    st.link(nc.vector.bn_aggr(mom, stats))


def rsqrt(nc, st, out, src, scale, eps):
    st.link(nc.scalar.activation(out, src, ACT.Ln, scale=scale, bias=eps))
    return nc.scalar.activation(out, out, ACT.Exp, scale=-0.5)


class Shared:

    def __init__(self, nc, ctx):
        def sb(name, shape, dt=F32):
            return ctx.enter_context(nc.sbuf_tensor(name, shape, dt))

        self.wq = sb("wq", [P, 2, D])
        self.wk = sb("wk", [P, 2, D])
        self.wv = sb("wv", [P, 2, VD])
        self.wg = sb("wg", [P, 2, VD])
        self.wo = sb("wo", [P, HEADS, D])
        self.gw1 = sb("gw1", [P, 2, RANK])
        self.gw2 = sb("gw2", [RANK, D])
        self.gb2 = sb("gb2", [P, 2])
        self.gnorm = sb("gnorm", [P, 1])
        self.gate = sb("gate", [P, 2, E])
        self.cls = sb("cls", [1, D])
        self.one = sb("one", [1, 1])
        self.eps = sb("eps", [P, 1])
        self.ident = sb("ident", [P, P])
        self.causal = sb("causal", [P, P])
        self.before = sb("before", [P, P])
        self.ones = sb("ones", [P, P])
        self.iota8 = sb("iota8", [P, E])
        self.region = sb("region", [P, E])
        self.spare = sb("spare", [P, 1])
        self.row0 = sb("row0", [P, 1])
        self.keep = sb("keep", [P, CH * 2 * P])
        self.s_cls = sb("s_cls", [P, 2, 2 * DV])
        self.h2 = sb("h2", [P, TILES + 1, D])
        self.x2c = sb("x2c", [P, D])
        self.sc_cls = sb("sc_cls", [P, E])
        self.top = sb("top", [P, TILES + 1, 8])
        self.pos = sb("pos", [P, TILES + 1, 2])
        self.carry = sb("carry", [P, E])
        self.experts_in = [ctx.enter_context(nc.semaphore(f"experts_in{e}")) for e in range(E)]
        self.weights_in = ctx.enter_context(nc.semaphore("weights_in"))


def load_weights(sp, sh, ins):
    pairs = [(sh.wq, ins["Wq"].rearrange("(k p) n -> p k n", p=P)), (sh.wk, ins["Wk"].rearrange("(k p) n -> p k n", p=P)),
             (sh.wv, ins["Wv"].rearrange("(k p) n -> p k n", p=P)), (sh.wg, ins["Wg"].rearrange("(k p) n -> p k n", p=P)),
             (sh.wo, ins["Wo"].rearrange("(k p) n -> p k n", p=P)), (sh.gw1, ins["gk_w1"].rearrange("(k p) n -> p k n", p=P)),
             (sh.gw2, ins["gk_w2"]), (sh.gb2, ins["gk_b2"]), (sh.gnorm, ins["gnorm"]), (sh.gate, ins["gate"]), (sh.cls, ins["cls"])]
    for dst, src in pairs:
        sp.dma_start(dst[:], src).then_inc(sh.weights_in, 16)
    return 16 * len(pairs)


def stage_class_token(nc, ctx, sh, bk, weights_count):
    def sb(name, shape, dt=F32):
        return ctx.enter_context(nc.sbuf_tensor(name, shape, dt))

    xn = sb("c_xn", [1, D])
    stats = sb("c_stats", [1, 6])
    mom = sb("c_mom", [1, 2])
    xc = sb("c_xc", [P, 2])
    qk = sb("c_qk", [1, 2, D])
    vg = sb("c_vg", [1, 2, VD])
    og = sb("c_og", [1, VD])
    sq = sb("c_sq", [1, VD])
    dot = sb("c_dot", [1, 2, HEADS])
    oc = sb("c_oc", [P, HEADS])
    x2t = sb("c_x2t", [P, 2])
    self_chain = ctx.enter_context(nc.semaphore("c_chain"))
    pool_made = ctx.enter_context(nc.semaphore("c_pool_made"))
    eps_made = ctx.enter_context(nc.semaphore("c_eps_made"))
    a_chain = ctx.enter_context(nc.semaphore("c_act_chain"))
    rstd = sb("c_rstd", [1, 2])
    dve_did = ctx.enter_context(nc.semaphore("c_dve_did"))
    act_did = ctx.enter_context(nc.semaphore("c_act_did"))
    pe_did = ctx.enter_context(nc.semaphore("c_pe_did"))

    with nc.Block() as block:
        @block.gpsimd
        def _(pool):
            nc.gpsimd.memset(sh.ident[:], 0.0).then_inc(pool_made, 1)
            nc.gpsimd.memset(sh.causal[:], 1.0).then_inc(pool_made, 1)
            nc.gpsimd.memset(sh.before[:], 1.0).then_inc(pool_made, 1)
            nc.gpsimd.memset(sh.ones[:], 1.0).then_inc(pool_made, 1)
            nc.gpsimd.memset(sh.keep[:], 1.0).then_inc(pool_made, 1)
            nc.gpsimd.memset(sh.row0[:], 0.0).then_inc(pool_made, 1)
            pool.wait_ge(pool_made, 6)
            nc.gpsimd.affine_select(out=sh.ident[:], in_=sh.ident[:], compare_op=ALU.not_equal, fill=1.0, base=0,
                                    pattern=[[-1, P]], channel_multiplier=1).then_inc(pool_made, 1)
            nc.gpsimd.affine_select(out=sh.causal[:], in_=sh.causal[:], compare_op=ALU.is_ge, fill=0.0, base=0,
                                    pattern=[[1, P]], channel_multiplier=-1).then_inc(pool_made, 1)
            nc.gpsimd.affine_select(out=sh.before[:], in_=sh.before[:], compare_op=ALU.is_ge, fill=0.0, base=-1,
                                    pattern=[[1, P]], channel_multiplier=-1).then_inc(pool_made, 1)
            nc.gpsimd.affine_select(out=sh.row0[:], in_=sh.row0[:], compare_op=ALU.not_equal, fill=1.0, base=0,
                                    pattern=[[0, 1]], channel_multiplier=1).then_inc(pool_made, 1)
            nc.gpsimd.memset(sh.keep[:].rearrange("p (b s) -> p b s", s=SUB)[:, :, 0:1], 0.0).then_inc(pool_made, 1)
            nc.gpsimd.iota(sh.iota8[:], [[1, E]], base=0, channel_multiplier=0,
                           allow_small_or_imprecise_dtypes=True).then_inc(pool_made, 1)
            nc.gpsimd.iota(sh.region[:], [[REGION, E]], base=0, channel_multiplier=0,
                           allow_small_or_imprecise_dtypes=True).then_inc(pool_made, 1)
            nc.gpsimd.iota(sh.spare[:], [[0, 1]], base=SPARE, channel_multiplier=1,
                           allow_small_or_imprecise_dtypes=True).then_inc(pool_made, 1)
            nc.gpsimd.memset(sh.x2c[:], 0.0).then_inc(pool_made, 1)
            nc.gpsimd.memset(sh.s_cls[:], 0.0).then_inc(pool_made, 1)
            nc.gpsimd.memset(sh.h2[:, TILES], 0.0).then_inc(pool_made, 1)
            nc.gpsimd.memset(sh.eps[:], EPS).then_inc(eps_made, 1)
            nc.gpsimd.memset(sh.sc_cls[:], 0.0).then_inc(pool_made, 1)

        @block.vector
        def _(dve):
            st = Steps(dve, self_chain)
            dve.wait_ge(sh.weights_in, weights_count)
            st.link(nc.vector.memset(sh.one[:], 1.0))
            moments(nc, st, sh.cls[:], stats[:], mom[:])
            nc.vector.sem_inc(dve_did, 1)
            st.link(nc.vector.tensor_scalar(sh.wo[:], sh.wo[:], sh.gnorm[:], None, ALU.mult))
            dve.wait_ge(act_did, 1)
            st.link(nc.vector.tensor_scalar(xn[:], sh.cls[:], mom[:, 0:1], rstd[:, 0:1], ALU.subtract, ALU.mult))
            nc.vector.sem_inc(dve_did, 1)
            dve.wait_ge(pe_did, 2)
            st.mark(nc.vector.tensor_copy(qk[:], bk[1][0:1].rearrange("p (r n) -> p r n", r=2)))
            st.link(nc.vector.tensor_copy(vg[:, 0], bk[2][0:1]))
            nc.vector.sem_inc(dve_did, 1)
            st.link(nc.vector.scalar_tensor_tensor(sq[:, 0:D], qk[:, 0], DK ** -0.5, qk[:, 1], ALU.mult, ALU.mult))
            st.link(nc.vector.reduce_sum(dot[:, 0], sq[:, 0:D].rearrange("p (h c) -> p h c", c=DK), axis=mybir.AxisListType.X))
            bh = dot[:, 0].unsqueeze(2).to_broadcast([1, HEADS, DV])
            hv = lambda t: t.rearrange("p (h c) -> p h c", c=DV)
            st.link(nc.vector.tensor_tensor(hv(og[:]), hv(vg[:, 0]), bh, ALU.mult))
            st.link(nc.vector.tensor_tensor(sq[:], og[:], og[:], ALU.mult))
            st.link(nc.vector.reduce_sum(dot[:, 1], hv(sq[:]), axis=mybir.AxisListType.X))
            nc.vector.sem_inc(dve_did, 1)
            dve.wait_ge(act_did, 4)
            br = dot[:, 1].unsqueeze(2).to_broadcast([1, HEADS, DV])
            st.link(nc.vector.tensor_tensor(hv(og[:]), hv(og[:]), br, ALU.mult))
            st.link(nc.vector.tensor_tensor(og[:], og[:], vg[:, 1], ALU.mult))
            nc.vector.sem_inc(dve_did, 1)
            dve.wait_ge(pe_did, 3)
            dve.wait_ge(pool_made, 18)
            for par in range(2):
                rows, cols = slice(par * DK, (par + 1) * DK), slice(par * DV, (par + 1) * DV)
                st.link(nc.vector.tensor_copy(sh.s_cls[rows, :, cols], bk[4][rows].rearrange("p (t n) -> p t n", t=2)[:, :, cols]))
            dve.wait_ge(pe_did, 5)
            dve.wait_ge(pool_made, 18)
            st.link(nc.vector.tensor_tensor(sh.h2[0:1, TILES], bk[6][0:1, 0:D], sh.cls[:], ALU.add))
            moments(nc, st, sh.h2[0:1, TILES], stats[:], mom[:])
            nc.vector.sem_inc(dve_did, 1)
            dve.wait_ge(act_did, 6)
            st.link(nc.vector.tensor_scalar(sh.x2c[0:1], sh.h2[0:1, TILES], mom[:, 0:1], rstd[:, 1:2], ALU.subtract, ALU.mult))
            nc.vector.sem_inc(dve_did, 1)
            dve.wait_ge(pe_did, 7)
            st.link(nc.vector.tensor_copy(sh.sc_cls[0:1], bk[0][0:1, 16:16 + E]))

        @block.tensor
        def _(pe):
            def column(out, row, n):
                for k in range(n):
                    last = nc.tensor.matmul(out[:, k:k + 1], row[:, k * P:(k + 1) * P], sh.one[:], start=True, stop=True)
                return last

            def rows(out, lhs, w):
                for k in range(2):
                    last = nc.tensor.matmul(out, lhs[:, k:k + 1], w[:, k], start=(k == 0), stop=(k == 1))
                return last

            pe.wait_ge(dve_did, 2)
            column(bk[0], xn, 2).then_inc(pe_did, 1)
            pe.wait_ge(act_did, 2)
            rows(bk[1][0:1, 0:D], xc, sh.wq)
            rows(bk[1][0:1, D:2 * D], xc, sh.wk)
            rows(bk[2][0:1, :], xc, sh.wv)
            rows(bk[3][0:1, :], xc, sh.wg).then_inc(pe_did, 1)
            pe.wait_ge(dve_did, 3)
            for t in range(2):
                last = nc.tensor.matmul(bk[4][:, t * D:(t + 1) * D], qk[:, 1, t * P:(t + 1) * P],
                                        vg[:, 0, t * D:(t + 1) * D], start=True, stop=True)
            last.then_inc(pe_did, 1)
            pe.wait_ge(dve_did, 5)
            column(bk[5], og, HEADS).then_inc(pe_did, 1)
            pe.wait_ge(act_did, 5)
            for h in range(HEADS):
                last = nc.tensor.matmul(bk[6][0:1, 0:D], oc[:, h:h + 1], sh.wo[:, h], start=(h == 0), stop=(h == HEADS - 1))
            last.then_inc(pe_did, 1)
            pe.wait_ge(dve_did, 7)
            column(bk[7], sh.x2c[0:1], 2).then_inc(pe_did, 1)
            pe.wait_ge(act_did, 7)
            rows(bk[0][0:1, 16:16 + E], x2t, sh.gate).then_inc(pe_did, 1)

        @block.scalar
        def _(act):
            st = Steps(act, a_chain)
            act.wait_ge(eps_made, 1)
            act.wait_ge(dve_did, 1)
            rsqrt(nc, st, rstd[:, 0:1], mom[:, 1:2], 1.0, sh.eps[0:1]).then_inc(act_did, 1)
            act.wait_ge(pe_did, 1)
            nc.scalar.copy(xc[:], bk[0][:, 0:2]).then_inc(act_did, 1)
            act.wait_ge(pe_did, 2)
            nc.scalar.activation(vg[:, 1], bk[3][0:1, :], ACT.Silu).then_inc(act_did, 1)
            act.wait_ge(dve_did, 4)
            rsqrt(nc, st, dot[:, 1], dot[:, 1], 1.0 / DV, sh.eps[0:1]).then_inc(act_did, 1)
            act.wait_ge(pe_did, 4)
            nc.scalar.copy(oc[:], bk[5][:, 0:HEADS]).then_inc(act_did, 1)
            act.wait_ge(dve_did, 6)
            rsqrt(nc, st, rstd[:, 1:2], mom[:, 1:2], 1.0, sh.eps[0:1]).then_inc(act_did, 1)
            act.wait_ge(pe_did, 6)
            nc.scalar.copy(x2t[:], bk[7][:, 0:2]).then_inc(act_did, 1)


def stage_attention(nc, ctx, sh, bk, h_rows, x_slots, experts, w_dram):
    def sb(name, shape, dt=F32):
        return ctx.enter_context(nc.sbuf_tensor("b_" + name, shape, dt))

    def sem(name):
        return ctx.enter_context(nc.semaphore(name))

    xn = sb("xn", [P, CH, D])
    xt = sb("xt", [P, 2, CH * P])
    t16 = sb("t16", [RANK, CH * P])
    ay = sb("ay", [P, 2, CH * P])
    mn = sb("mn", [P, 2, CH * P])
    e1 = sb("e1", [P, 2 * CH * P])
    e2 = sb("e2", [P, 2 * CH * P])
    e3 = sb("e3", [P, 2 * CH * P])
    q1 = sb("q1", [P, 2, 2 * CH, P])
    qp = sb("qp", [P, 2 * CH * P])
    qs = sb("qs", [P, 2 * CH, P])
    WIDE = 2 * CH * P + SUB
    kv = sb("kv", [P, NSUB * WIDE])
    kst = sb("kst", [P, 2, P])
    pb = sb("pb", [P, 2 * CH, NSUB + 1])
    v = sb("v", [P, CH, VD])
    sg = sb("sg", [P, CH, VD])
    am = sb("am", [P, CH, HEADS, P])
    krow = sb("krow", [P, 2 * P])
    s1 = sb("s1", [P, 2, 2 * DV])
    sq = sb("sq", [P, VD])
    ss = sb("ss", [P, CH, HEADS])
    rs = sb("rs", [P, CH, HEADS])
    og = sb("og", [P, CH, VD])
    ot = sb("ot", [P, CH, HEADS, P])
    x2 = [sb(f"x2{u}", [P, CH, D]) for u in range(2)]
    x2t = sb("x2t", [P, 2, CH * P])
    stats = sb("stats", [P, CH, 6])
    mom = sb("mom", [P, CH, 2])
    rstd = sb("rstd", [P, CH, 1])
    stats2 = sb("stats2", [P, CH, 6])
    mom2 = sb("mom2", [P, CH, 2])
    rstd2 = sb("rstd2", [P, CH, 1])
    half = sb("half", [P, HEADS])
    ix = sb("ix", [P, CH, 8], U32)
    ixf = sb("ixf", [P, CH, 8])
    oh = sb("oh", [P, 2, CH, E])
    hit = sb("hit", [P, CH, E])
    rank = sb("rank", [P, CH, E])
    pick = sb("pick", [P, 2, CH, E])
    posf = sb("posf", [P, 2, CH])
    sc = sb("sc_now", [P, CH, E])
    topc = sb("topc", [P, CH, 8])

    h_in = [sem(f"h_in{u}") for u in range(3)]
    dve_step, act_step, pool_step = sem("dve_step"), sem("act_step"), sem("pool_step")
    xn_ready, xt_ps, xt_sb = sem("xn_ready"), sem("xt_ps"), sem("xt_sb")
    t16_ps, t16_sb, y_ps, mn_ready, ln_ready = sem("t16_ps"), sem("t16_sb"), sem("y_ps"), sem("mn_ready"), sem("ln_ready")
    cums_ready, exps_ready = sem("cums_ready"), sem("exps_ready")
    q_ps, k_ps, qk_used, kv_ready = sem("q_ps"), sem("k_pst"), sem("qk_used"), sem("kv_ready")
    v_ps, v_sb, g_ps, tanh_sb, sg_ready = sem("v_ps"), sem("v_sb"), sem("g_ps"), sem("tanh_sb"), sem("sg_ready")
    a_ps, masked, krow_ps, krow_sb = sem("a_ps"), sem("masked"), sem("krow_ps"), sem("krow_sb")
    s_ps, s1_ready, o_ps, squared, rs_ready, gated = sem("s_ps"), sem("s1_ready"), sem("o_ps"), sem("squared"), sem("rs_ready"), sem("gated")
    ot_ps, ot_sb, wo_ps, res_used, x2_ready = sem("ot_ps"), sem("ot_sb"), sem("wo_ps"), sem("res_used"), sem("x2_ready")
    x2t_ps, x2t_sb, score_ps, hit_ready = sem("x2t_ps"), sem("x2t_sb"), sem("score_ps"), sem("hit_ready")
    rank_ps, routed = sem("rank_ps"), sem("routed")
    kv_zero = sem("kv_zero")
    q1_ready, idx_ready = sem("q1_ready"), sem("idx_ready")
    apart, act_apart, pool_apart = sem("apart"), sem("act_apart"), sem("pool_apart")
    var_ready, rstd_ready, var2_ready, rstd2_ready = sem("var_ready"), sem("rstd_ready"), sem("var2_ready"), sem("rstd2_ready")
    scattered = [sem(f"scattered{u}") for u in range(2)]

    kv_all = kv[:, 0:NSUB * 2 * CH * P].rearrange("p (i c j) -> p i c j", i=NSUB, j=P)
    kv_diag = kv[:].rearrange("p (i w) -> p i w", w=WIDE)[:, :, 0:2 * CH * P] \
        .rearrange("p i (c j) -> p i c j", j=P)[:, :, :, 0:SUB]
    kv_next = kv[:, 2 * CH * P:2 * CH * P + (NSUB - 1) * WIDE].rearrange("p (i w) -> p i w", w=WIDE)[:, :, 0:2 * CH * P] \
        .rearrange("p i (c j) -> p i c j", j=P)[:, :, :, 0:SUB]

    def sub(t):
        return t.rearrange("p (c i s) -> p i c s", i=NSUB, s=SUB)

    def at(b, c):
        return sh.h2[:, bass.ds(CH * b + c, 1)].rearrange("p o d -> p (o d)")

    def schedule(eng, turn):
        turn(-1, 1, True, False, False)
        turn(0, 0, True, True, False)
        with eng.Fori(0, (BATCH - 2) // 2) as i:
            turn(2 * i + 1, 1, True, True, True)
            turn(2 * i + 2, 0, True, True, True)
        turn(BATCH - 1, 1, False, True, True)
        turn(BATCH, 0, False, False, True)

    with nc.Block() as block:
        @block.sync
        def _(sp):
            for b in range(BATCH):
                src = h_rows[:, b:b + 1, :].rearrange("(c p) o d -> p (c o) d", p=P)
                sp.dma_start(sh.h2[:, CH * b:CH * (b + 1)], src).then_inc(h_in[min(b, 2)], 16)
            for e in range(E):
                sp.wait_ge(xn_ready, e + 1)
                sp.dma_start(experts[:, e], w_dram[:, e]).then_inc(sh.experts_in[e], 16)

        @block.vector
        def _(dve):
            def route(st, n, scores):
                for c in range(n):
                    st.mark(nc.vector.max(topc[:, c], scores[:, c]))
                st.wait_apart()
                for c in range(n):
                    st.mark(nc.vector.max_index(ix[:, c], topc[:, c], scores[:, c]))
                st.wait()
                st.link(nc.vector.tensor_copy(ixf[:, 0:n], ix[:, 0:n]))
                for k in range(2):
                    st.mark(nc.vector.tensor_tensor(oh[:, k, 0:n], ixf[:, 0:n, k:k + 1].to_broadcast([P, n, E]),
                                                    sh.iota8[:].unsqueeze(1).to_broadcast([P, n, E]), ALU.is_equal))
                st.wait()
                st.mark(nc.vector.tensor_tensor(hit[:, 0:n], oh[:, 0, 0:n], oh[:, 1, 0:n], ALU.add))

            def two_moments(st, b, stats, mom):
                for c in range(CH):
                    st.mark(nc.vector.bn_stats(stats[:, c], at(b, c)))
                st.wait_apart()
                for c in range(CH):
                    st.mark(nc.vector.bn_aggr(mom[:, c], stats[:, c]))
                st.wait()

            def turn(b, u, pre, post, tail):
                w = 1 - u
                total = 56
                st = Steps(dve, dve_step, (b + 1) * total + PRO, apart)
                if pre:
                    dve.wait_ge(h_in[2 if tail else b + 1], 16 * (BATCH - 2) if tail else 16)
                    two_moments(st, b + 1, stats, mom)
                    nc.vector.sem_inc(var_ready, 1)
                    if not (isinstance(b, int) and b < 0):
                        dve.wait_ge(xt_ps, b + 1)
                    dve.wait_ge(rstd_ready, b + 2)
                    dve.sem_inc(apart, 1)
                    for c in range(CH):
                        st.mark(nc.vector.tensor_scalar(xn[:, c], at(b + 1, c), mom[:, c, 0:1], rstd[:, c], ALU.subtract, ALU.mult))
                    st.wait()
                    nc.vector.sem_inc(xn_ready, 1)
                elif post:
                    nc.vector.sem_inc(var_ready, 1)
                if tail:
                    dve.wait_ge(wo_ps, CH * b)
                    dve.sem_inc(apart, 1)
                    for c in range(CH):
                        st.mark(nc.vector.tensor_tensor(at(b - 1, c), bk[6][:, c * D:(c + 1) * D], at(b - 1, c), ALU.add))
                    st.wait_apart()
                    nc.vector.sem_inc(res_used, 1)
                    two_moments(st, b - 1, stats2, mom2)
                    nc.vector.sem_inc(var2_ready, 1)
                if post:
                    for c in range(CH):
                        dve.wait_ge(tanh_sb, CH * b + c + 1)
                        st.mark(nc.vector.scalar_tensor_tensor(sg[:, c], sg[:, c], 1.0, bk[4 + c][:], ALU.add, ALU.mult))
                    st.wait()
                    nc.vector.sem_inc(sg_ready, 1)
                if tail:
                    dve.wait_ge(scattered[w], 32 * (b - w) - 16)
                    dve.wait_ge(rstd2_ready, b)
                    dve.sem_inc(apart, 1)
                    for c in range(CH):
                        st.mark(nc.vector.tensor_scalar(x2[w][:, c], at(b - 1, c), mom2[:, c, 0:1], rstd2[:, c], ALU.subtract, ALU.mult))
                    st.wait()
                    nc.vector.sem_inc(x2_ready, 1)
                if post:
                    for c in range(CH):
                        dve.wait_ge(a_ps, CH * b + c + 1)
                        nc.vector.tensor_tensor(am[:, c], bk[6 + c][:].rearrange("p (h i) -> p h i", i=P),
                                                sh.causal[:].unsqueeze(1).to_broadcast([P, HEADS, P]), ALU.mult) \
                            .then_inc(masked, 1)
                    dve.wait_ge(s_ps, b + 1)
                    for t in range(2):
                        for par in range(2):
                            rows, cols = slice(par * DK, (par + 1) * DK), slice(par * DV, (par + 1) * DV)
                            st.mark(nc.vector.scalar_tensor_tensor(
                                s1[rows, t, cols], sh.s_cls[rows, t, cols], pb[rows, CH * t, NSUB:NSUB + 1],
                                bk[2][rows, t * 2 * DV + cols.start:t * 2 * DV + cols.stop], ALU.mult, ALU.add))
                    st.wait()
                    nc.vector.sem_inc(s1_ready, 1)
                if pre:
                    dve.wait_ge(y_ps, b + 2)
                    for t in range(2):
                        st.mark(nc.vector.tensor_scalar(mn[:, t], bk[3][:, t * CH * P:(t + 1) * CH * P], sh.gb2[:, t:t + 1], None,
                                                        ALU.add))
                    st.wait()
                    nc.vector.sem_inc(mn_ready, 1)
                if tail:
                    dve.wait_ge(score_ps, b)
                    st.mark(nc.vector.tensor_copy(sc[:], bk[0][:, 0:CH * E].rearrange("p (c e) -> p c e", e=E)))
                    st.wait_apart()
                    route(st, CH, sc)
                    st.mark(nc.vector.tensor_copy(sh.top[:, bass.ds(CH * (b - 1), CH)], topc[:]))
                    st.wait()
                    nc.vector.sem_inc(hit_ready, 1)

                def gate_out(c):
                    dve.wait_ge(rs_ready, CH * b + c + 1)
                    for h in range(HEADS):
                        cols = slice(h * DV, (h + 1) * DV)
                        st.mark(nc.vector.scalar_tensor_tensor(og[:, c, cols], bk[6 + c][:, cols], rs[:, c, h:h + 1],
                                                               sg[:, c, cols], ALU.mult, ALU.mult))
                    st.wait()
                    nc.vector.sem_inc(gated, 1)

                if post:
                    gate_out(0)
                if pre:
                    dve.wait_ge(ln_ready, b + 2)
                    if not (isinstance(b, int) and b < 0):
                        dve.wait_ge(kv_ready, b + 1)
                    st.link(nc.vector.scalar_tensor_tensor(mn[:], mn[:], 0.0, ay[:], ALU.min, ALU.subtract))
                    st.link(nc.vector.tensor_tensor_scan(e1[:], sh.keep[:], mn[:].rearrange("p t n -> p (t n)"), 0.0,
                                                         ALU.mult, ALU.add))
                    blk = e1[:].rearrange("p (b s) -> p b s", s=SUB)
                    st.mark(nc.vector.tensor_tensor(e3[:].rearrange("p (b s) -> p b s", s=SUB),
                                                    blk[:, :, SUB - 1:SUB].to_broadcast([P, 2 * CH * NSUB, SUB]), blk, ALU.subtract))
                    st.mark(nc.vector.tensor_scalar(e2[:], e1[:], -80.0 * GATE_NORM, None, ALU.max))
                    st.wait()
                    nc.vector.sem_inc(cums_ready, 1)
                if post:
                    gate_out(1)
                if pre:
                    dve.wait_ge(exps_ready, b + 2)
                    dve.wait_ge(kv_zero, 5)
                    dve.wait_ge(k_ps, b + 2)
                    st.mark(nc.vector.tensor_tensor(kv_diag, sub(bk[2][:]), sub(e2[:]), ALU.mult))
                    kn, en = sub(bk[2][:])[:, 0:NSUB - 1], sub(e3[:])[:, 0:NSUB - 1]
                    st.mark(nc.vector.tensor_tensor(kv_next, kn, en, ALU.mult))
                    last = lambda t: t.rearrange("p (t c j) -> p t c j", t=2, c=CH)[:, :, 0, P - SUB:P]
                    st.mark(nc.vector.tensor_tensor(kst[:, :, P - SUB:P], last(bk[2][:]), last(e3[:]), ALU.mult))
                    dve.wait_ge(q_ps, b + 2)
                    if not (isinstance(b, int) and b < 0):
                        dve.wait_ge(q1_ready, 2 * (b + 1))
                    st.mark(nc.vector.scalar_tensor_tensor(qp[:], bk[1][:], DK ** -0.5, e1[:], ALU.mult, ALU.mult))
                    st.wait()
                    nc.vector.sem_inc(qk_used, 1)
                if tail:
                    dve.wait_ge(rank_ps, b + 1)
                    ranks = bk[0][:, 16:16 + CH * E].rearrange("p (c e) -> p c e", e=E)
                    counts = bk[0][:, 32:32 + CH * E].rearrange("p (c e) -> p c e", e=E)
                    st.link(nc.vector.tensor_tensor(rank[:], ranks, sh.carry[:].unsqueeze(1).to_broadcast([P, CH, E]), ALU.add))
                    st.mark(nc.vector.tensor_tensor(rank[:, 1], rank[:, 1], counts[:, 0], ALU.add))
                    st.link(nc.vector.tensor_tensor(sh.carry[:], sh.carry[:], counts[:, 0], ALU.add))
                    st.link(nc.vector.tensor_tensor(sh.carry[:], sh.carry[:], counts[:, 1], ALU.add))
                    for k in range(2):
                        st.mark(nc.vector.tensor_tensor(pick[:, k], oh[:, k], rank[:], ALU.mult))
                    st.wait()
                    st.link(nc.vector.reduce_sum(posf[:], pick[:], axis=mybir.AxisListType.X))
                    st.link(nc.vector.tensor_copy(sh.pos[:, bass.ds(CH * (b - 1), CH)], posf[:].rearrange("p k c -> p c k")))
                    nc.vector.sem_inc(routed, 1)
                if st.n < total:
                    nc.vector.sem_inc(dve_step, total - st.n)
                assert st.n <= total, st.n

            st = Steps(dve, dve_step, 0, apart)
            route(st, 1, sh.sc_cls[:].unsqueeze(1))
            st.wait()
            st.mark(nc.vector.tensor_copy(sh.top[:, TILES:TILES + 1], topc[:, 0:1]))
            st.link(nc.vector.tensor_scalar(hit[:, 0], hit[:, 0], sh.row0[:], None, ALU.mult))
            nc.vector.sem_inc(hit_ready, 1)
            for k in range(2):
                st.mark(nc.vector.tensor_tensor(pick[:, k, 0], oh[:, k, 0], sh.region[:], ALU.mult))
            st.wait()
            st.link(nc.vector.reduce_sum(posf[:, :, 0:1], pick[:, :, 0:1], axis=mybir.AxisListType.X))
            for k in range(2):
                st.link(nc.vector.tensor_tensor(posf[:, k, 0:1], posf[:, k, 0:1], sh.spare[:], ALU.subtract))
                st.link(nc.vector.scalar_tensor_tensor(posf[:, k, 0:1], posf[:, k, 0:1], sh.row0[:], sh.spare[:], ALU.mult, ALU.add))
            st.link(nc.vector.tensor_copy(sh.pos[:, TILES], posf[:, :, 0]))
            nc.vector.sem_inc(routed, 1)
            dve.wait_ge(rank_ps, 1)
            st.link(nc.vector.tensor_tensor(sh.carry[:], bk[0][:, 32:32 + E], sh.region[:], ALU.add))
            PRO = st.n
            schedule(dve, turn)

        @block.gpsimd
        def _(pool):
            nc.gpsimd.memset(half[:], -0.5).then_inc(kv_zero, 1)
            nc.gpsimd.memset(q1[:], 0.0).then_inc(kv_zero, 1)
            nc.gpsimd.memset(kv[:], 0.0).then_inc(kv_zero, 1)
            nc.gpsimd.memset(pb[:, :, 0:1], 1.0).then_inc(kv_zero, 1)
            nc.gpsimd.memset(s1[:], 0.0).then_inc(kv_zero, 1)

            idx = [sb(f"idx{c}{k}", [P, 1], U32) for c in range(CH) for k in range(2)]

            def inverse_root(st, out, src, scale, eps, n):
                pool.sem_inc(pool_apart, 1)
                st.link(nc.gpsimd.tensor_scalar(out, src, scale, eps, ALU.mult, ALU.add))
                return nc.gpsimd.tensor_tensor(out, out, half[:, 0:n], ALU.pow)

            def root_of_rows(st, b):
                pool.wait_ge(var_ready, b + 1)
                flat = lambda t: t.rearrange("p c o -> p (c o)")
                inverse_root(st, flat(rstd[:]), flat(mom[:, :, 1:2]), 1.0, EPS, CH).then_inc(rstd_ready, 1)

            root_of_rows(Steps(pool, pool_step, 0, pool_apart), 0)
            pool.wait_ge(routed, 1)
            for k in range(2):
                nc.gpsimd.tensor_copy(idx[k][:], sh.pos[:, TILES, k:k + 1]).then_inc(idx_ready, 1)
            pool.wait_ge(idx_ready, 2)
            for k in range(2):
                nc.gpsimd.indirect_dma_start(x_slots, bass.IndirectOffsetOnAxis(ap=idx[k][:], axis=0), sh.x2c[:], None) \
                    .then_inc(scattered[k], 16)
                pool.wait_ge(scattered[k], 16)

            def turn(b, u, pre, post, tail):
                w = 1 - u
                total = 17
                st = Steps(pool, pool_step, (b + 1) * total + 1, pool_apart)
                flat = lambda t: t.rearrange("p c o -> p (c o)")
                if tail:
                    pool.wait_ge(var2_ready, b)
                    inverse_root(st, flat(rstd2[:]), flat(mom2[:, :, 1:2]), 1.0, EPS, CH).then_inc(rstd2_ready, 1)
                if post:
                    for c in range(CH):
                        pool.wait_ge(squared, CH * b + c + 1)
                        inverse_root(st, rs[:, c], ss[:, c], 4.0 / DV, 4.0 * EPS, HEADS).then_inc(rs_ready, 1)
                if pre:
                    pool.wait_ge(qk_used, b + 2)
                    blk = e1[:].rearrange("p (c i s) -> p c i s", i=NSUB, s=SUB)[:, :, :, SUB - 1]
                    pool.sem_inc(pool_apart, 1)
                    st.link(nc.gpsimd.tensor_copy(pb[:, :, 1:2], blk[:, :, 0:1]))
                    for i in range(1, NSUB):
                        st.link(nc.gpsimd.tensor_tensor(pb[:, :, i + 1:i + 2], pb[:, :, i:i + 1], blk[:, :, i:i + 1], ALU.mult))
                    st.mark(nc.gpsimd.tensor_tensor(
                        qs[:].rearrange("p c (i s) -> p c i s", s=SUB), qp[:].rearrange("p (c i s) -> p c i s", i=NSUB, s=SUB),
                        pb[:, :, 0:NSUB].unsqueeze(3).to_broadcast([P, 2 * CH, NSUB, SUB]), ALU.mult))
                    for i in range(2, NSUB + 1):
                        n = (i - 1) * SUB
                        if i < NSUB:
                            dec = blk[:, :, i - 1:i].to_broadcast([P, 2 * CH, n])
                            st.link(nc.gpsimd.tensor_tensor(kv_all[:, i, :, 0:n], kv_all[:, i - 1, :, 0:n], dec, ALU.mult))
                        else:
                            src = kv_all[:, i - 1].rearrange("p (t c) j -> p t c j", c=CH)[:, :, 0, 0:n]
                            dec = blk.rearrange("p (t c) i -> p t c i", c=CH)[:, :, 0, i - 1:i].to_broadcast([P, 2, n])
                            st.link(nc.gpsimd.tensor_tensor(kst[:, :, 0:n], src, dec, ALU.mult))
                    nc.gpsimd.sem_inc(kv_ready, 1)
                if pre:
                    root_of_rows(st, b + 2)
                if tail:
                    pool.wait_ge(routed, b + 1)
                    pool.wait_ge(scattered[u], 32 * (b - u) + 16)
                    pool.sem_inc(pool_apart, 1)
                    for c in range(CH):
                        for k in range(2):
                            st.mark(nc.gpsimd.tensor_copy(idx[2 * c + k][:], sh.pos[:, bass.ds(CH * (b - 1) + c, 1), k:k + 1]
                                                          .rearrange("p o k -> p (o k)")))
                    st.wait_apart()
                    for c in range(CH):
                        for k in range(2):
                            nc.gpsimd.indirect_dma_start(
                                x_slots, bass.IndirectOffsetOnAxis(ap=idx[2 * c + k][:], axis=0), x2[w][:, c], None) \
                                .then_inc(scattered[w], 16)
                if total - st.n:
                    nc.gpsimd.sem_inc(pool_step, total - st.n)
                assert st.n <= total, st.n

            schedule(pool, turn)
            pool.wait_ge(scattered[0], 16 * 4 * (BATCH // 2) + 16)
            pool.wait_ge(scattered[1], 16 * 4 * (BATCH // 2) + 16)

        @block.scalar
        def _(act):
            def turn(b, u, pre, post, tail):
                total = 11
                st = Steps(act, act_step, (b + 1) * total)
                if pre:
                    act.wait_ge(xt_ps, b + 2)
                    nc.scalar.copy(xt[:], bk[0][:].rearrange("p (k n) -> p k n", k=2)).then_inc(xt_sb, 1)
                    act.wait_ge(t16_ps, b + 2)
                    nc.scalar.copy(t16[:], bk[0][0:RANK, 0:CH * P]).then_inc(t16_sb, 1)
                if post:
                    act.wait_ge(krow_ps, b + 1)
                    nc.scalar.copy(krow[:], bk[1][:, 0:2 * P]).then_inc(krow_sb, 1)
                if tail:
                    act.wait_ge(x2t_ps, b)
                    nc.scalar.copy(x2t[:], bk[3][:].rearrange("p (k n) -> p k n", k=2)).then_inc(x2t_sb, 1)

                def squares(c):
                    act.wait_ge(o_ps, CH * b + c + 1)
                    for h in range(HEADS):
                        st.mark(nc.scalar.activation(sq[:, h * DV:(h + 1) * DV], bk[6 + c][:, h * DV:(h + 1) * DV], ACT.Square,
                                                     accum_out=ss[:, c, h:h + 1]))
                    st.wait()
                    nc.scalar.sem_inc(squared, 1)

                if post:
                    squares(0)
                if pre:
                    act.wait_ge(mn_ready, b + 2)
                    st.link(nc.scalar.activation(ay[:], mn[:], ACT.Abs))
                    st.link(nc.scalar.activation(ay[:], ay[:], ACT.Exp, scale=-1.0))
                    st.link(nc.scalar.activation(ay[:], ay[:], ACT.Ln, bias=1.0))
                    nc.scalar.sem_inc(ln_ready, 1)
                if post:
                    squares(1)
                if pre:
                    act.wait_ge(cums_ready, b + 2)
                    nc.scalar.activation(e2[:], e2[:], ACT.Exp, scale=-1.0 / GATE_NORM)
                    nc.scalar.activation(e3[:], e3[:], ACT.Exp, scale=1.0 / GATE_NORM)
                    nc.scalar.activation(e1[:], e1[:], ACT.Exp, scale=1.0 / GATE_NORM).then_inc(exps_ready, 1)
                    for c in range(CH):
                        act.wait_ge(v_ps, CH * (b + 1) + c + 1)
                        nc.scalar.copy(v[:, c], bk[4 + c][:]).then_inc(v_sb, 1)
                if post:
                    for c in range(CH):
                        act.wait_ge(ot_ps, CH * b + c + 1)
                        nc.scalar.copy(ot[:, c], bk[3][:].rearrange("p (h n) -> p h n", h=HEADS)).then_inc(ot_sb, 1)
                if pre:
                    act.wait_ge(qk_used, b + 2)
                    for par in range(2):
                        rows = slice(par * DK, (par + 1) * DK)
                        nc.scalar.copy(q1[rows, par].rearrange("p c j -> p (c j)"), qp[rows]).then_inc(q1_ready, 1)
                    for c in range(CH):
                        act.wait_ge(g_ps, CH * (b + 1) + c + 1)
                        nc.scalar.activation(sg[:, c], bk[4 + c][:], ACT.Tanh, scale=0.5).then_inc(tanh_sb, 1)
                if total - st.n:
                    nc.scalar.sem_inc(act_step, total - st.n)
                assert st.n <= total, st.n

            schedule(act, turn)

        @block.tensor
        def _(pe):
            def project(out, lhs, rhs):
                for k in range(2):
                    last = nc.tensor.matmul(out, lhs(k), rhs(k), start=(k == 0), stop=(k == 1))
                return last

            pe.wait_ge(hit_ready, 1)
            nc.tensor.matmul(bk[0][:, 32:32 + E], sh.ones[:], hit[:, 0], start=True, stop=True).then_inc(rank_ps, 1)

            def turn(b, u, pre, post, tail):
                w = 1 - u
                if pre:
                    pe.wait_ge(xn_ready, b + 2)
                    pe.wait_ge(routed, (b if tail else 1))
                    for c in range(CH):
                        for k in range(2):
                            last = nc.tensor.transpose(bk[0][:, k * CH * P + c * P:k * CH * P + (c + 1) * P],
                                                       xn[:, c, k * P:(k + 1) * P], sh.ident[:])
                    last.then_inc(xt_ps, 1)
                if post:
                    pe.wait_ge(kv_ready, b + 1)
                    for t in range(2):
                        last = nc.tensor.transpose(bk[1][:, t * P:(t + 1) * P], kst[:, t], sh.ident[:])
                    last.then_inc(krow_ps, 1)
                if pre:
                    pe.wait_ge(xt_sb, b + 2)
                    project(bk[0][0:RANK, 0:CH * P], lambda k: sh.gw1[:, k], lambda k: xt[:, k]).then_inc(t16_ps, 1)
                if post:
                    pe.wait_ge(q1_ready, 2 * (b + 1))
                    if tail:
                        pe.wait_ge(res_used, b)
                    for c in range(CH):
                        heads = bk[6 + c][:].rearrange("p (h i) -> p h i", i=P)
                        for t in range(2):
                            for i in range(NSUB):
                                cols = slice(i * SUB, (i + 1) * SUB)
                                last = nc.tensor.matmul(heads[:, 2 * t:2 * t + 2, cols], kv_all[:, i, CH * t + c],
                                                        q1[:, :, CH * t + c, cols], start=True, stop=True)
                        last.then_inc(a_ps, 1)
                    pe.wait_ge(krow_sb, b + 1)
                    for t in range(2):
                        last = nc.tensor.matmul(bk[2][:, t * 2 * DV:(t + 1) * 2 * DV], krow[:, t * P:(t + 1) * P],
                                                v[:, 0, t * 2 * DV:(t + 1) * 2 * DV], start=True, stop=True)
                    last.then_inc(s_ps, 1)
                if tail:
                    pe.wait_ge(x2_ready, b)
                    pe.wait_ge(ot_sb, CH * b)
                    for c in range(CH):
                        for k in range(2):
                            last = nc.tensor.transpose(bk[3][:, k * CH * P + c * P:k * CH * P + (c + 1) * P],
                                                       x2[w][:, c, k * P:(k + 1) * P], sh.ident[:])
                    last.then_inc(x2t_ps, 1)

                def outputs(c):
                    pe.wait_ge(masked, CH * b + c + 1)
                    for t in range(2):
                        nc.tensor.matmul(bk[6 + c][:, t * 2 * DV:(t + 1) * 2 * DV], qs[:, CH * t + c],
                                         (sh.s_cls if c == 0 else s1)[:, t], start=True, stop=False)
                        for h in (2 * t, 2 * t + 1):
                            cols = slice(h * DV, (h + 1) * DV)
                            last = nc.tensor.matmul(bk[6 + c][:, cols], am[:, c, h], v[:, c, cols], start=False, stop=(h % 2 == 1))
                    last.then_inc(o_ps, 1)

                if post:
                    outputs(0)
                if tail:
                    pe.wait_ge(x2t_sb, b)
                    if pre:
                        pe.wait_ge(t16_sb, b + 2)
                    for c in range(CH):
                        last = project(bk[0][:, c * E:(c + 1) * E], lambda k: x2t[:, k, c * P:(c + 1) * P], lambda k: sh.gate[:, k])
                    last.then_inc(score_ps, 1)
                if pre:
                    pe.wait_ge(t16_sb, b + 2)
                    for t in range(2):
                        last = nc.tensor.matmul(bk[3][:, t * CH * P:(t + 1) * CH * P], sh.gw2[:, t * P:(t + 1) * P], t16[:],
                                                start=True, stop=True)
                    last.then_inc(y_ps, 1)
                if post:
                    pe.wait_ge(s1_ready, b + 1)
                    outputs(1)
                if pre:
                    for out, wt, done in ((bk[2], sh.wk, k_ps), (bk[1], sh.wq, q_ps)):
                        for t in range(2):
                            last = project(out[:, t * CH * P:(t + 1) * CH * P], lambda k: wt[:, k, t * P:(t + 1) * P],
                                           lambda k: xt[:, k])
                        last.then_inc(done, 1)
                    if not (isinstance(b, int) and b < 0):
                        pe.wait_ge(sg_ready, b + 1)
                    for c in range(CH):
                        project(bk[4 + c][:], lambda k: xt[:, k, c * P:(c + 1) * P], lambda k: sh.wv[:, k]).then_inc(v_ps, 1)
                if tail:
                    pe.wait_ge(hit_ready, b + 1)
                    flat = hit[:].rearrange("p c e -> p (c e)")
                    nc.tensor.matmul(bk[0][:, 16:16 + CH * E], sh.before[:], flat, start=True, stop=True)
                    nc.tensor.matmul(bk[0][:, 32:32 + CH * E], sh.ones[:], flat, start=True, stop=True).then_inc(rank_ps, 1)

                def o_transpose(c):
                    pe.wait_ge(gated, CH * b + c + 1)
                    if c == 0:
                        if pre:
                            pe.wait_ge(mn_ready, b + 2)
                    else:
                        pe.wait_ge(ot_sb, CH * b + 1)
                    for h in range(HEADS):
                        last = nc.tensor.transpose(bk[3][:, h * P:(h + 1) * P], og[:, c, h * DV:(h + 1) * DV], sh.ident[:])
                    last.then_inc(ot_ps, 1)

                def g_rows(c):
                    pe.wait_ge(v_sb, CH * (b + 1) + c + 1)
                    project(bk[4 + c][:], lambda k: xt[:, k, c * P:(c + 1) * P], lambda k: sh.wg[:, k]).then_inc(g_ps, 1)

                def out_rows(c):
                    pe.wait_ge(ot_sb, CH * b + c + 1)
                    for h in range(HEADS):
                        last = nc.tensor.matmul(bk[6][:, c * D:(c + 1) * D], ot[:, c, h], sh.wo[:, h],
                                                start=(h == 0), stop=(h == HEADS - 1))
                    last.then_inc(wo_ps, 1)

                if post:
                    o_transpose(0)
                if pre:
                    g_rows(0)
                if post:
                    o_transpose(1)
                    out_rows(0)
                if pre:
                    g_rows(1)
                if post:
                    out_rows(1)

            schedule(pe, turn)


def stage_experts(nc, ctx, sh, bk, experts, w_dram, x_slots, y_slots, out):
    def sb(name, shape, dt=F32):
        return ctx.enter_context(nc.sbuf_tensor(name, shape, dt))

    def sem(name):
        return ctx.enter_context(nc.semaphore(name))

    n_tiles = sb("n_tiles", [P, E])
    ends = sb("ends", [P, E])
    one8 = sb("one8", [P, E])
    pad_f = sb("pad_f", [P, E + 1])
    pad = sb("pad", [P, E + 1], U32)
    zeros = sb("zeros", [P, D])
    lane = sb("lane", [P, 1])
    slot = sb("slot", [1, SLOTS])
    past = sb("past", [1, SLOTS, E])
    tab = sb("tab", [1, 4, SLOTS])
    tabi = sb("tabi", [1, 2, SLOTS], I32)
    shift = sb("shift", [P, E])
    rise = sb("rise", [P, E])
    N = TILES + 1
    above = sb("above", [P, N * 2, E])
    moved = sb("moved", [P, N * 2])
    ypos = sb("ypos", [P, N * 2], U32)
    tw = sb("tw", [P, TILES + 1, 2])
    tz = sb("tz", [P, TILES + 1, 1])
    xs = [sb(f"xs{u}", [P, D]) for u in range(2)]
    xt = [sb(f"ext{u}", [P, 2, P]) for u in range(2)]
    sl = [sb(f"sl{u}", [P, FF]) for u in range(2)]
    hh = [sb(f"hh{u}", [P, FF]) for u in range(2)]
    ht = [sb(f"ht{u}", [P, FF // P, P]) for u in range(2)]
    ys = [sb(f"ys{u}", [P, D]) for u in range(2)]
    RING = 3
    yg = [sb(f"yg{u}", [P, 2, D]) for u in range(2 * RING)]

    step = sem("e_step")
    made = sem("e_made")
    pads_ready, pads_done, table_ready, weights_ready, exp_ready = sem("pads_ready"), sem("pads_done"), sem("table_ready"), sem("tw_ready"), sem("e_exp")
    x_in = [sem(f"x_in{u}") for u in range(2)]
    xt_ps, xt_sb, up_ps, silu_ready, h_ready = sem("ext_ps"), sem("ext_sb"), sem("up_ps"), sem("silu_ready"), sem("h_ready")
    ht_ps, ht_sb, y_ps, y_sb = sem("ht_ps"), sem("ht_sb"), sem("ey_ps"), sem("ey_sb")
    y_stored = [sem(f"y_stored{u}") for u in range(2)]
    tiles_ready = sem("tiles_ready")
    all_stored, ypos_ready = sem("all_stored"), sem("ypos_ready")
    gathered = [sem(f"gathered{u}") for u in range(2 * RING)]
    summed = sem("summed")
    out_stored = sem("out_stored")
    bt, ba, bb, bh, by = bk[0], bk[1:3], bk[3:5], bk[5], bk[6:8]

    def schedule(eng, turn):
        for u in range(2):
            turn(u, u, 4)
        with eng.Fori(1, SLOTS // 2 - 2) as i:
            for u in range(2):
                turn(2 * i + u, u, 4)
        for n in range(4):
            turn(SLOTS - 4 + n, n % 2, 3 - n)

    with nc.Block() as block:
        @block.sync
        def _(sp):
            sp.wait_ge(table_ready, 1)
            sp.wait_ge(pads_done, 16 * (E + 1))

            sp.sem_inc(tiles_ready, 1)

            def turn(s, u, left):
                sp.wait_ge(y_sb, s + 1)
                sp.dma_start(y_slots[bass.ds(s * P, P), :], ys[u][:]).then_inc(y_stored[u], 16)

            schedule(sp, turn)
            for u in range(2):
                sp.wait_ge(y_stored[u], 8 * SLOTS)
            nc.sync.sem_inc(all_stored, 1)
            with sp.Fori(0, BATCH) as b:
                for c in range(CH):
                    sp.wait_ge(summed, CH * b + c + 1)
                    sp.dma_start(out[bass.ds(b, 1), 1 + c * P:1 + (c + 1) * P, :].rearrange("o p d -> p (o d)"),
                                 sh.h2[:, bass.ds(CH * b + c, 1)].rearrange("p o d -> p (o d)")).then_inc(out_stored, 16)
            sp.wait_ge(summed, TILES + 1)
            sp.dma_start(out[:, 0:1, :].rearrange("b o d -> o b d"),
                         sh.h2[0:1, TILES].unsqueeze(1).to_broadcast([1, BATCH, D])).then_inc(out_stored, 16)
            sp.wait_ge(out_stored, 16 * (TILES + 1))

        @block.gpsimd
        def _(pool):
            nc.gpsimd.memset(zeros[:], 0.0).then_inc(made, 1)
            nc.gpsimd.iota(lane[:], [[0, 1]], base=0, channel_multiplier=1, allow_small_or_imprecise_dtypes=True).then_inc(made, 1)
            nc.gpsimd.iota(slot[:], [[1, SLOTS]], base=0, channel_multiplier=0, allow_small_or_imprecise_dtypes=True).then_inc(made, 1)
            nc.gpsimd.memset(one8[:], 1.0).then_inc(made, 1)
            pool.wait_ge(pads_ready, 1)
            pool.wait_ge(made, 4)
            for e in range(E + 1):
                nc.gpsimd.indirect_dma_start(x_slots, bass.IndirectOffsetOnAxis(ap=pad[:, e:e + 1], axis=0), zeros[:], None) \
                    .then_inc(pads_done, 16)
            pool.wait_ge(pads_done, 16 * (E + 1))
            pool.wait_ge(all_stored, 1)
            pool.wait_ge(ypos_ready, 1)
            for t in range(N):
                r = t % (2 * RING)
                if t >= 2 * RING:
                    pool.wait_ge(summed, t - 2 * RING + 1)
                for k in range(2):
                    nc.gpsimd.indirect_dma_start(yg[r][:, k], None, y_slots, bass.IndirectOffsetOnAxis(ap=ypos[:, 2 * t + k:2 * t + k + 1], axis=0)) \
                        .then_inc(gathered[r], 16)

        @block.vector
        def _(dve):
            st = Steps(dve, step)
            dve.wait_ge(made, 4)
            big = 1.5 * 2.0 ** 23
            st.link(nc.vector.tensor_tensor(n_tiles[:], sh.carry[:], sh.region[:], ALU.subtract))
            st.mark(nc.vector.tensor_scalar(pad_f[:, 0:E], sh.carry[:], lane[:], None, ALU.add))
            st.link(nc.vector.tensor_copy(pad_f[:, E:E + 1], sh.spare[:]))
            st.link(nc.vector.tensor_copy(pad[:], pad_f[:]))
            nc.vector.sem_inc(pads_ready, 1)
            st.link(nc.vector.tensor_scalar(n_tiles[:], n_tiles[:], 1.0 / P, (P - 1) / (2.0 * P), ALU.mult, ALU.add))
            st.link(nc.vector.tensor_scalar(n_tiles[:], n_tiles[:], big, -big, ALU.add, ALU.add))
            st.link(nc.vector.tensor_tensor_scan(ends[:], one8[:], n_tiles[:], 0.0, ALU.mult, ALU.add))
            shape = [1, SLOTS, E]
            st.link(nc.vector.tensor_tensor(past[:], slot[:].unsqueeze(2).to_broadcast(shape),
                                            ends[0:1].unsqueeze(1).to_broadcast(shape), ALU.is_ge))
            st.link(nc.vector.reduce_sum(tab[:, 0], past[:], axis=mybir.AxisListType.X))
            st.link(nc.vector.tensor_tensor(past[:], past[:], n_tiles[0:1].unsqueeze(1).to_broadcast(shape), ALU.mult))
            st.link(nc.vector.reduce_sum(tab[:, 1], past[:], axis=mybir.AxisListType.X))
            st.link(nc.vector.tensor_tensor(tab[:, 1], slot[:], tab[:, 1], ALU.subtract))
            st.link(nc.vector.tensor_scalar(tab[:, 2], tab[:, 0], float(E), float(P), ALU.is_lt, ALU.mult))
            st.link(nc.vector.tensor_tensor(tab[:, 2], tab[:, 2], tab[:, 1], ALU.mult))
            st.link(nc.vector.scalar_tensor_tensor(tab[:, 3], tab[:, 0], float(REGION), tab[:, 2], ALU.mult, ALU.add))
            st.link(nc.vector.tensor_copy(tabi[:, 0], tab[:, 3]))
            st.link(nc.vector.tensor_scalar(tab[:, 3], tab[:, 0], float(E - 1), None, ALU.min))
            st.link(nc.vector.tensor_copy(tabi[:, 1], tab[:, 3]))
            nc.vector.sem_inc(table_ready, 1)
            st.link(nc.vector.tensor_tensor(shift[:], ends[:], n_tiles[:], ALU.subtract))
            st.link(nc.vector.scalar_tensor_tensor(shift[:], shift[:], float(P), sh.region[:], ALU.mult, ALU.subtract))
            st.mark(nc.vector.tensor_copy(rise[:, 0:1], shift[:, 0:1]))
            st.mark(nc.vector.tensor_tensor(rise[:, 1:E], shift[:, 1:E], shift[:, 0:E - 1], ALU.subtract))
            shape = [P, N * 2, E]
            flat = sh.pos[:].rearrange("p t k -> p (t k)")
            st.link(nc.vector.tensor_tensor(above[:], flat.unsqueeze(2).to_broadcast(shape),
                                            sh.region[:].unsqueeze(1).to_broadcast(shape), ALU.is_ge))
            st.link(nc.vector.tensor_tensor(above[:], above[:], rise[:].unsqueeze(1).to_broadcast(shape), ALU.mult))
            st.link(nc.vector.reduce_sum(moved[:], above[:], axis=mybir.AxisListType.X))
            st.link(nc.vector.tensor_tensor(moved[:], moved[:], flat, ALU.add))
            st.link(nc.vector.tensor_scalar(moved[:], moved[:], float(SLOTS * P - 1), None, ALU.min))
            st.link(nc.vector.tensor_copy(ypos[:], moved[:]))
            nc.vector.sem_inc(ypos_ready, 1)
            st.link(nc.vector.tensor_tensor(tw[:], sh.top[:, :, 0:2], sh.top[:, :, 0:1].to_broadcast([P, TILES + 1, 2]), ALU.subtract))
            nc.vector.sem_inc(weights_ready, 1)
            dve.wait_ge(exp_ready, 1)
            st.link(nc.vector.tensor_tensor(tz[:], tw[:, :, 0:1], tw[:, :, 1:2], ALU.add))
            st.link(nc.vector.reciprocal(tz[:], tz[:]))
            st.link(nc.vector.tensor_tensor(tw[:], tw[:], tz[:].to_broadcast([P, TILES + 1, 2]), ALU.mult))

            def gate(s, u):
                dve.wait_ge(silu_ready, s + 1)
                nc.vector.tensor_tensor(hh[u][:], sl[u][:], bb[u][:], ALU.mult).then_inc(h_ready, 1)

            gate(0, 0)

            def turn(s, u, left):
                dve.wait_ge(ht_ps, s + 1)
                nc.vector.tensor_copy(ht[u][:], bh[:].rearrange("p (j n) -> p j n", n=P)).then_inc(ht_sb, 1)
                if left >= 1:
                    gate(s + 1, 1 - u)

            schedule(dve, turn)
            for t in range(TILES + 1):
                r = t % (2 * RING)
                dve.wait_ge(gathered[r], 32 * (t // (2 * RING) + 1))
                for k in range(2):
                    nc.vector.scalar_tensor_tensor(sh.h2[:, t], yg[r][:, k], tw[:, t, k:k + 1], sh.h2[:, t], ALU.mult, ALU.add) \
                        .then_inc(summed if k else step, 1)
                    if not k:
                        st.n += 1
                        st.wait()

        @block.scalar
        def _(act):
            act.wait_ge(weights_ready, 1)
            nc.scalar.activation(tw[:], tw[:], ACT.Exp).then_inc(exp_ready, 1)

            def load(s, u):
                row = act.value_load(tabi[0:1, 0, bass.ds(s, 1)], min_val=0, max_val=SPARE)
                act.dma_start(xs[u][:], x_slots[bass.ds(row, P), :]).then_inc(x_in[u], 16)

            def x_copy(s, u, more):
                act.wait_ge(xt_ps, s + 1)
                nc.scalar.copy(xt[u][:], bt[:, 0:2 * P].rearrange("p (k n) -> p k n", k=2)).then_inc(xt_sb, 1)
                if more:
                    load(s + 2, u)

            def silu(s, u):
                act.wait_ge(up_ps, s + 1)
                nc.scalar.activation(sl[u][:], ba[u][:], ACT.Silu).then_inc(silu_ready, 1)

            act.wait_ge(table_ready, 1)
            act.wait_ge(tiles_ready, 1)
            for u in range(2):
                load(u, u)
            for u in range(2):
                x_copy(u, u, True)
            silu(0, 0)

            def turn(s, u, left):
                if left >= 2:
                    x_copy(s + 2, u, left >= 4)
                if left >= 1:
                    silu(s + 1, 1 - u)
                act.wait_ge(y_ps, s + 1)
                if not (isinstance(s, int) and s < 2):
                    act.wait_ge(y_stored[u], 8 * (s - u))
                nc.scalar.copy(ys[u][:], by[u][:, 0:D]).then_inc(y_sb, 1)

            schedule(act, turn)

        @block.tensor
        def _(pe):
            pe.wait_ge(table_ready, 1)
            for e in range(E):
                pe.wait_ge(sh.experts_in[e], 16)

            def x_transpose(s, u):
                pe.wait_ge(x_in[u], 8 * (s - u) + 16)
                if not (isinstance(s, int) and s == 0):
                    pe.wait_ge(xt_sb, s)
                for k in range(2):
                    last = nc.tensor.transpose(bt[:, k * P:(k + 1) * P], xs[u][:, k * P:(k + 1) * P], sh.ident[:])
                last.then_inc(xt_ps, 1)

            def expert_of(s):
                return pe.value_load(tabi[0:1, 1, bass.ds(s, 1)], min_val=0, max_val=E - 1)

            def up(s, u):
                e = expert_of(s)
                pe.wait_ge(xt_sb, s + 1)
                for m, bank in enumerate((ba[u], bb[u])):
                    for k in range(2):
                        col = (2 * m + k) * FF
                        last = nc.tensor.matmul(bank[:], xt[u][:, k], experts[:, bass.ds(e, 1), col:col + FF]
                                                .rearrange("p o n -> p (o n)"), start=(k == 0), stop=(k == 1))
                last.then_inc(up_ps, 1)

            x_transpose(0, 0)
            x_transpose(1, 1)
            up(0, 0)

            def turn(s, u, left):
                if left >= 2:
                    x_transpose(s + 2, u)
                pe.wait_ge(h_ready, s + 1)
                for j in range(FF // P):
                    last = nc.tensor.transpose(bh[:, j * P:(j + 1) * P], hh[u][:, j * P:(j + 1) * P], sh.ident[:])
                last.then_inc(ht_ps, 1)
                if left >= 1:
                    up(s + 1, 1 - u)
                e = expert_of(s)
                pe.wait_ge(ht_sb, s + 1)
                if not (isinstance(s, int) and s < 2):
                    pe.wait_ge(y_sb, s - 1)
                for j in range(FF // P):
                    col = 4 * FF + j * D
                    last = nc.tensor.matmul(by[u][:, 0:D], ht[u][:, j], experts[:, bass.ds(e, 1), col:col + D]
                                            .rearrange("p o n -> p (o n)"), start=(j == 0), stop=(j == FF // P - 1))
                last.then_inc(y_ps, 1)

            schedule(pe, turn)


def build(nc, ins, out):
    h_rows = nc.dram_tensor("h_rows", (TOK, BATCH, D), F32, kind="Internal").ap()
    x_slots = nc.dram_tensor("x_slots", (SPARE + P, D), F32, kind="Internal").ap()
    y_slots = nc.dram_tensor("y_slots", (SLOTS * P, D), F32, kind="Internal").ap()
    with ExitStack() as ctx:
        sh = Shared(nc, ctx)
        count = []
        with ExitStack() as stage:
            stage_kernel(nc, stage, ins["params"], ins["b"], ins["c"], h_rows, lambda sp: count.append(load_weights(sp, sh, ins)))
        experts = ctx.enter_context(nc.sbuf_tensor("experts", [P, E, EW], F32))
        bk = [ctx.enter_context(nc.psum_tensor(f"bank{n}", [P, 512], F32)) for n in range(8)]
        with ExitStack() as stage:
            stage_class_token(nc, stage, sh, bk, count[0])
        with ExitStack() as stage:
            stage_attention(nc, stage, sh, bk, h_rows, x_slots, experts, ins["experts"])
        with ExitStack() as stage:
            stage_experts(nc, stage, sh, bk, experts, ins["experts"], x_slots, y_slots, out)


def kernel(**inputs):
    import numpy as _np
    import concourse.bacc as _bacc
    from concourse import mybir as _mybir
    from concourse.bass_utils import run_bass_kernel_spmd as _run

    g = {k: _np.asarray(a) for k, a in inputs.items()}
    par = lambda a: a.reshape(PAIRS, 2, N_STATE).transpose(1, 2, 0).reshape(P, PAIRS)
    log_dt = _np.repeat(g["L0_tok_log_dt"][:, None], N_STATE, axis=1)
    split = lambda w: w.transpose(2, 0, 1).reshape(w.shape[2] // P, P, E, w.shape[1]).transpose(1, 2, 0, 3).reshape(P, E, -1)
    a = {
        "params": _np.stack([par(log_dt), par(g["L0_tok_inv_A_real"]), par(g["L0_tok_A_imag"])], axis=1),
        "b": _np.stack([par(g["L0_tok_B_ri"][..., r]) for r in range(2)], axis=1),
        "c": g["x"].reshape(BATCH, PAIRS, 2, N_STATE, 2).transpose(2, 3, 4, 1, 0).reshape(P, 2, PAIRS, BATCH),
        "cls": g["cls_tok"].reshape(1, D),
        "Wq": g["L0_attn_Wq"], "Wk": g["L0_attn_Wk"], "Wv": g["L0_attn_Wv"], "Wg": g["L0_attn_Wg"], "Wo": g["L0_attn_Wo"],
        "gk_w1": g["L0_attn_gk_w1"], "gk_w2": g["L0_attn_gk_w2"],
        "gk_b2": g["L0_attn_gk_b2"].reshape(2, P).T,
        "gnorm": g["L0_attn_g_norm_w"].reshape(P, 1),
        "gate": g["L0_ffn_gate_w"].T.reshape(2, P, E).transpose(1, 0, 2),
        "experts": _np.concatenate([split(g["L0_ffn_w1"]), split(g["L0_ffn_w3"]), split(g["L0_ffn_w2"])], axis=2),
    }
    nc = _bacc.Bacc("TRN2", target_bir_lowering=False, num_devices=1)
    arrays, ins = {}, {}
    for name, v in a.items():
        v = _np.ascontiguousarray(v)
        arrays[f"in_{name}"] = v
        ins[name] = nc.dram_tensor(f"in_{name}", v.shape, _mybir.dt.from_np(v.dtype), kind="ExternalInput").ap()
    out = nc.dram_tensor("out", (BATCH, TOK + 1, D), F32, kind="ExternalOutput").ap()
    build(nc, ins, out)
    r = _run(nc, [arrays], core_ids=[0])
    return r.results[0]["out"]
```

```python
from contextlib import ExitStack
import math

import numpy as np
import concourse.bass as bass
from concourse import mybir

F32 = mybir.dt.float32
I32 = mybir.dt.int32
U32 = mybir.dt.uint32
ALU = mybir.AluOpType
ACT = mybir.ActivationFunctionType

P = 128
BATCH = 8
TOK = 256
D = 256
N_STATE = 64

HEADS = 4
DK = 64
DV = 128
VD = HEADS * DV
RANK = 16
CH = 2
SUB = 32
NSUB = P // SUB
GATE_NORM = 16.0
EPS = 1e-5
E = 8
FF = 512
EW = 2 * 2 * FF + FF // P * D
TILES = BATCH * CH
REGION = BATCH * TOK + P + 8
SPARE = E * REGION
WEIGHTS = 10
XW = D + 2
ROW0 = TOK + 1
SINK = BATCH * ROW0
PAIRED = 2 * (BATCH * TOK + 1)
SLOTS = -(-((PAIRED + E * (P - 1)) // P) // 2) * 2

PAIRS = TOK // 2
LOW = 8
POW = 64
SHIFTS = D // POW
GROUP = 16
TURNS = PAIRS // GROUP
ROWS = 2 * BATCH * SHIFTS


def stage_kernel(nc, ctx, params, bri, crv, h_rows, first):
    def sb(name, shape, dt=F32):
        return ctx.enter_context(nc.sbuf_tensor(name, shape, dt))

    def sem(name):
        return ctx.enter_context(nc.semaphore(name))

    logs = sb("logs", [P, 3, PAIRS])
    b_in = sb("b_in", [P, 2, PAIRS])
    c_in = sb("c_in", [P, 2, PAIRS, BATCH])
    et = sb("et", [P, 2, PAIRS])
    ek = sb("ek", [P, 2, PAIRS])
    er = sb("er", [P, 2, PAIRS])
    ep = sb("ep", [P, 2, PAIRS])
    ei = sb("ei", [P, 2, PAIRS], I32)
    ab = sb("ab", [P, 2, PAIRS])
    tmp = sb("tmp", [P, 4, PAIRS])
    zp = sb("zp", [P, 8, 2, PAIRS])
    low = sb("low", [P, 2, PAIRS, LOW])
    lt = sb("lt", [P, 2, 2, PAIRS, 4])
    wsrc = sb("wsrc", [P, SHIFTS, 2, PAIRS])
    w = sb("w", [P, 3, PAIRS, SHIFTS])
    v = [sb(f"v{u}", [P, 2, GROUP, POW]) for u in range(2)]
    vt = sb("vt", [P, 2, 2, GROUP, POW // 2])
    x = [sb(f"x{u}", [P, 2, GROUP, ROWS]) for u in range(2)]
    xt = [sb(f"xt{u}", [P, 2, 2, GROUP, BATCH, SHIFTS]) for u in range(2)]
    k_sb = [sb(f"k_sb{u}", [ROWS, GROUP, POW]) for u in range(2)]
    k_ps = [ctx.enter_context(nc.psum_tensor(f"k_ps{u}", [ROWS, GROUP, POW], F32)) for u in range(2)]

    params_in, b_arrived, c_arrived = sem("params_in"), sem("b_arrived"), sem("c_arrived")
    chain = sem("a_chain")
    powers_ready = sem("powers_ready")
    w_ready = sem("w_ready")
    low_ready = sem("low_ready")
    xzero = sem("xzero")
    v_step = sem("v_step")
    v_ready = sem("v_ready")
    x_step = sem("x_step")
    x_ready = sem("x_ready")
    xt_ready, x_half = sem("xt_ready"), sem("x_half")
    products_done = sem("products_done")
    k_copied = sem("k_copied")
    k_stored = [sem(f"k_stored{u}") for u in range(2)]

    def x_sum(u, par):
        ps, cols = slice(par * N_STATE, (par + 1) * N_STATE), slice(par * ROWS // 2, (par + 1) * ROWS // 2)
        return (x[u][ps, :, :, cols], xt[u][ps, 0].rearrange("p r j c a -> p r j (c a)"),
                xt[u][ps, 1].rearrange("p r j c a -> p r j (c a)"))

    with nc.Block() as block:
        @block.sync
        def _(sp):
            first.sync(sp)
            sp.dma_start(logs[:], params).then_inc(params_in, 16)
            first.load_weights(sp)
            sp.dma_start(b_in[:], bri).then_inc(b_arrived, 16)
            sp.dma_start(c_in[:], crv).then_inc(c_arrived, 16)

            def turn(t, u):
                sp.wait_ge(k_copied, t + 1)
                for par in range(2):
                    half = ROWS // 2
                    src = k_sb[u][par * half:(par + 1) * half]
                    dst = h_rows[bass.ds(t * 2 * GROUP + par, GROUP, step=2)] \
                        .rearrange("j c (a b) -> (c a) j b", b=POW)
                    sp.dma_start(dst, src).then_inc(k_stored[u], 16)

            with sp.Fori(0, TURNS // 2) as i:
                for u in range(2):
                    turn(2 * i + u, u)
            for u in range(2):
                sp.wait_ge(k_stored[u], 16 * TURNS)

        @block.vector
        def _(dve):
            count = [0]

            def link(ins):
                count[0] += 1
                ins.then_inc(chain, 1)
                dve.wait_ge(chain, count[0])

            dve.wait_ge(params_in, 16)
            big = 1.5 * 2.0 ** 23
            lg = logs[:, 0:2]
            link(nc.vector.tensor_scalar(et[:], lg, 1.0 / math.log(2.0), big, ALU.mult, ALU.add))
            link(nc.vector.tensor_scalar(ek[:], et[:], -big, -126.0, ALU.add, ALU.max))
            hi = 0.693359375
            link(nc.vector.scalar_tensor_tensor(er[:], ek[:], -hi, lg, ALU.mult, ALU.add))
            link(nc.vector.scalar_tensor_tensor(er[:], ek[:], hi - math.log(2.0), er[:], ALU.mult, ALU.add))
            link(nc.vector.tensor_scalar(et[:], ek[:], 127.0, 2.0 ** 23, ALU.add, ALU.mult))
            link(nc.vector.tensor_copy(ei[:], et[:]))
            link(nc.vector.tensor_scalar(ep[:], er[:], 1.0 / math.factorial(7), None, ALU.mult))
            for k in range(6, 0, -1):
                link(nc.vector.scalar_tensor_tensor(ep[:], ep[:], 1.0 / math.factorial(k), er[:], ALU.add, ALU.mult))
            link(nc.vector.scalar_tensor_tensor(ek[:], ep[:], 1.0, ei[:].bitcast(F32), ALU.add, ALU.mult))
            link(nc.vector.scalar_tensor_tensor(ab[:, 0], ek[:, 1], 0.5, ek[:, 0], ALU.mult, ALU.mult))
            link(nc.vector.scalar_tensor_tensor(ab[:, 1], logs[:, 2], 0.5, ek[:, 0], ALU.mult, ALU.mult))
            a, b = ab[:, 0], ab[:, 1]
            link(nc.vector.tensor_scalar(tmp[:, 0], a, 1.0, None, ALU.add))
            link(nc.vector.tensor_tensor(tmp[:, 0], tmp[:, 0], tmp[:, 0], ALU.mult))
            link(nc.vector.tensor_tensor(tmp[:, 1], b, b, ALU.mult))
            link(nc.vector.tensor_tensor(tmp[:, 0], tmp[:, 0], tmp[:, 1], ALU.add))
            link(nc.vector.reciprocal(tmp[:, 0], tmp[:, 0]))
            link(nc.vector.tensor_tensor(tmp[:, 2], a, a, ALU.mult))
            link(nc.vector.tensor_tensor(tmp[:, 2], tmp[:, 2], tmp[:, 1], ALU.add))
            link(nc.vector.tensor_scalar(tmp[:, 2], tmp[:, 2], -1.0, 1.0, ALU.mult, ALU.add))
            link(nc.vector.tensor_tensor(zp[:, 0, 0], tmp[:, 2], tmp[:, 0], ALU.mult))
            link(nc.vector.scalar_tensor_tensor(zp[:, 0, 1], b, 2.0, tmp[:, 0], ALU.mult, ALU.mult))
            for k in range(1, 8):
                zr, zi = zp[:, k - 1, 0], zp[:, k - 1, 1]
                nc.vector.tensor_tensor(tmp[:, 0:2], zp[:, k - 1], zp[:, k - 1], ALU.mult).then_inc(chain, 1)
                count[0] += 1
                link(nc.vector.scalar_tensor_tensor(zp[:, k, 1], zr, 2.0, zi, ALU.mult, ALU.mult))
                link(nc.vector.tensor_tensor(zp[:, k, 0], tmp[:, 0], tmp[:, 1], ALU.subtract))

            def times(out_re, out_im, p, q, zr, zi, src, op_im=ALU.add, neg=False):
                nc.vector.tensor_tensor(p, src, zr, ALU.mult).then_inc(chain, 1)
                count[0] += 1
                link(nc.vector.tensor_tensor(q, src, zi, ALU.mult))
                nc.vector.tensor_tensor(out_re, p[:, 0], q[:, 1], ALU.subtract).then_inc(chain, 1)
                count[0] += 1
                link(nc.vector.tensor_tensor(out_im, p[:, 1], q[:, 0], ALU.add))

            dve.wait_ge(b_arrived, 16)
            link(nc.vector.tensor_scalar(tmp[:, 0:2], b_in[:], 2.0, None, ALU.mult))
            cur = tmp[:, 0:2]
            link(nc.vector.tensor_copy(wsrc[:, 0], cur))
            for dst, src, k in ((1, 0, 6), (2, 0, 7), (3, 1, 7)):
                zr = zp[:, k, 0].unsqueeze(1).to_broadcast([P, 2, PAIRS])
                zi = zp[:, k, 1].unsqueeze(1).to_broadcast([P, 2, PAIRS])
                times(wsrc[:, dst, 0], wsrc[:, dst, 1], tmp[:, 0:2], tmp[:, 2:4], zr, zi, wsrc[:, src])
            nc.vector.sem_inc(powers_ready, 1)
            link(nc.vector.memset(low[:, 0, :, 0:1], 1.0))
            link(nc.vector.memset(low[:, 1, :, 0:1], 0.0))
            link(nc.vector.tensor_copy(low[:, :, :, 1], zp[:, 0]))
            for k in (1, 2):
                n = 2 ** k
                zr = zp[:, k, 0].unsqueeze(1).unsqueeze(3).to_broadcast([P, 2, PAIRS, n])
                zi = zp[:, k, 1].unsqueeze(1).unsqueeze(3).to_broadcast([P, 2, PAIRS, n])
                times(low[:, 0, :, n:2 * n], low[:, 1, :, n:2 * n], lt[:, 0, :, :, 0:n], lt[:, 1, :, :, 0:n],
                      zr, zi, low[:, :, :, 0:n])
            per_turn = 12

            def turn(t, u, first):
                base = t * (per_turn + 1) if first else (t - 2) * per_turn + 2 * (per_turn + 1)
                js = bass.ds(t * GROUP, GROUP)
                if first:
                    nc.vector.tensor_copy(v[u][:, :, :, 0:LOW], low[:, :, js, :]).then_inc(v_step, 1)
                    dve.wait_ge(v_step, base + 1)
                    done = 1
                else:
                    dve.wait_ge(low_ready, t - 1)
                    done = 0
                for k in (3, 4, 5):
                    n = 2 ** k
                    zr = zp[:, k, 0, js].unsqueeze(1).unsqueeze(3).to_broadcast([P, 2, GROUP, n])
                    zi = zp[:, k, 1, js].unsqueeze(1).unsqueeze(3).to_broadcast([P, 2, GROUP, n])
                    p, q = vt[:, 0, :, :, 0:n], vt[:, 1, :, :, 0:n]
                    nc.vector.tensor_tensor(p, v[u][:, :, :, 0:n], zr, ALU.mult).then_inc(v_step, 1)
                    nc.vector.tensor_tensor(q, v[u][:, :, :, 0:n], zi, ALU.mult).then_inc(v_step, 1)
                    done += 2
                    dve.wait_ge(v_step, base + done)
                    nc.vector.tensor_tensor(v[u][:, 0, :, n:2 * n], p[:, 0], q[:, 1], ALU.subtract).then_inc(v_step, 1)
                    last = nc.vector.tensor_tensor(v[u][:, 1, :, n:2 * n], p[:, 1], q[:, 0], ALU.add)
                    last.then_inc(v_step, 1)
                    done += 2
                    dve.wait_ge(v_step, base + done)
                nc.vector.sem_inc(v_ready, 1)
                if u == 1:
                    dve.wait_ge(xt_ready, t + 1)
                    nc.vector.tensor_tensor(*x_sum(u, 1), ALU.add).then_inc(x_half, 1)

            for u in range(2):
                turn(u, u, True)
            with dve.Fori(1, TURNS // 2) as i:
                for u in range(2):
                    turn(2 * i + u, u, False)

        @block.gpsimd
        def _(pool):
            first.pool_constants(pool)
            for u in range(2):
                nc.gpsimd.memset(x[u][:], 0.0).then_inc(xzero, 1)
            first.pool_heads(pool)
            pool.wait_ge(xzero, 2)
            pool.wait_ge(c_arrived, 16)
            pool.wait_ge(w_ready, 3)

            def turn(t, u, first, i=0):
                js = bass.ds(t * GROUP, GROUP)
                shape = [P, GROUP, BATCH, SHIFTS]
                if u == 1 and not first:
                    pool.wait_ge(x_half, i)
                for half in range(2):
                    for r in range(2):
                        cc = c_in[:, half, js].unsqueeze(3).to_broadcast(shape)
                        ww = w[:, half + r, js].unsqueeze(2).to_broadcast(shape)
                        nc.gpsimd.tensor_tensor(xt[u][:, half, r], cc, ww, ALU.mult).then_inc(x_step, 1)
                pool.wait_ge(x_step, 4 * (t + 1))
                nc.gpsimd.sem_inc(xt_ready, 1)
                if not first:
                    pool.wait_ge(products_done, t - 1)
                for par in range(2 - u):
                    nc.gpsimd.tensor_tensor(*x_sum(u, par), ALU.add).then_inc(x_ready, 1)
                pool.wait_ge(x_ready, 3 * i + 2 + u)

            turn(0, 0, True)
            first.pool_norm(pool)
            turn(1, 1, True)
            with pool.Fori(1, TURNS // 2) as i:
                for u in range(2):
                    turn(2 * i + u, u, False, i)

        @block.tensor
        def _(pe):
            first.tensor(pe)

            def turn(t, u, first, i=0):
                pe.wait_ge(x_ready, 3 * i + 2 + u)
                if u == 1:
                    pe.wait_ge(x_half, i + 1)
                pe.wait_ge(v_ready, t + 1)
                if not first:
                    pe.wait_ge(k_copied, t - 1)
                for j in range(GROUP):
                    for r in range(2):
                        last = nc.tensor.matmul(k_ps[u][:, j], x[u][:, r, j], v[u][:, r, j],
                                                start=(r == 0), stop=(r == 1))
                last.then_inc(products_done, 1)

            for u in range(2):
                turn(u, u, True)
            with pe.Fori(1, TURNS // 2) as i:
                for u in range(2):
                    turn(2 * i + u, u, False, i)

        @block.scalar
        def _(act):
            first.scalar_heads(act)
            act.wait_ge(powers_ready, 1)
            for r, (part, sign) in enumerate(((0, 1.0), (1, -1.0), (0, -1.0))):
                nc.scalar.mul(w[:, r], wsrc[:, :, part].rearrange("p a j -> p j a"), sign).then_inc(w_ready, 1)

            first.scalar_rows(act)

            def turn(t, u, first, last=False):
                act.wait_ge(products_done, t + 1)
                if not last:
                    nc.scalar.copy(v[u][:, :, :, 0:LOW], low[:, :, bass.ds((t + 2) * GROUP, GROUP), :]).then_inc(low_ready, 1)
                if not first:
                    act.wait_ge(k_stored[u], 16 * (t - u))
                nc.scalar.copy(k_sb[u][:], k_ps[u][:]).then_inc(k_copied, 1)

            for u in range(2):
                turn(u, u, True)
            with act.Fori(1, TURNS // 2 - 1) as i:
                for u in range(2):
                    turn(2 * i + u, u, False)
            for u in range(2):
                turn(TURNS - 2 + u, u, False, True)

class Steps:

    def __init__(self, eng, sem, base=0, apart=None):
        self.eng, self.sem, self.base, self.n, self.apart = eng, sem, base, 0, apart

    def mark(self, ins):
        ins.then_inc(self.sem, 1)
        self.n += 1

    def wait(self):
        self.eng.wait_ge(self.sem, self.base + self.n)

    def wait_apart(self):
        self.wait()
        self.eng.sem_inc(self.apart, 1)

    def link(self, ins):
        self.mark(ins)
        self.wait()


class Shared:

    def __init__(self, nc, ctx):
        def sb(name, shape, dt=F32):
            return ctx.enter_context(nc.sbuf_tensor(name, shape, dt))

        self.wq = sb("wq", [P, 2, D])
        self.wk = sb("wk", [P, 2, D])
        self.wv = sb("wv", [P, 2, VD])
        self.wg = sb("wg", [P, 2, VD])
        self.wo = sb("wo", [P, HEADS, D])
        self.gw1 = sb("gw1", [P, 2, RANK])
        self.gw2 = sb("gw2", [RANK, D])
        self.gb2 = sb("gb2", [P, 2])
        self.gnorm = sb("gnorm", [P, 1])
        self.gate = sb("gate", [P, 2, E])
        self.ident = sb("ident", [P, P])
        self.causal = sb("causal", [P, P])
        self.before = sb("before", [P, P])
        self.ones = sb("ones", [P, P])
        self.iota8 = sb("iota8", [P, E])
        self.region = sb("region", [P, E])
        self.pad = sb("pad", [P, XW])
        self.tok = sb("tok", [P, TILES])
        self.row0 = sb("row0", [P, 1])
        self.keep = sb("keep", [P, CH * 2 * P])
        self.s_cls = sb("s_cls", [P, 2, 2 * DV])
        self.h2 = sb("h2", [P, TILES + 1, D])
        self.x2c = sb("x2c", [1, 2, XW])
        self.sc_cls = sb("sc_cls", [P, E])
        self.tabi = sb("tabi", [1, 2, SLOTS], I32)
        self.carry = sb("carry", [P, E])
        self.experts_in = ctx.enter_context(nc.semaphore("experts_in"))
        self.weights_in = ctx.enter_context(nc.semaphore("weights_in"))


class ClassToken:

    def __init__(self, nc, ctx, sh, ins):
        def sb(name, shape, dt=F32):
            return ctx.enter_context(nc.sbuf_tensor("c_" + name, shape, dt))

        def sem(name):
            return ctx.enter_context(nc.semaphore("c_" + name))

        self.nc, self.sh, self.ins = nc, sh, ins
        self.cls = sb("cls", [P, 2])
        self.neg_mean, self.var, self.rstd = (sb(n, [P, 2]) for n in ("neg_mean", "var", "rstd"))
        self.xm, self.sq2, self.spill = sb("xm", [P, 2]), sb("sq2", [P, 2]), sb("spill", [P, 2])
        self.xc = sb("xc", [P, 2])
        self.xb = sb("xb", [P, 2, P])
        self.cols = sb("cols", [P, 2 + 2 + HEADS])
        self.qk = sb("qk", [P, HEADS])
        self.gate = sb("gate", [P, HEADS])
        self.dots = sb("dots", [P, 2, HEADS])
        self.oc, self.sq4, self.rs = sb("oc", [P, HEADS]), sb("sq4", [P, HEADS]), sb("rs", [P, HEADS])
        self.h2, self.x2 = sb("h2", [P, 2]), sb("x2", [P, 2])
        self.half = sb("half", [P, HEADS])
        self.sums, self.proj, self.vrow, self.rows = (ctx.enter_context(nc.psum_tensor("c_" + n, [P, 512], F32))
                                                      for n in ("sums", "proj", "vrow", "rows"))
        self.cls_in = sem("cls_in")
        self.made, self.pool_chain, self.act_chain = sem("made"), sem("pool_chain"), sem("act_chain")
        self.pe_did, self.act_did, self.pool_did = sem("pe_did"), sem("act_did"), sem("pool_did")

    def sync(self, sp):
        sp.dma_start(self.cls[:], self.ins["cls"]).then_inc(self.cls_in, 16)

    def load_weights(self, sp):
        sh, ins = self.sh, self.ins
        wide = lambda name: ins[name].rearrange("(k p) n -> p k n", p=P)
        pairs = [(sh.wq, wide("Wq")), (sh.wk, wide("Wk")), (sh.wv, wide("Wv")), (sh.wg, wide("Wg")), (sh.wo, wide("Wo")),
                 (sh.gw1, wide("gk_w1")), (sh.gw2, ins["gk_w2"]), (sh.gb2, ins["gk_b2"]), (sh.gnorm, ins["gnorm"]),
                 (sh.gate, ins["gate"])]
        for dst, src in pairs:
            sp.dma_start(dst[:], src).then_inc(sh.weights_in, 16)
        assert len(pairs) == WEIGHTS

    def pool_constants(self, pool):
        nc, sh = self.nc, self.sh
        nc.gpsimd.memset(sh.ones[:], 1.0).then_inc(self.pool_did, 1)
        nc.gpsimd.memset(self.half[:], -0.5).then_inc(self.made, 1)
        nc.gpsimd.memset(self.qk[:], 0.0).then_inc(self.made, 1)
        nc.gpsimd.memset(sh.ident[:], 0.0).then_inc(self.made, 1)
        nc.gpsimd.memset(sh.causal[:], 1.0).then_inc(self.made, 1)
        nc.gpsimd.memset(sh.before[:], 1.0).then_inc(self.made, 1)
        nc.gpsimd.memset(sh.row0[:], 0.0).then_inc(self.made, 1)
        nc.gpsimd.memset(sh.s_cls[:], 0.0).then_inc(self.made, 1)
        nc.gpsimd.memset(sh.sc_cls[:], 0.0).then_inc(self.made, 1)
        nc.gpsimd.memset(sh.x2c[:, :, D + 1:XW], 0.0).then_inc(self.made, 1)
        pool.wait_ge(self.made, 9)
        nc.gpsimd.affine_select(out=sh.ident[:], in_=sh.ident[:], compare_op=ALU.not_equal, fill=1.0, base=0,
                                pattern=[[-1, P]], channel_multiplier=1).then_inc(self.made, 1)
        nc.gpsimd.affine_select(out=sh.causal[:], in_=sh.causal[:], compare_op=ALU.is_ge, fill=0.0, base=0,
                                pattern=[[1, P]], channel_multiplier=-1).then_inc(self.made, 1)
        nc.gpsimd.affine_select(out=sh.before[:], in_=sh.before[:], compare_op=ALU.is_ge, fill=0.0, base=-1,
                                pattern=[[1, P]], channel_multiplier=-1).then_inc(self.made, 1)
        nc.gpsimd.affine_select(out=sh.row0[:], in_=sh.row0[:], compare_op=ALU.not_equal, fill=1.0, base=0,
                                pattern=[[0, 1]], channel_multiplier=1).then_inc(self.made, 1)
        nc.gpsimd.memset(sh.keep[:], 1.0).then_inc(self.made, 1)
        pool.wait_ge(self.made, 14)
        nc.gpsimd.memset(sh.keep[:].rearrange("p (b s) -> p b s", s=SUB)[:, :, 0:1], 0.0).then_inc(self.made, 1)
        nc.gpsimd.iota(sh.iota8[:], [[1, E]], base=0, channel_multiplier=0,
                       allow_small_or_imprecise_dtypes=True).then_inc(self.made, 1)
        nc.gpsimd.iota(sh.region[:], [[REGION, E]], base=0, channel_multiplier=0,
                       allow_small_or_imprecise_dtypes=True).then_inc(self.made, 1)
        nc.gpsimd.iota(sh.pad[:, D + 1:XW], [[0, 1]], base=SINK, channel_multiplier=1,
                       allow_small_or_imprecise_dtypes=True).then_inc(self.made, 1)
        nc.gpsimd.iota(sh.tok[:], [[ROW0, BATCH], [P, CH]], base=1, channel_multiplier=1,
                       allow_small_or_imprecise_dtypes=True).then_inc(self.made, 1)
        nc.gpsimd.memset(sh.pad[:, 0:D + 1], 0.0).then_inc(self.made, 1)

    def root(self, pool, n_chain, out, src, scale, n):
        self.nc.gpsimd.tensor_scalar(out, src, scale, EPS, ALU.mult, ALU.add).then_inc(self.pool_chain, 1)
        pool.wait_ge(self.pool_chain, n_chain)
        return self.nc.gpsimd.tensor_tensor(out, out, self.half[:, 0:n], ALU.pow)

    def pool_heads(self, pool):
        nc, root = self.nc, lambda *args: self.root(pool, *args)
        pool.wait_ge(self.act_did, 2)
        root(1, self.rstd[:, 0:1], self.var[:, 0:1], 1.0, 1).then_inc(self.pool_did, 1)
        pool.wait_ge(self.act_did, 7)
        nc.gpsimd.tensor_tensor(self.oc[:], self.cols[:, 4:], self.dots[:, 0], ALU.mult).then_inc(self.pool_did, 1)
        pool.wait_ge(self.act_did, 9)
        root(2, self.rs[:], self.dots[:, 1], 1.0 / DV, HEADS).then_inc(self.pool_chain, 1)
        pool.wait_ge(self.pool_chain, 3)
        nc.gpsimd.tensor_tensor(self.rs[:], self.rs[:], self.oc[:], ALU.mult).then_inc(self.pool_chain, 1)
        pool.wait_ge(self.pool_chain, 4)
        nc.gpsimd.tensor_tensor(self.rs[:], self.rs[:], self.gate[:], ALU.mult).then_inc(self.pool_did, 1)

    def pool_norm(self, pool):
        pool.wait_ge(self.act_did, 12)
        self.root(pool, 5, self.rstd[:, 1:2], self.var[:, 1:2], 1.0, 1).then_inc(self.pool_did, 1)

    def norm(self, act, n, src, sums, out):
        nc, st = self.nc, self.steps
        st.link(nc.scalar.activation(self.spill[:], sums(0), ACT.Copy, scale=-1.0 / D, accum_out=self.neg_mean[:, n:n + 1]))
        st.link(nc.scalar.activation(self.xm[:], src, ACT.Identity, bias=self.neg_mean[:, n:n + 1]))
        nc.scalar.activation(self.sq2[:], self.xm[:], ACT.Square).then_inc(self.act_did, 1)
        act.wait_ge(self.pe_did, 2 + 6 * n)
        nc.scalar.activation(self.spill[:], sums(1), ACT.Copy, scale=1.0 / D, accum_out=self.var[:, n:n + 1]).then_inc(self.act_did, 1)
        act.wait_ge(self.pool_did, 2 + 3 * n)
        nc.scalar.activation(out, self.xm[:], ACT.Copy, scale=self.rstd[:, n:n + 1]).then_inc(self.act_did, 1)

    def scalar_heads(self, act):
        nc, sh = self.nc, self.sh
        st = self.steps = Steps(act, self.act_chain)
        act.wait_ge(self.pe_did, 1)
        act.wait_ge(self.cls_in, 16)
        self.norm(act, 0, self.cls[:], lambda k: self.sums[:, 2 * k:2 * k + 2], self.xc[:])
        act.wait_ge(self.act_did, 3)
        nc.scalar.copy(self.xb[:], self.xc[:].unsqueeze(2).to_broadcast([P, 2, P])).then_inc(self.act_did, 1)
        act.wait_ge(sh.weights_in, 16 * WEIGHTS)
        st.mark(nc.scalar.activation(sh.wo[:], sh.wo[:], ACT.Copy, scale=sh.gnorm[:]))
        act.wait_ge(self.pe_did, 3)
        st.mark(nc.scalar.mul(self.cols[:, 0:2], self.proj[:, 0:2], DK ** -0.5))
        st.link(nc.scalar.copy(self.cols[:, 2:], self.proj[:, 2:4 + HEADS]))
        act.wait_ge(self.made, 9)
        for t in range(2):
            for par in range(2):
                rows, h = slice(par * DK, (par + 1) * DK), 2 * t + par
                st.mark(nc.scalar.activation(self.qk[rows, h:h + 1], self.cols[rows, t:t + 1], ACT.Copy, scale=self.cols[rows, 2 + t:3 + t]))
        st.wait()
        nc.scalar.sem_inc(self.act_did, 1)
        nc.scalar.activation(self.gate[:], self.proj[:, 8:8 + HEADS], ACT.Silu).then_inc(self.act_did, 1)
        act.wait_ge(self.pe_did, 4)
        nc.scalar.copy(self.dots[:, 0], self.sums[:, 4:4 + HEADS]).then_inc(self.act_did, 1)
        act.wait_ge(self.pool_did, 3)
        nc.scalar.activation(self.sq4[:], self.oc[:], ACT.Square).then_inc(self.act_did, 1)
        act.wait_ge(self.pe_did, 5)
        nc.scalar.copy(self.dots[:, 1], self.sums[:, 8:8 + HEADS]).then_inc(self.act_did, 1)

    def scalar_rows(self, act):
        nc, sh, st = self.nc, self.sh, self.steps
        act.wait_ge(self.pe_did, 6)
        for t in range(2):
            st.mark(nc.scalar.activation(self.h2[:, t:t + 1], self.proj[:, 12 + t:13 + t], ACT.Identity, bias=self.cls[:, t:t + 1]))
        st.wait()
        nc.scalar.sem_inc(self.act_did, 1)
        act.wait_ge(self.pe_did, 7)
        self.norm(act, 1, self.h2[:], lambda k: self.sums[:, 12 + 2 * k:14 + 2 * k], self.x2[:])
        act.wait_ge(self.pe_did, 9)
        act.wait_ge(self.made, 20)
        st.mark(nc.scalar.copy(sh.h2[0:1, TILES], self.rows[0:1, 0:D]))
        for k in range(2):
            st.mark(nc.scalar.copy(sh.x2c[:, k, 0:D], self.rows[0:1, D:2 * D]))
        st.mark(nc.scalar.copy(sh.sc_cls[0:1], self.proj[0:1, 16:16 + E]))
        act.wait_ge(self.pe_did, 10)
        for t in range(2):
            for par in range(2):
                rows, cols = slice(par * DK, (par + 1) * DK), slice(par * DV, (par + 1) * DV)
                st.mark(nc.scalar.activation(sh.s_cls[rows, t, cols], self.vrow[rows, (2 * t + par) * DV:(2 * t + par + 1) * DV],
                                             ACT.Copy, scale=self.cols[rows, 2 + t:3 + t]))
        st.wait()

    def tensor(self, pe):
        nc, sh = self.nc, self.sh

        def total(out, src):
            return nc.tensor.matmul(out, sh.ones[:], src, start=True, stop=True)

        def column(out, w, n):
            for t in range(n):
                for k in range(2):
                    last = nc.tensor.matmul(out[:, t:t + 1], w[:, k, t * P:(t + 1) * P], self.xc[:, k:k + 1], start=(k == 0), stop=(k == 1))
            return last

        pe.wait_ge(self.pool_did, 1)
        pe.wait_ge(self.cls_in, 16)
        total(self.sums[:, 0:2], self.cls[:]).then_inc(self.pe_did, 1)
        pe.wait_ge(self.act_did, 1)
        total(self.sums[:, 2:4], self.sq2[:]).then_inc(self.pe_did, 1)
        pe.wait_ge(self.act_did, 3)
        pe.wait_ge(sh.weights_in, 16 * WEIGHTS)
        column(self.proj[:, 0:2], sh.wq, 2)
        column(self.proj[:, 2:4], sh.wk, 2)
        column(self.proj[:, 4:4 + HEADS], sh.wv, HEADS)
        column(self.proj[:, 8:8 + HEADS], sh.wg, HEADS).then_inc(self.pe_did, 1)
        pe.wait_ge(self.act_did, 5)
        total(self.sums[:, 4:4 + HEADS], self.qk[:]).then_inc(self.pe_did, 1)
        pe.wait_ge(self.act_did, 8)
        total(self.sums[:, 8:8 + HEADS], self.sq4[:]).then_inc(self.pe_did, 1)
        pe.wait_ge(self.pool_did, 4)
        for t in range(2):
            for h in range(HEADS):
                last = nc.tensor.matmul(self.proj[:, 12 + t:13 + t], sh.wo[:, h, t * P:(t + 1) * P], self.rs[:, h:h + 1],
                                        start=(h == 0), stop=(h == HEADS - 1))
        last.then_inc(self.pe_did, 1)
        pe.wait_ge(self.act_did, 10)
        total(self.sums[:, 12:14], self.h2[:]).then_inc(self.pe_did, 1)
        pe.wait_ge(self.act_did, 11)
        total(self.sums[:, 14:16], self.sq2[:]).then_inc(self.pe_did, 1)
        pe.wait_ge(self.act_did, 13)
        pe.wait_ge(self.made, 20)
        for n, src in enumerate((self.h2, self.x2)):
            for t in range(2):
                nc.tensor.matmul(self.rows[0:1, n * D + t * P:n * D + (t + 1) * P], src[:, t:t + 1], sh.ident[:], start=True, stop=True)
        for t in range(2):
            last = nc.tensor.matmul(self.proj[0:1, 16:16 + E], self.x2[:, t:t + 1], sh.gate[:, t], start=(t == 0), stop=(t == 1))
        last.then_inc(self.pe_did, 1)
        for k in range(2):
            last = nc.tensor.matmul(self.vrow[:], self.xb[:, k], sh.wv[:, k], start=(k == 0), stop=(k == 1))
        last.then_inc(self.pe_did, 1)


def stage_attention(nc, ctx, sh, bk, h_rows, x_slots, experts, w_dram, out):
    def sb(name, shape, dt=F32):
        return ctx.enter_context(nc.sbuf_tensor("b_" + name, shape, dt))

    def sem(name):
        return ctx.enter_context(nc.semaphore(name))

    xn = sb("xn", [P, CH, D])
    xt = sb("xt", [P, 2, CH * P])
    t16 = sb("t16", [RANK, CH * P])
    ay = sb("ay", [P, 2, CH * P])
    mn = sb("mn", [P, 2, CH * P])
    e1 = sb("e1", [P, 2 * CH * P])
    e2 = sb("e2", [P, 2 * CH * P])
    e3 = sb("e3", [P, 2 * CH * P])
    q1 = sb("q1", [P, 2, 2 * CH, P])
    qp = sb("qp", [P, 2 * CH * P])
    qs = sb("qs", [P, 2 * CH, P])
    WIDE = 2 * CH * P + SUB
    kv = sb("kv", [P, NSUB * WIDE])
    kst = sb("kst", [P, 2, P])
    pb = sb("pb", [P, 2 * CH, NSUB + 1])
    v = sb("v", [P, CH, VD])
    sg = sb("sg", [P, CH, VD])
    am = sb("am", [P, CH, HEADS, P])
    krow = sb("krow", [P, 2 * P])
    s1 = sb("s1", [P, 2, 2 * DV])
    ss = sb("ss", [P, CH, HEADS])
    rs = sb("rs", [P, CH, HEADS])
    og = sb("og", [P, CH, VD])
    ot = sb("ot", [P, CH, HEADS, P])
    x2 = [sb(f"x2{u}", [P, 2, CH, XW]) for u in range(2)]
    posi = [sb(f"posi{u}", [P, 2, CH], U32) for u in range(2)]
    tw = sb("tw", [P, CH, 2])
    cls_row = sb("cls_row", [1, 2], I32)
    pad_row = sb("pad_row", [1, E], I32)
    n_tiles = sb("n_tiles", [P, E])
    ends = sb("ends", [P, E])
    slot = sb("slot", [1, SLOTS])
    past = mn[0:1].rearrange("p t n -> p (t n)")[:, 0:SLOTS * E].rearrange("p (s e) -> p s e", e=E)
    tab = sb("tab", [1, 4, SLOTS])
    x2t = xn
    stats = sb("stats", [P, CH, 6])
    mom = sb("mom", [P, CH, 2])
    rstd = sb("rstd", [P, CH, 1])
    stats2 = sb("stats2", [P, CH, 6])
    mom2 = sb("mom2", [P, CH, 2])
    rstd2 = sb("rstd2", [P, CH, 1])
    half = sb("half", [P, HEADS])
    ix = sb("ix", [P, CH, 8], U32)
    ixf = sb("ixf", [P, CH, 8])
    oh = sb("oh", [P, 2, CH, E])
    hit = sb("hit", [P, CH, E])
    rank = sb("rank", [P, CH, E])
    pick = sb("pick", [P, 2, CH, E])
    posf = sb("posf", [P, 2, CH])
    sc = sb("sc_now", [P, CH, E])
    topc = sb("topc", [P, CH, 8])

    h_in = [sem(f"h_in{u}") for u in range(3)]
    dve_step, act_step, pool_step = sem("dve_step"), sem("act_step"), sem("pool_step")
    xn_ready, xt_ps, xt_sb = sem("xn_ready"), sem("xt_ps"), sem("xt_sb")
    t16_ps, t16_sb, y_ps, mn_ready, ln_ready = sem("t16_ps"), sem("t16_sb"), sem("y_ps"), sem("mn_ready"), sem("ln_ready")
    cums_ready, exps_ready = sem("cums_ready"), sem("exps_ready")
    q_ps, k_ps, qk_used, kv_ready = sem("q_ps"), sem("k_pst"), sem("qk_used"), sem("kv_ready")
    v_ps, v_sb, g_ps, tanh_sb, sg_ready = sem("v_ps"), sem("v_sb"), sem("g_ps"), sem("tanh_sb"), sem("sg_ready")
    a_ps, masked, krow_ps, krow_sb = sem("a_ps"), sem("masked"), sem("krow_ps"), sem("krow_sb")
    s_ps, s1_ready, o_ps, squared, rs_ready, gated = sem("s_ps"), sem("s1_ready"), sem("o_ps"), sem("squared"), sem("rs_ready"), sem("gated")
    ot_ps, ot_sb, wo_ps, res_used, x2_ready = sem("ot_ps"), sem("ot_sb"), sem("wo_ps"), sem("res_used"), sem("x2_ready")
    x2t_ps, x2t_sb, score_ps, hit_ready = sem("x2t_ps"), sem("x2t_sb"), sem("score_ps"), sem("hit_ready")
    rank_ps, routed = sem("rank_ps"), sem("routed")
    kv_zero = sem("kv_zero")
    q1_ready, diff_ready, exp_ready, cls_ready, counted = sem("q1_ready"), sem("diff_ready"), sem("exp_ready"), sem("cls_ready"), sem("counted")
    stored = sem("stored")
    apart, pool_apart = sem("apart"), sem("pool_apart")
    var_ready, rstd_ready, var2_ready, rstd2_ready = sem("var_ready"), sem("rstd_ready"), sem("var2_ready"), sem("rstd2_ready")
    scattered = [sem(f"scattered{u}") for u in range(2)]

    kv_all = kv[:, 0:NSUB * 2 * CH * P].rearrange("p (i c j) -> p i c j", i=NSUB, j=P)
    kv_diag = kv[:].rearrange("p (i w) -> p i w", w=WIDE)[:, :, 0:2 * CH * P] \
        .rearrange("p i (c j) -> p i c j", j=P)[:, :, :, 0:SUB]
    kv_next = kv[:, 2 * CH * P:2 * CH * P + (NSUB - 1) * WIDE].rearrange("p (i w) -> p i w", w=WIDE)[:, :, 0:2 * CH * P] \
        .rearrange("p i (c j) -> p i c j", j=P)[:, :, :, 0:SUB]

    def sub(t):
        return t.rearrange("p (c i s) -> p i c s", i=NSUB, s=SUB)

    def at(b, c):
        return sh.h2[:, bass.ds(CH * b + c, 1)].rearrange("p o d -> p (o d)")

    def schedule(eng, turn):
        turn(-1, 1, True, False, False)
        turn(0, 0, True, True, False)
        with eng.Fori(0, (BATCH - 2) // 2) as i:
            turn(2 * i + 1, 1, True, True, True)
            turn(2 * i + 2, 0, True, True, True)
        turn(BATCH - 1, 1, False, True, True)
        turn(BATCH, 0, False, False, True)

    def pad_rows(eng, n):
        eng.wait_ge(counted, 1)
        for e in range(n, E, 2):
            row = eng.value_load(pad_row[0:1, e:e + 1], min_val=0, max_val=SPARE)
            eng.dma_start(x_slots[bass.ds(row, P), :], sh.pad[:]).then_inc(stored, 16)

    with nc.Block() as block:
        @block.sync
        def _(sp):
            for b in range(BATCH):
                src = h_rows[:, b:b + 1, :].rearrange("(c p) o d -> p (c o) d", p=P)
                sp.dma_start(sh.h2[:, CH * b:CH * (b + 1)], src).then_inc(h_in[min(b, 2)], 16)
            sp.dma_start(x_slots[SPARE:SPARE + P], sh.pad[:]).then_inc(stored, 16)
            sp.dma_start(out[SINK:SINK + P], sh.pad[:, 0:D]).then_inc(stored, 16)
            sp.dma_start(out[0:1], sh.h2[0:1, TILES]).then_inc(stored, 16)
            assert E == BATCH
            with sp.Fori(0, BATCH) as b:
                sp.wait_ge(xn_ready, b + 1)
                sp.dma_start(experts[:, bass.ds(b, 1)], w_dram[:, bass.ds(b, 1)]).then_inc(sh.experts_in, 16)
                sp.wait_ge(res_used, b + 1)
                sp.dma_start(out[bass.ds(b * ROW0 + 1, TOK), :].rearrange("(c p) d -> p c d", p=P),
                             sh.h2[:, bass.ds(CH * b, CH)]).then_inc(stored, 16)
            pad_rows(sp, 0)
            sp.wait_ge(stored, 16 * (3 + BATCH + E))

        @block.vector
        def _(dve):
            def route(st, n, scores):
                for c in range(n):
                    st.mark(nc.vector.max(topc[:, c], scores[:, c]))
                st.wait_apart()
                for c in range(n):
                    st.mark(nc.vector.max_index(ix[:, c], topc[:, c], scores[:, c]))
                st.wait()
                st.link(nc.vector.tensor_copy(ixf[:, 0:n], ix[:, 0:n]))
                for k in range(2):
                    st.mark(nc.vector.tensor_tensor(oh[:, k, 0:n], ixf[:, 0:n, k:k + 1].to_broadcast([P, n, E]),
                                                    sh.iota8[:].unsqueeze(1).to_broadcast([P, n, E]), ALU.is_equal))
                st.wait()
                st.mark(nc.vector.tensor_tensor(hit[:, 0:n], oh[:, 0, 0:n], oh[:, 1, 0:n], ALU.add))
                st.mark(nc.vector.tensor_tensor(tw[:, 0:n, 0:1], topc[:, 0:n, 1:2], topc[:, 0:n, 0:1], ALU.subtract))
                st.wait()
                nc.vector.sem_inc(diff_ready, 1)

            def weights(st, e, total, out0, out1):
                st.link(nc.vector.tensor_scalar(total, e, 1.0, None, ALU.add))
                st.link(nc.vector.reciprocal(out0, total))
                st.link(nc.vector.tensor_tensor(out1, out0, e, ALU.mult))

            def two_moments(st, b, stats, mom):
                for c in range(CH):
                    st.mark(nc.vector.bn_stats(stats[:, c], at(b, c)))
                st.wait_apart()
                for c in range(CH):
                    st.mark(nc.vector.bn_aggr(mom[:, c], stats[:, c]))
                st.wait()

            def turn(b, u, pre, post, tail):
                w = 1 - u
                total = 62
                st = Steps(dve, dve_step, (b + 1) * total + PRO, apart)
                if pre:
                    dve.wait_ge(h_in[2 if tail else b + 1], 16 * (BATCH - 2) if tail else 16)
                    two_moments(st, b + 1, stats, mom)
                    nc.vector.sem_inc(var_ready, 1)
                    if not (isinstance(b, int) and b < 0):
                        dve.wait_ge(xt_ps, b + 1)
                    dve.wait_ge(rstd_ready, b + 2)
                    dve.sem_inc(apart, 1)
                    for c in range(CH):
                        st.mark(nc.vector.tensor_scalar(xn[:, c], at(b + 1, c), mom[:, c, 0:1], rstd[:, c], ALU.subtract, ALU.mult))
                    st.wait()
                    nc.vector.sem_inc(xn_ready, 1)
                elif post:
                    nc.vector.sem_inc(var_ready, 1)
                if tail:
                    dve.wait_ge(wo_ps, CH * b)
                    dve.sem_inc(apart, 1)
                    for c in range(CH):
                        st.mark(nc.vector.tensor_tensor(at(b - 1, c), bk[6][:, c * D:(c + 1) * D], at(b - 1, c), ALU.add))
                    st.wait_apart()
                    nc.vector.sem_inc(res_used, 1)
                    two_moments(st, b - 1, stats2, mom2)
                    nc.vector.sem_inc(var2_ready, 1)
                if post:
                    for c in range(CH):
                        dve.wait_ge(tanh_sb, CH * b + c + 1)
                        st.mark(nc.vector.scalar_tensor_tensor(sg[:, c], sg[:, c], 1.0, bk[4 + c][:], ALU.add, ALU.mult))
                    st.wait()
                    nc.vector.sem_inc(sg_ready, 1)
                if tail:
                    dve.wait_ge(scattered[w], 32 * (b - w) - 16)
                    dve.wait_ge(rstd2_ready, b)
                    dve.sem_inc(apart, 1)
                    for c in range(CH):
                        st.mark(nc.vector.tensor_scalar(x2[w][:, 0, c, 0:D], at(b - 1, c), mom2[:, c, 0:1], rstd2[:, c], ALU.subtract, ALU.mult))
                    st.wait()
                    nc.vector.sem_inc(x2_ready, 1)
                    st.mark(nc.vector.tensor_copy(x2[w][:, 1, :, 0:D], x2[w][:, 0, :, 0:D]))
                    st.mark(nc.vector.tensor_copy(x2[w][:, :, :, D + 1], sh.tok[:, bass.ds(CH * (b - 1), CH)].unsqueeze(1)
                                                  .to_broadcast([P, 2, CH])))
                if post:
                    for c in range(CH):
                        dve.wait_ge(a_ps, CH * b + c + 1)
                        nc.vector.tensor_tensor(am[:, c], bk[6 + c][:].rearrange("p (h i) -> p h i", i=P),
                                                sh.causal[:].unsqueeze(1).to_broadcast([P, HEADS, P]), ALU.mult) \
                            .then_inc(masked, 1)
                    dve.wait_ge(s_ps, b + 1)
                    for t in range(2):
                        for par in range(2):
                            rows, cols = slice(par * DK, (par + 1) * DK), slice(par * DV, (par + 1) * DV)
                            st.mark(nc.vector.scalar_tensor_tensor(
                                s1[rows, t, cols], sh.s_cls[rows, t, cols], pb[rows, CH * t, NSUB:NSUB + 1],
                                bk[2][rows, t * 2 * DV + cols.start:t * 2 * DV + cols.stop], ALU.mult, ALU.add))
                    st.wait()
                    nc.vector.sem_inc(s1_ready, 1)
                if pre:
                    dve.wait_ge(y_ps, b + 2)
                    for t in range(2):
                        st.mark(nc.vector.tensor_scalar(mn[:, t], bk[3][:, t * CH * P:(t + 1) * CH * P], sh.gb2[:, t:t + 1], None,
                                                        ALU.add))
                    st.wait()
                    nc.vector.sem_inc(mn_ready, 1)
                if tail:
                    dve.wait_ge(score_ps, b)
                    st.mark(nc.vector.tensor_copy(sc[:], bk[0][:, 0:CH * E].rearrange("p (c e) -> p c e", e=E)))
                    st.wait_apart()
                    route(st, CH, sc)
                    st.wait()
                    nc.vector.sem_inc(hit_ready, 1)

                def gate_out(c):
                    dve.wait_ge(rs_ready, CH * b + c + 1)
                    for h in range(HEADS):
                        cols = slice(h * DV, (h + 1) * DV)
                        st.mark(nc.vector.scalar_tensor_tensor(og[:, c, cols], bk[6 + c][:, cols], rs[:, c, h:h + 1],
                                                               sg[:, c, cols], ALU.mult, ALU.mult))
                    st.wait()
                    nc.vector.sem_inc(gated, 1)

                if post:
                    gate_out(0)
                if pre:
                    dve.wait_ge(ln_ready, b + 2)
                    if not (isinstance(b, int) and b < 0):
                        dve.wait_ge(kv_ready, b + 1)
                    st.link(nc.vector.scalar_tensor_tensor(mn[:], mn[:], 0.0, ay[:], ALU.min, ALU.subtract))
                    st.link(nc.vector.tensor_tensor_scan(e1[:], sh.keep[:], mn[:].rearrange("p t n -> p (t n)"), 0.0,
                                                         ALU.mult, ALU.add))
                    blk = e1[:].rearrange("p (b s) -> p b s", s=SUB)
                    st.mark(nc.vector.tensor_tensor(e3[:].rearrange("p (b s) -> p b s", s=SUB),
                                                    blk[:, :, SUB - 1:SUB].to_broadcast([P, 2 * CH * NSUB, SUB]), blk, ALU.subtract))
                    st.mark(nc.vector.tensor_scalar(e2[:], e1[:], -80.0 * GATE_NORM, None, ALU.max))
                    st.wait()
                    nc.vector.sem_inc(cums_ready, 1)
                if post:
                    gate_out(1)
                if pre:
                    dve.wait_ge(exps_ready, b + 2)
                    dve.wait_ge(kv_zero, 6)
                    dve.wait_ge(k_ps, b + 2)
                    st.mark(nc.vector.tensor_tensor(kv_diag, sub(bk[2][:]), sub(e2[:]), ALU.mult))
                    kn, en = sub(bk[2][:])[:, 0:NSUB - 1], sub(e3[:])[:, 0:NSUB - 1]
                    st.mark(nc.vector.tensor_tensor(kv_next, kn, en, ALU.mult))
                    last = lambda t: t.rearrange("p (t c j) -> p t c j", t=2, c=CH)[:, :, 0, P - SUB:P]
                    st.mark(nc.vector.tensor_tensor(kst[:, :, P - SUB:P], last(bk[2][:]), last(e3[:]), ALU.mult))
                    dve.wait_ge(q_ps, b + 2)
                    if not (isinstance(b, int) and b < 0):
                        dve.wait_ge(q1_ready, 2 * (b + 1))
                    st.mark(nc.vector.scalar_tensor_tensor(qp[:], bk[1][:], DK ** -0.5, e1[:], ALU.mult, ALU.mult))
                    st.wait()
                    nc.vector.sem_inc(qk_used, 1)
                if tail:
                    dve.wait_ge(rank_ps, b + 1)
                    ranks = bk[0][:, 16:16 + CH * E].rearrange("p (c e) -> p c e", e=E)
                    counts = bk[0][:, 32:32 + CH * E].rearrange("p (c e) -> p c e", e=E)
                    st.link(nc.vector.tensor_tensor(rank[:], ranks, sh.carry[:].unsqueeze(1).to_broadcast([P, CH, E]), ALU.add))
                    st.mark(nc.vector.tensor_tensor(rank[:, 1], rank[:, 1], counts[:, 0], ALU.add))
                    st.link(nc.vector.tensor_tensor(sh.carry[:], sh.carry[:], counts[:, 0], ALU.add))
                    st.link(nc.vector.tensor_tensor(sh.carry[:], sh.carry[:], counts[:, 1], ALU.add))
                    for k in range(2):
                        st.mark(nc.vector.tensor_tensor(pick[:, k], oh[:, k], rank[:], ALU.mult))
                    st.wait()
                    st.link(nc.vector.reduce_sum(posf[:], pick[:], axis=mybir.AxisListType.X))
                    st.link(nc.vector.tensor_copy(posi[w][:], posf[:]))
                    dve.wait_ge(exp_ready, b + 1)
                    weights(st, tw[:, :, 0], tw[:, :, 1], x2[w][:, 0, :, D], x2[w][:, 1, :, D])
                    nc.vector.sem_inc(routed, 1)
                if st.n < total:
                    nc.vector.sem_inc(dve_step, total - st.n)
                assert st.n <= total, st.n

            st = Steps(dve, dve_step, 0, apart)
            route(st, 1, sh.sc_cls[:].unsqueeze(1))
            st.link(nc.vector.tensor_scalar(hit[:, 0], hit[:, 0], sh.row0[:], None, ALU.mult))
            nc.vector.sem_inc(hit_ready, 1)
            for k in range(2):
                st.mark(nc.vector.tensor_tensor(pick[:, k, 0], oh[:, k, 0], sh.region[:], ALU.mult))
            st.wait()
            st.link(nc.vector.reduce_sum(posf[:, :, 0:1], pick[:, :, 0:1], axis=mybir.AxisListType.X))
            st.link(nc.vector.tensor_copy(cls_row[:], posf[0:1, :, 0]))
            dve.wait_ge(exp_ready, 1)
            weights(st, tw[0:1, 0:1, 0], tw[0:1, 0:1, 1], sh.x2c[:, 0, D:D + 1], sh.x2c[:, 1, D:D + 1])
            nc.vector.sem_inc(cls_ready, 1)
            dve.wait_ge(rank_ps, 1)
            st.link(nc.vector.tensor_tensor(sh.carry[:], bk[0][:, 32:32 + E], sh.region[:], ALU.add))
            nc.vector.sem_inc(routed, 1)
            PRO = st.n
            schedule(dve, turn)

            st = Steps(dve, dve_step, PRO + (BATCH + 2) * 62, apart)
            big = 1.5 * 2.0 ** 23
            st.link(nc.vector.tensor_copy(pad_row[:], sh.carry[0:1]))
            nc.vector.sem_inc(counted, 1)
            st.link(nc.vector.tensor_tensor(n_tiles[:], sh.carry[:], sh.region[:], ALU.subtract))
            st.link(nc.vector.tensor_scalar(n_tiles[:], n_tiles[:], 1.0 / P, (P - 1) / (2.0 * P), ALU.mult, ALU.add))
            st.link(nc.vector.tensor_scalar(n_tiles[:], n_tiles[:], big, -big, ALU.add, ALU.add))
            st.link(nc.vector.tensor_tensor_scan(ends[:], sh.ones[:, 0:E], n_tiles[:], 0.0, ALU.mult, ALU.add))
            shape = [1, SLOTS, E]
            st.link(nc.vector.tensor_tensor(past, slot[:].unsqueeze(2).to_broadcast(shape),
                                            ends[0:1].unsqueeze(1).to_broadcast(shape), ALU.is_ge))
            st.link(nc.vector.reduce_sum(tab[:, 0], past, axis=mybir.AxisListType.X))
            st.mark(nc.vector.tensor_scalar(tab[:, 3], tab[:, 0], float(E - 1), None, ALU.min))
            st.link(nc.vector.tensor_tensor(past, past, n_tiles[0:1].unsqueeze(1).to_broadcast(shape), ALU.mult))
            st.mark(nc.vector.tensor_copy(sh.tabi[:, 1], tab[:, 3]))
            st.link(nc.vector.reduce_sum(tab[:, 1], past, axis=mybir.AxisListType.X))
            st.mark(nc.vector.tensor_scalar(tab[:, 2], tab[:, 0], float(E), float(P), ALU.is_lt, ALU.mult))
            st.link(nc.vector.tensor_tensor(tab[:, 1], slot[:], tab[:, 1], ALU.subtract))
            st.link(nc.vector.tensor_tensor(tab[:, 2], tab[:, 2], tab[:, 1], ALU.mult))
            st.link(nc.vector.scalar_tensor_tensor(tab[:, 3], tab[:, 0], float(REGION), tab[:, 2], ALU.mult, ALU.add))
            st.link(nc.vector.tensor_copy(sh.tabi[:, 0], tab[:, 3]))

        @block.gpsimd
        def _(pool):
            nc.gpsimd.memset(half[:], -0.5).then_inc(kv_zero, 1)
            nc.gpsimd.memset(q1[:], 0.0).then_inc(kv_zero, 1)
            nc.gpsimd.memset(kv[:], 0.0).then_inc(kv_zero, 1)
            nc.gpsimd.memset(pb[:, :, 0:1], 1.0).then_inc(kv_zero, 1)
            nc.gpsimd.memset(s1[:], 0.0).then_inc(kv_zero, 1)
            nc.gpsimd.iota(slot[:], [[1, SLOTS]], base=0, channel_multiplier=0, allow_small_or_imprecise_dtypes=True).then_inc(kv_zero, 1)

            def inverse_root(st, out, src, scale, eps, n):
                pool.sem_inc(pool_apart, 1)
                st.link(nc.gpsimd.tensor_scalar(out, src, scale, eps, ALU.mult, ALU.add))
                return nc.gpsimd.tensor_tensor(out, out, half[:, 0:n], ALU.pow)

            def root_of_rows(st, b):
                pool.wait_ge(var_ready, b + 1)
                flat = lambda t: t.rearrange("p c o -> p (c o)")
                inverse_root(st, flat(rstd[:]), flat(mom[:, :, 1:2]), 1.0, EPS, CH).then_inc(rstd_ready, 1)

            root_of_rows(Steps(pool, pool_step, 0, pool_apart), 0)
            pool.wait_ge(cls_ready, 1)
            for k in range(2):
                row = pool.value_load(cls_row[0:1, k:k + 1], min_val=0, max_val=(E - 1) * REGION)
                pool.dma_start(x_slots[bass.ds(row, 1), :], sh.x2c[:, k]).then_inc(scattered[k], 16)

            def turn(b, u, pre, post, tail):
                w = 1 - u
                total = 17
                st = Steps(pool, pool_step, (b + 1) * total + 1, pool_apart)
                flat = lambda t: t.rearrange("p c o -> p (c o)")
                if tail:
                    pool.wait_ge(var2_ready, b)
                    inverse_root(st, flat(rstd2[:]), flat(mom2[:, :, 1:2]), 1.0, EPS, CH).then_inc(rstd2_ready, 1)
                if post:
                    for c in range(CH):
                        pool.wait_ge(squared, CH * b + c + 1)
                        inverse_root(st, rs[:, c], ss[:, c], 4.0 / DV, 4.0 * EPS, HEADS).then_inc(rs_ready, 1)
                if pre:
                    pool.wait_ge(qk_used, b + 2)
                    blk = e1[:].rearrange("p (c i s) -> p c i s", i=NSUB, s=SUB)[:, :, :, SUB - 1]
                    pool.sem_inc(pool_apart, 1)
                    st.link(nc.gpsimd.tensor_copy(pb[:, :, 1:2], blk[:, :, 0:1]))
                    for i in range(1, NSUB):
                        st.link(nc.gpsimd.tensor_tensor(pb[:, :, i + 1:i + 2], pb[:, :, i:i + 1], blk[:, :, i:i + 1], ALU.mult))
                    st.mark(nc.gpsimd.tensor_tensor(
                        qs[:].rearrange("p c (i s) -> p c i s", s=SUB), qp[:].rearrange("p (c i s) -> p c i s", i=NSUB, s=SUB),
                        pb[:, :, 0:NSUB].unsqueeze(3).to_broadcast([P, 2 * CH, NSUB, SUB]), ALU.mult))
                    for i in range(2, NSUB + 1):
                        n = (i - 1) * SUB
                        if i < NSUB:
                            dec = blk[:, :, i - 1:i].to_broadcast([P, 2 * CH, n])
                            st.link(nc.gpsimd.tensor_tensor(kv_all[:, i, :, 0:n], kv_all[:, i - 1, :, 0:n], dec, ALU.mult))
                        else:
                            src = kv_all[:, i - 1].rearrange("p (t c) j -> p t c j", c=CH)[:, :, 0, 0:n]
                            dec = blk.rearrange("p (t c) i -> p t c i", c=CH)[:, :, 0, i - 1:i].to_broadcast([P, 2, n])
                            st.link(nc.gpsimd.tensor_tensor(kst[:, :, 0:n], src, dec, ALU.mult))
                    nc.gpsimd.sem_inc(kv_ready, 1)
                if pre:
                    root_of_rows(st, b + 2)
                if tail:
                    pool.wait_ge(routed, b + 1)
                    pool.sem_inc(pool_apart, 1)
                    for c in range(CH):
                        for k in range(2):
                            nc.gpsimd.indirect_dma_start(
                                x_slots, bass.IndirectOffsetOnAxis(ap=posi[w][:, k, c:c + 1], axis=0), x2[w][:, k, c], None) \
                                .then_inc(scattered[w], 16)
                if total - st.n:
                    nc.gpsimd.sem_inc(pool_step, total - st.n)
                assert st.n <= total, st.n

            schedule(pool, turn)
            pool.wait_ge(scattered[0], 16 * 4 * (BATCH // 2) + 16)
            pool.wait_ge(scattered[1], 16 * 4 * (BATCH // 2) + 16)

        @block.scalar
        def _(act):
            def turn(b, u, pre, post, tail):
                total = 11
                st = Steps(act, act_step, (b + 1) * total)
                if pre:
                    act.wait_ge(xt_ps, b + 2)
                    nc.scalar.copy(xt[:], bk[0][:].rearrange("p (k n) -> p k n", k=2)).then_inc(xt_sb, 1)
                    act.wait_ge(t16_ps, b + 2)
                    nc.scalar.copy(t16[:], bk[0][0:RANK, 0:CH * P]).then_inc(t16_sb, 1)
                if post:
                    act.wait_ge(krow_ps, b + 1)
                    nc.scalar.copy(krow[:], bk[1][:, 0:2 * P]).then_inc(krow_sb, 1)
                if tail:
                    act.wait_ge(x2t_ps, b)
                    nc.scalar.copy(x2t[:], bk[3][:].rearrange("p (k n) -> p k n", k=2)).then_inc(x2t_sb, 1)

                def squares(c):
                    act.wait_ge(o_ps, CH * b + c + 1)
                    for h in range(HEADS):
                        st.mark(nc.scalar.activation(og[:, c, h * DV:(h + 1) * DV], bk[6 + c][:, h * DV:(h + 1) * DV], ACT.Square,
                                                     accum_out=ss[:, c, h:h + 1]))
                    st.wait()
                    nc.scalar.sem_inc(squared, 1)

                if post:
                    squares(0)
                if pre:
                    act.wait_ge(mn_ready, b + 2)
                    st.link(nc.scalar.activation(ay[:], mn[:], ACT.Abs))
                    st.link(nc.scalar.activation(ay[:], ay[:], ACT.Exp, scale=-1.0))
                    st.link(nc.scalar.activation(ay[:], ay[:], ACT.Ln, bias=1.0))
                    nc.scalar.sem_inc(ln_ready, 1)
                if post:
                    squares(1)
                if pre:
                    act.wait_ge(cums_ready, b + 2)
                    nc.scalar.activation(e2[:], e2[:], ACT.Exp, scale=-1.0 / GATE_NORM)
                    nc.scalar.activation(e3[:], e3[:], ACT.Exp, scale=1.0 / GATE_NORM)
                    nc.scalar.activation(e1[:], e1[:], ACT.Exp, scale=1.0 / GATE_NORM).then_inc(exps_ready, 1)
                if tail:
                    act.wait_ge(diff_ready, b + 1)
                    nc.scalar.activation(tw[:, :, 0], tw[:, :, 0], ACT.Exp).then_inc(exp_ready, 1)
                if pre:
                    for c in range(CH):
                        act.wait_ge(v_ps, CH * (b + 1) + c + 1)
                        nc.scalar.copy(v[:, c], bk[4 + c][:]).then_inc(v_sb, 1)
                if post:
                    for c in range(CH):
                        act.wait_ge(ot_ps, CH * b + c + 1)
                        nc.scalar.copy(ot[:, c], bk[3][:].rearrange("p (h n) -> p h n", h=HEADS)).then_inc(ot_sb, 1)
                if pre:
                    act.wait_ge(qk_used, b + 2)
                    for par in range(2):
                        rows = slice(par * DK, (par + 1) * DK)
                        nc.scalar.copy(q1[rows, par].rearrange("p c j -> p (c j)"), qp[rows]).then_inc(q1_ready, 1)
                    for c in range(CH):
                        act.wait_ge(g_ps, CH * (b + 1) + c + 1)
                        nc.scalar.activation(sg[:, c], bk[4 + c][:], ACT.Tanh, scale=0.5).then_inc(tanh_sb, 1)
                if total - st.n:
                    nc.scalar.sem_inc(act_step, total - st.n)
                assert st.n <= total, st.n

            act.wait_ge(diff_ready, 1)
            nc.scalar.activation(tw[:, 0:1, 0], tw[:, 0:1, 0], ACT.Exp).then_inc(exp_ready, 1)
            schedule(act, turn)
            pad_rows(act, 1)

        @block.tensor
        def _(pe):
            def project(out, lhs, rhs):
                for k in range(2):
                    last = nc.tensor.matmul(out, lhs(k), rhs(k), start=(k == 0), stop=(k == 1))
                return last

            pe.wait_ge(hit_ready, 1)
            nc.tensor.matmul(bk[0][:, 32:32 + E], sh.ones[:], hit[:, 0], start=True, stop=True).then_inc(rank_ps, 1)

            def turn(b, u, pre, post, tail):
                w = 1 - u
                if pre:
                    pe.wait_ge(xn_ready, b + 2)
                    pe.wait_ge(routed, (b if tail else 1))
                    for c in range(CH):
                        for k in range(2):
                            last = nc.tensor.transpose(bk[0][:, k * CH * P + c * P:k * CH * P + (c + 1) * P],
                                                       xn[:, c, k * P:(k + 1) * P], sh.ident[:])
                    last.then_inc(xt_ps, 1)
                if post:
                    pe.wait_ge(kv_ready, b + 1)
                    for t in range(2):
                        last = nc.tensor.transpose(bk[1][:, t * P:(t + 1) * P], kst[:, t], sh.ident[:])
                    last.then_inc(krow_ps, 1)
                if pre:
                    pe.wait_ge(xt_sb, b + 2)
                    project(bk[0][0:RANK, 0:CH * P], lambda k: sh.gw1[:, k], lambda k: xt[:, k]).then_inc(t16_ps, 1)
                if post:
                    pe.wait_ge(q1_ready, 2 * (b + 1))
                    if tail:
                        pe.wait_ge(res_used, b)
                    for c in range(CH):
                        heads = bk[6 + c][:].rearrange("p (h i) -> p h i", i=P)
                        for t in range(2):
                            for i in range(NSUB):
                                cols = slice(i * SUB, (i + 1) * SUB)
                                last = nc.tensor.matmul(heads[:, 2 * t:2 * t + 2, cols], kv_all[:, i, CH * t + c],
                                                        q1[:, :, CH * t + c, cols], start=True, stop=True)
                        last.then_inc(a_ps, 1)
                    pe.wait_ge(krow_sb, b + 1)
                    for t in range(2):
                        last = nc.tensor.matmul(bk[2][:, t * 2 * DV:(t + 1) * 2 * DV], krow[:, t * P:(t + 1) * P],
                                                v[:, 0, t * 2 * DV:(t + 1) * 2 * DV], start=True, stop=True)
                    last.then_inc(s_ps, 1)
                if tail:
                    pe.wait_ge(x2_ready, b)
                    pe.wait_ge(ot_sb, CH * b)
                    for c in range(CH):
                        for k in range(2):
                            last = nc.tensor.transpose(bk[3][:, k * CH * P + c * P:k * CH * P + (c + 1) * P],
                                                       x2[w][:, 0, c, k * P:(k + 1) * P], sh.ident[:])
                    last.then_inc(x2t_ps, 1)

                def outputs(c):
                    pe.wait_ge(masked, CH * b + c + 1)
                    for t in range(2):
                        nc.tensor.matmul(bk[6 + c][:, t * 2 * DV:(t + 1) * 2 * DV], qs[:, CH * t + c],
                                         (sh.s_cls if c == 0 else s1)[:, t], start=True, stop=False)
                        for h in (2 * t, 2 * t + 1):
                            cols = slice(h * DV, (h + 1) * DV)
                            last = nc.tensor.matmul(bk[6 + c][:, cols], am[:, c, h], v[:, c, cols], start=False, stop=(h % 2 == 1))
                    last.then_inc(o_ps, 1)

                if post:
                    outputs(0)
                if tail:
                    pe.wait_ge(x2t_sb, b)
                    if pre:
                        pe.wait_ge(t16_sb, b + 2)
                    for c in range(CH):
                        last = project(bk[0][:, c * E:(c + 1) * E], lambda k: x2t[:, k, c * P:(c + 1) * P], lambda k: sh.gate[:, k])
                    last.then_inc(score_ps, 1)
                if pre:
                    pe.wait_ge(t16_sb, b + 2)
                    for t in range(2):
                        last = nc.tensor.matmul(bk[3][:, t * CH * P:(t + 1) * CH * P], sh.gw2[:, t * P:(t + 1) * P], t16[:],
                                                start=True, stop=True)
                    last.then_inc(y_ps, 1)
                if post:
                    pe.wait_ge(s1_ready, b + 1)
                    outputs(1)
                if pre:
                    for out, wt, done in ((bk[2], sh.wk, k_ps), (bk[1], sh.wq, q_ps)):
                        for t in range(2):
                            last = project(out[:, t * CH * P:(t + 1) * CH * P], lambda k: wt[:, k, t * P:(t + 1) * P],
                                           lambda k: xt[:, k])
                        last.then_inc(done, 1)
                    if not (isinstance(b, int) and b < 0):
                        pe.wait_ge(sg_ready, b + 1)
                    for c in range(CH):
                        project(bk[4 + c][:], lambda k: xt[:, k, c * P:(c + 1) * P], lambda k: sh.wv[:, k]).then_inc(v_ps, 1)
                if tail:
                    pe.wait_ge(hit_ready, b + 1)
                    flat = hit[:].rearrange("p c e -> p (c e)")
                    nc.tensor.matmul(bk[0][:, 16:16 + CH * E], sh.before[:], flat, start=True, stop=True)
                    nc.tensor.matmul(bk[0][:, 32:32 + CH * E], sh.ones[:], flat, start=True, stop=True).then_inc(rank_ps, 1)

                def o_transpose(c):
                    pe.wait_ge(gated, CH * b + c + 1)
                    if c == 0:
                        if pre:
                            pe.wait_ge(mn_ready, b + 2)
                    else:
                        pe.wait_ge(ot_sb, CH * b + 1)
                    for h in range(HEADS):
                        last = nc.tensor.transpose(bk[3][:, h * P:(h + 1) * P], og[:, c, h * DV:(h + 1) * DV], sh.ident[:])
                    last.then_inc(ot_ps, 1)

                def g_rows(c):
                    pe.wait_ge(v_sb, CH * (b + 1) + c + 1)
                    project(bk[4 + c][:], lambda k: xt[:, k, c * P:(c + 1) * P], lambda k: sh.wg[:, k]).then_inc(g_ps, 1)

                def out_rows(c):
                    pe.wait_ge(ot_sb, CH * b + c + 1)
                    for h in range(HEADS):
                        last = nc.tensor.matmul(bk[6][:, c * D:(c + 1) * D], ot[:, c, h], sh.wo[:, h],
                                                start=(h == 0), stop=(h == HEADS - 1))
                    last.then_inc(wo_ps, 1)

                if post:
                    o_transpose(0)
                if pre:
                    g_rows(0)
                if post:
                    o_transpose(1)
                    out_rows(0)
                if pre:
                    g_rows(1)
                if post:
                    out_rows(1)

            schedule(pe, turn)


def stage_experts(nc, ctx, sh, bk, experts, x_slots, out):
    def sb(name, shape, dt=F32):
        return ctx.enter_context(nc.sbuf_tensor(name, shape, dt))

    def sem(name):
        return ctx.enter_context(nc.semaphore(name))

    xs = [sb(f"xs{u}", [P, XW]) for u in range(2)]
    meta = sb("meta", [P, SLOTS, 2])
    wt = [sb(f"wt{u}", [P, 1]) for u in range(2)]
    out_row = [sb(f"out_row{u}", [P, 1], U32) for u in range(2)]
    xt = [sb(f"ext{u}", [P, 2, P]) for u in range(2)]
    sl = [sb(f"sl{u}", [P, FF]) for u in range(2)]
    hh = [sb(f"hh{u}", [P, FF]) for u in range(2)]
    ht = [sb(f"ht{u}", [P, FF // P, P]) for u in range(2)]
    ys = [sb(f"ys{u}", [P, D]) for u in range(2)]

    x_in = [sem(f"x_in{u}") for u in range(2)]
    xt_ps, xt_sb, up_ps, silu_ready, h_ready = sem("ext_ps"), sem("ext_sb"), sem("up_ps"), sem("silu_ready"), sem("h_ready")
    ht_ps, ht_sb, y_ps, y_sb = sem("ht_ps"), sem("ht_sb"), sem("ey_ps"), sem("ey_sb")
    meta_taken, meta_ready, added, apart = sem("meta_taken"), sem("meta_ready"), sem("added"), sem("e_apart")
    out_stored = sem("out_stored")
    bt, ba, bb, bh, by = bk[0], bk[1:3], bk[3:5], bk[5], bk[6:8]

    def schedule(eng, turn):
        for u in range(2):
            turn(u, u, 4)
        with eng.Fori(1, SLOTS // 2 - 2) as i:
            for u in range(2):
                turn(2 * i + u, u, 4)
        for n in range(4):
            turn(SLOTS - 4 + n, n % 2, 3 - n)

    with nc.Block() as block:
        @block.sync
        def _(sp):
            sp.wait_ge(added, 16 * SLOTS)
            sp.dma_start(out[ROW0:SINK].rearrange("(b r) d -> b r d", r=ROW0)[:, 0],
                         out[0:1].to_broadcast([BATCH - 1, D])).then_inc(out_stored, 16)
            sp.wait_ge(out_stored, 16)

        @block.gpsimd
        def _(pool):
            def take(s, u):
                pool.wait_ge(x_in[u], 8 * (s - u) + 16)
                pool.sem_inc(apart, 1)
                nc.gpsimd.tensor_copy(meta[:, bass.ds(s, 1)].rearrange("p o k -> p (o k)"), xs[u][:, D:XW]).then_inc(meta_taken, 1)

            take(0, 0)
            take(1, 1)

            def turn(s, u, left):
                if left >= 2:
                    take(s + 2, u)
                if not (isinstance(s, int) and s < 1):
                    pool.wait_ge(added, 16 * s)
                pool.wait_ge(meta_taken, s + 1)
                pool.sem_inc(apart, 1)
                nc.gpsimd.tensor_copy(wt[u][:], meta[:, bass.ds(s, 1), 0:1].rearrange("p o k -> p (o k)")).then_inc(meta_ready, 1)
                nc.gpsimd.tensor_copy(out_row[u][:], meta[:, bass.ds(s, 1), 1:2].rearrange("p o k -> p (o k)")).then_inc(meta_ready, 1)
                pool.wait_ge(meta_ready, 2 * s + 2)
                pool.wait_ge(y_sb, s + 1)
                pool.sem_inc(apart, 1)
                nc.gpsimd.indirect_dma_start(out, bass.IndirectOffsetOnAxis(ap=out_row[u][:], axis=0), ys[u][:], None,
                                             compute_op=ALU.add).then_inc(added, 16)

            schedule(pool, turn)

        @block.vector
        def _(dve):
            def gate(s, u):
                dve.wait_ge(silu_ready, s + 1)
                nc.vector.tensor_tensor(hh[u][:], sl[u][:], bb[u][:], ALU.mult).then_inc(h_ready, 1)

            gate(0, 0)

            def turn(s, u, left):
                dve.wait_ge(ht_ps, s + 1)
                nc.vector.tensor_copy(ht[u][:], bh[:].rearrange("p (j n) -> p j n", n=P)).then_inc(ht_sb, 1)
                if left >= 1:
                    gate(s + 1, 1 - u)

            schedule(dve, turn)

        @block.scalar
        def _(act):
            def load(s, u):
                row = act.value_load(sh.tabi[0:1, 0, bass.ds(s, 1)], min_val=0, max_val=SPARE)
                act.dma_start(xs[u][:], x_slots[bass.ds(row, P), :]).then_inc(x_in[u], 16)

            def x_copy(s, u, more):
                act.wait_ge(xt_ps, s + 1)
                nc.scalar.copy(xt[u][:], bt[:, 0:2 * P].rearrange("p (k n) -> p k n", k=2)).then_inc(xt_sb, 1)
                if more:
                    act.wait_ge(meta_taken, s + 1)
                    load(s + 2, u)

            def silu(s, u):
                act.wait_ge(up_ps, s + 1)
                nc.scalar.activation(sl[u][:], ba[u][:], ACT.Silu).then_inc(silu_ready, 1)

            for u in range(2):
                load(u, u)
            for u in range(2):
                x_copy(u, u, True)
            silu(0, 0)

            def turn(s, u, left):
                if left >= 2:
                    x_copy(s + 2, u, left >= 4)
                if left >= 1:
                    silu(s + 1, 1 - u)
                act.wait_ge(y_ps, s + 1)
                act.wait_ge(meta_ready, 2 * s + 2)
                act.sem_inc(apart, 1)
                nc.scalar.activation(ys[u][:], by[u][:, 0:D], ACT.Copy, scale=wt[u][:]).then_inc(y_sb, 1)

            schedule(act, turn)

        @block.tensor
        def _(pe):
            pe.wait_ge(sh.experts_in, 16 * E)

            def x_transpose(s, u):
                pe.wait_ge(x_in[u], 8 * (s - u) + 16)
                if not (isinstance(s, int) and s == 0):
                    pe.wait_ge(xt_sb, s)
                for k in range(2):
                    last = nc.tensor.transpose(bt[:, k * P:(k + 1) * P], xs[u][:, k * P:(k + 1) * P], sh.ident[:])
                last.then_inc(xt_ps, 1)

            def expert_of(s):
                return pe.value_load(sh.tabi[0:1, 1, bass.ds(s, 1)], min_val=0, max_val=E - 1)

            def up(s, u, e):
                pe.wait_ge(xt_sb, s + 1)
                for m, bank in enumerate((ba[u], bb[u])):
                    for k in range(2):
                        col = (2 * m + k) * FF
                        last = nc.tensor.matmul(bank[:], xt[u][:, k], experts[:, bass.ds(e, 1), col:col + FF]
                                                .rearrange("p o n -> p (o n)"), start=(k == 0), stop=(k == 1))
                last.then_inc(up_ps, 1)

            x_transpose(0, 0)
            x_transpose(1, 1)
            up(0, 0, expert_of(0))

            def turn(s, u, left):
                e = expert_of(s)
                e_next = expert_of(s + 1) if left >= 1 else None
                if left >= 2:
                    x_transpose(s + 2, u)
                pe.wait_ge(h_ready, s + 1)
                for j in range(FF // P):
                    last = nc.tensor.transpose(bh[:, j * P:(j + 1) * P], hh[u][:, j * P:(j + 1) * P], sh.ident[:])
                last.then_inc(ht_ps, 1)
                if left >= 1:
                    up(s + 1, 1 - u, e_next)
                pe.wait_ge(ht_sb, s + 1)
                if not (isinstance(s, int) and s < 2):
                    pe.wait_ge(y_sb, s - 1)
                for j in range(FF // P):
                    col = 4 * FF + j * D
                    last = nc.tensor.matmul(by[u][:, 0:D], ht[u][:, j], experts[:, bass.ds(e, 1), col:col + D]
                                            .rearrange("p o n -> p (o n)"), start=(j == 0), stop=(j == FF // P - 1))
                last.then_inc(y_ps, 1)

            schedule(pe, turn)


def build(nc, ins, out):
    h_rows = nc.dram_tensor("h_rows", (TOK, BATCH, D), F32, kind="Internal").ap()
    x_slots = nc.dram_tensor("x_slots", (SPARE + P, XW), F32, kind="Internal").ap()
    with ExitStack() as ctx:
        sh = Shared(nc, ctx)
        with ExitStack() as stage:
            stage_kernel(nc, stage, ins["params"], ins["b"], ins["c"], h_rows, ClassToken(nc, stage, sh, ins))
        experts = ctx.enter_context(nc.sbuf_tensor("experts", [P, E, EW], F32))
        bk = [ctx.enter_context(nc.psum_tensor(f"bank{n}", [P, 512], F32)) for n in range(8)]
        with ExitStack() as stage:
            stage_attention(nc, stage, sh, bk, h_rows, x_slots, experts, ins["experts"], out)
        with ExitStack() as stage:
            stage_experts(nc, stage, sh, bk, experts, x_slots, out)


def kernel(**inputs):
    import numpy as _np
    import concourse.bacc as _bacc
    from concourse import mybir as _mybir
    from concourse.bass_utils import run_bass_kernel_spmd as _run

    g = {k: _np.asarray(a) for k, a in inputs.items()}
    par = lambda a: a.reshape(PAIRS, 2, N_STATE).transpose(1, 2, 0).reshape(P, PAIRS)
    log_dt = _np.repeat(g["L0_tok_log_dt"][:, None], N_STATE, axis=1)
    split = lambda w: w.transpose(2, 0, 1).reshape(w.shape[2] // P, P, E, w.shape[1]).transpose(1, 2, 0, 3).reshape(P, E, -1)
    a = {
        "params": _np.stack([par(log_dt), par(g["L0_tok_inv_A_real"]), par(g["L0_tok_A_imag"])], axis=1),
        "b": _np.stack([par(g["L0_tok_B_ri"][..., r]) for r in range(2)], axis=1),
        "c": g["x"].reshape(BATCH, PAIRS, 2, N_STATE, 2).transpose(2, 3, 4, 1, 0).reshape(P, 2, PAIRS, BATCH),
        "cls": g["cls_tok"].reshape(2, P).T,
        "Wq": g["L0_attn_Wq"], "Wk": g["L0_attn_Wk"], "Wv": g["L0_attn_Wv"], "Wg": g["L0_attn_Wg"], "Wo": g["L0_attn_Wo"],
        "gk_w1": g["L0_attn_gk_w1"], "gk_w2": g["L0_attn_gk_w2"],
        "gk_b2": g["L0_attn_gk_b2"].reshape(2, P).T,
        "gnorm": g["L0_attn_g_norm_w"].reshape(P, 1),
        "gate": g["L0_ffn_gate_w"].T.reshape(2, P, E).transpose(1, 0, 2),
        "experts": _np.concatenate([split(g["L0_ffn_w1"]), split(g["L0_ffn_w3"]), split(g["L0_ffn_w2"])], axis=2),
    }
    nc = _bacc.Bacc("TRN2", target_bir_lowering=False, num_devices=1)
    arrays, ins = {}, {}
    for name, v in a.items():
        v = _np.ascontiguousarray(v)
        arrays[f"in_{name}"] = v
        ins[name] = nc.dram_tensor(f"in_{name}", v.shape, _mybir.dt.from_np(v.dtype), kind="ExternalInput").ap()
    out = nc.dram_tensor("out", (SINK + P, D), F32, kind="ExternalOutput").ap()
    build(nc, ins, out)
    r = _run(nc, [arrays], core_ids=[0])
    return r.results[0]["out"][:SINK].reshape(BATCH, ROW0, D)
```
